# Optimizing a Trainium2 kernel written in Bass

```python
import numpy as np
import jax
import jax.numpy as jnp

def _softmax(x, axis=-1):
    return jax.nn.softmax(x, axis=axis)

def _gelu(x):
    return jax.nn.gelu(x, approximate=True)

def _silu(x):
    return jax.nn.silu(x)

def _sigmoid(x):
    return jax.nn.sigmoid(x)

def _layernorm(x, axis=-1, eps=1e-05):
    m = jnp.mean(x, axis=axis, keepdims=True)
    v = jnp.var(x, axis=axis, keepdims=True)
    return (x - m) / jnp.sqrt(v + eps)

def _scatter_add(tgt, idx, src, axis=0):
    return tgt.at[idx].add(src)

def _segment_sum(src, seg, n):
    return jax.ops.segment_sum(src, seg, n)
kernel_name = 'mk_adaln_d2_jaxref_r8_6ee58f'

def setup_inputs(seed: int=0):
    np.random.seed(seed)
    _w = jnp.asarray

    def _L0_attn_setup():
        import jax, jax.numpy as jnp
        import numpy as np
        B, L, D = (2, 256, 128)
        H, HD = (16, 64)
        LD = 32
        key = jax.random.key(seed)
        ks = jax.random.split(key, 6)
        s = lambda fan_in: 1.0 / np.sqrt(fan_in)
        x_bld = jax.random.normal(ks[0], (B, L, D), dtype=jnp.float32)
        Wq = jax.random.normal(ks[1], (D, H, HD), dtype=jnp.float32) * s(D)
        Wkv_down = jax.random.normal(ks[2], (D, LD), dtype=jnp.float32) * s(D)
        Wk_up = jax.random.normal(ks[3], (LD, H, HD), dtype=jnp.float32) * s(LD)
        Wv_up = jax.random.normal(ks[4], (LD, H, HD), dtype=jnp.float32) * s(LD)
        Wout = jax.random.normal(ks[5], (H, HD, D), dtype=jnp.float32) * s(H * HD)
        return {'x_bld': x_bld, 'Wq': Wq, 'Wkv_down': Wkv_down, 'Wk_up': Wk_up, 'Wv_up': Wv_up, 'Wout': Wout}
    _L0_attn_in = _L0_attn_setup()

    def _L0_ffn_setup():
        import jax, jax.numpy as jnp
        import numpy as np
        H = 128
        I = 256
        E = 8
        TOP_K = 2
        NUM_SHARED = 1
        key = jax.random.key(seed)
        ks = jax.random.split(key, 9)
        s = 0.02
        x = jax.random.normal(ks[0], (2, 256, H), dtype=jnp.float32)
        sg_w = jax.random.normal(ks[1], (I, H), dtype=jnp.float32) * s
        su_w = jax.random.normal(ks[2], (I, H), dtype=jnp.float32) * s
        sd_w = jax.random.normal(ks[3], (H, I), dtype=jnp.float32) * s
        router_w = jax.random.normal(ks[4], (E, H), dtype=jnp.float32) * s
        routing_bias = jnp.zeros((E,), dtype=jnp.float32)
        wg = jax.random.normal(ks[5], (E, I, H), dtype=jnp.float32) * s
        wu = jax.random.normal(ks[6], (E, I, H), dtype=jnp.float32) * s
        wd = jax.random.normal(ks[7], (E, H, I), dtype=jnp.float32) * s
        return {'x': x, 'sg_w': sg_w, 'su_w': su_w, 'sd_w': sd_w, 'router_w': router_w, 'routing_bias': routing_bias, 'wg': wg, 'wu': wu, 'wd': wd}
    _L0_ffn_in = _L0_ffn_setup()
    _L0_c = _w((lambda *s: np.random.randn(*s).astype(np.float32) * 0.05)(32, 128))
    _L0_wmod = _w((lambda *s: np.random.randn(*s).astype(np.float32) * 0.05)(128, 6 * 128) * 128 ** (-0.5))

    def _L1_attn_setup():
        import jax, jax.numpy as jnp
        import numpy as np
        import math
        E, N, K, R = (128, 16, 4, 64)
        B, L = (2, 256)
        key = jax.random.key(seed)
        ks = jax.random.split(key, 8)
        gn = lambda k, sh, sc: jax.random.normal(k, sh, dtype=jnp.float32) * sc
        W_z = gn(ks[0], (E, E), E ** (-0.5))
        W_params = gn(ks[1], (R + 2 * N, E), E ** (-0.5))
        conv_w = gn(ks[2], (E, 1, K), 0.5)
        dt_std = R ** (-0.5) * 0.1
        W_dt = jax.random.uniform(ks[3], (E, R), jnp.float32, -dt_std, dt_std)
        b_dt = jnp.full((E,), math.log(math.expm1(0.001)), dtype=jnp.float32)
        A_log = jnp.tile(jnp.log(jnp.arange(1, N + 1, dtype=jnp.float32))[None, :], (E, 1))
        D = jnp.ones((E,), dtype=jnp.float32)
        W_out = gn(ks[4], (E, E), E ** (-0.5))
        x = jax.random.normal(ks[5], (B, L, E), dtype=jnp.float32)
        return dict(x=x, W_z=W_z, W_params=W_params, conv_w=conv_w, W_dt=W_dt, b_dt=b_dt, A_log=A_log, D=D, W_out=W_out)
    _L1_attn_in = _L1_attn_setup()

    def _L1_ffn_setup():
        import jax, jax.numpy as jnp
        import numpy as np
        DIM = 128

        def _reference_tuple_inner(x, W_r, W_k, W_v, mu_r, mu_k):
            B, T, C = x.shape
            x_prev = jnp.concatenate([jnp.zeros((B, 1, C), x.dtype), x[:, :-1, :]], axis=1)
            xr = mu_r * x + (1.0 - mu_r) * x_prev
            xk = mu_k * x + (1.0 - mu_k) * x_prev
            r = jax.nn.sigmoid(jnp.einsum('btc,dc->btd', xr, W_r))
            k = jnp.einsum('btc,dc->btd', xk, W_k)
            k_act = jnp.square(jax.nn.relu(k))
            out = r * jnp.einsum('btc,dc->btd', k_act, W_v)
            new_state = x[:, -1, :]
            return (out, new_state)
        key = jax.random.key(seed)
        ks = jax.random.split(key, 6)
        B, T, C = (8, 256, DIM)
        x = jax.random.normal(ks[0], (B, T, C), dtype=jnp.float32)
        s = 1.0 / np.sqrt(C)
        W_r = jax.random.uniform(ks[1], (C, C), jnp.float32, -s, s)
        W_k = jax.random.uniform(ks[2], (C, C), jnp.float32, -s, s)
        W_v = jax.random.uniform(ks[3], (C, C), jnp.float32, -s, s)
        mu_r = jax.random.uniform(ks[4], (C,), jnp.float32)
        mu_k = jax.random.uniform(ks[5], (C,), jnp.float32)
        return {'x': x, 'W_r': W_r, 'W_k': W_k, 'W_v': W_v, 'mu_r': mu_r, 'mu_k': mu_k}
    _L1_ffn_in = _L1_ffn_setup()
    _L1_c = _w((lambda *s: np.random.randn(*s).astype(np.float32) * 0.05)(32, 128))
    _L1_wmod = _w((lambda *s: np.random.randn(*s).astype(np.float32) * 0.05)(128, 6 * 128) * 128 ** (-0.5))
    _d = {'L0_attn_x_bld': _L0_attn_in['x_bld'], 'L0_attn_Wq': _L0_attn_in['Wq'], 'L0_attn_Wkv_down': _L0_attn_in['Wkv_down'], 'L0_attn_Wk_up': _L0_attn_in['Wk_up'], 'L0_attn_Wv_up': _L0_attn_in['Wv_up'], 'L0_attn_Wout': _L0_attn_in['Wout'], 'L0_ffn_sg_w': _L0_ffn_in['sg_w'], 'L0_ffn_su_w': _L0_ffn_in['su_w'], 'L0_ffn_sd_w': _L0_ffn_in['sd_w'], 'L0_ffn_router_w': _L0_ffn_in['router_w'], 'L0_ffn_routing_bias': _L0_ffn_in['routing_bias'], 'L0_ffn_wg': _L0_ffn_in['wg'], 'L0_ffn_wu': _L0_ffn_in['wu'], 'L0_ffn_wd': _L0_ffn_in['wd'], 'L0_c': _L0_c, 'L0_wmod': _L0_wmod, 'L1_attn_W_z': _L1_attn_in['W_z'], 'L1_attn_W_params': _L1_attn_in['W_params'], 'L1_attn_conv_w': _L1_attn_in['conv_w'], 'L1_attn_W_dt': _L1_attn_in['W_dt'], 'L1_attn_b_dt': _L1_attn_in['b_dt'], 'L1_attn_A_log': _L1_attn_in['A_log'], 'L1_attn_D': _L1_attn_in['D'], 'L1_attn_W_out': _L1_attn_in['W_out'], 'L1_ffn_W_r': _L1_ffn_in['W_r'], 'L1_ffn_W_k': _L1_ffn_in['W_k'], 'L1_ffn_W_v': _L1_ffn_in['W_v'], 'L1_ffn_mu_r': _L1_ffn_in['mu_r'], 'L1_ffn_mu_k': _L1_ffn_in['mu_k'], 'L1_c': _L1_c, 'L1_wmod': _L1_wmod}
    _x0 = _d['L0_attn_x_bld']
    _d['L0_attn_x_bld'] = jax.random.normal(jax.random.fold_in(jax.random.key(seed), 1), (32, 256, 128), dtype=_x0.dtype)
    del _x0
    return _d

def reference(L0_attn_x_bld, L0_attn_Wq, L0_attn_Wkv_down, L0_attn_Wk_up, L0_attn_Wv_up, L0_attn_Wout, L0_ffn_sg_w, L0_ffn_su_w, L0_ffn_sd_w, L0_ffn_router_w, L0_ffn_routing_bias, L0_ffn_wg, L0_ffn_wu, L0_ffn_wd, L0_c, L0_wmod, L1_attn_W_z, L1_attn_W_params, L1_attn_conv_w, L1_attn_W_dt, L1_attn_b_dt, L1_attn_A_log, L1_attn_D, L1_attn_W_out, L1_ffn_W_r, L1_ffn_W_k, L1_ffn_W_v, L1_ffn_mu_r, L1_ffn_mu_k, L1_c, L1_wmod):

    def _L0_attn_ref(x_bld, Wq, Wkv_down, Wk_up, Wv_up, Wout):
        import jax, jax.numpy as jnp
        import numpy as np
        B, L, D = (2, 256, 128)
        H, HD = (16, 64)
        LD = 32
        q_blhd = jnp.einsum('bld,dhk->blhk', x_bld, Wq)
        latent_bll = jnp.einsum('bld,dc->blc', x_bld, Wkv_down)
        k_blhd = jnp.einsum('blc,chk->blhk', latent_bll, Wk_up)
        v_blhd = jnp.einsum('blc,chk->blhk', latent_bll, Wv_up)
        attn = jnp.einsum('bqhd,bkhd->bhqk', q_blhd, k_blhd) / jnp.sqrt(jnp.asarray(HD, dtype=x_bld.dtype))
        l = x_bld.shape[1]
        mask = (jnp.arange(l)[None, :] <= jnp.arange(l)[:, None])[None, None]
        neg_inf = jnp.finfo(attn.dtype).min
        attn = jax.nn.softmax(jnp.where(mask, attn, neg_inf), axis=-1)
        y_blhd = jnp.einsum('bhqk,bkhd->bqhd', attn, v_blhd)
        return jnp.einsum('bqhd,hdo->bqo', y_blhd, Wout)

    def _L0_ffn_ref(x, sg_w, su_w, sd_w, router_w, routing_bias, wg, wu, wd):
        import jax, jax.numpy as jnp
        import numpy as np
        H = 128
        I = 256
        E = 8
        TOP_K = 2
        NUM_SHARED = 1
        orig_shape = x.shape
        xt = x.reshape(-1, H)
        T = xt.shape[0]
        shared = jax.nn.silu(xt @ sg_w.T) * (xt @ su_w.T) @ sd_w.T
        shared = shared / NUM_SHARED
        logits = xt @ router_w.T + routing_bias
        probs = jax.nn.sigmoid(logits)
        topk_p, topk_idx = jax.lax.top_k(probs, TOP_K)
        topk_p = topk_p / jnp.sum(topk_p, axis=-1, keepdims=True)
        w = jnp.zeros((T, E), dtype=xt.dtype)
        w = w.at[jnp.arange(T)[:, None], topk_idx].add(topk_p)
        g = jnp.einsum('th,eih->tei', xt, wg)
        u = jnp.einsum('th,eih->tei', xt, wu)
        h = jax.nn.silu(g) * u
        y = jnp.einsum('tei,ehi->teh', h, wd)
        routed = jnp.einsum('te,teh->th', w, y)
        return (shared + routed).reshape(orig_shape)

    def _L1_attn_ref(x, W_z, W_params, conv_w, W_dt, b_dt, A_log, D, W_out):
        import jax, jax.numpy as jnp
        import numpy as np
        import math
        E, N, K, R = (128, 16, 4, 64)
        B, L = (2, 256)
        b, l, e = x.shape
        n = A_log.shape[1]
        r = W_dt.shape[1]
        k = conv_w.shape[-1]
        z = x @ W_z.T
        params = x @ W_params.T
        dt_unproj = params[..., :r]
        C_proj = params[..., r + n:]
        dt = jax.nn.softplus(dt_unproj @ W_dt.T + b_dt)
        xc = jax.lax.conv_general_dilated(x.transpose(0, 2, 1), conv_w, (1,), [(k - 1, 0)], dimension_numbers=('NCH', 'OIH', 'NCH'), feature_group_count=e)
        u = jax.nn.silu(xc.transpose(0, 2, 1))
        A = -jnp.exp(A_log)
        A_tilde = jnp.exp(dt[..., None] * A[None, None])
        B_tilde = jnp.where(jnp.abs(A)[None, None] < 1e-05, dt[..., None], (A_tilde - 1.0) / (A[None, None] + 1e-10))
        h0 = B_tilde[:, 0] * u[:, 0, :, None]

        def step(h, inp):
            a, bt, uu = inp
            h_new = a * h + bt * uu[..., None]
            return (h_new, h_new)
        xs = (A_tilde[:, :-1].transpose(1, 0, 2, 3), B_tilde[:, :-1].transpose(1, 0, 2, 3), u[:, :-1].transpose(1, 0, 2))
        _, hs = jax.lax.scan(step, h0, xs)
        h = jnp.concatenate([h0[None], hs], axis=0).transpose(1, 0, 2, 3)
        y = jnp.einsum('bln,blen->ble', C_proj, h)
        y_ssm = y + u * D
        y_gated = y_ssm * jax.nn.silu(z)
        return y_gated @ W_out.T

    def _L1_ffn_ref(x, W_r, W_k, W_v, mu_r, mu_k):
        import jax, jax.numpy as jnp
        import numpy as np
        DIM = 128

        def _reference_tuple_inner(x, W_r, W_k, W_v, mu_r, mu_k):
            B, T, C = x.shape
            x_prev = jnp.concatenate([jnp.zeros((B, 1, C), x.dtype), x[:, :-1, :]], axis=1)
            xr = mu_r * x + (1.0 - mu_r) * x_prev
            xk = mu_k * x + (1.0 - mu_k) * x_prev
            r = jax.nn.sigmoid(jnp.einsum('btc,dc->btd', xr, W_r))
            k = jnp.einsum('btc,dc->btd', xk, W_k)
            k_act = jnp.square(jax.nn.relu(k))
            out = r * jnp.einsum('btc,dc->btd', k_act, W_v)
            new_state = x[:, -1, :]
            return (out, new_state)
        return _reference_tuple_inner(x, W_r, W_k, W_v, mu_r, mu_k)[0]
    x = L0_attn_x_bld
    mod = (_silu(L0_c) @ L0_wmod).reshape(L0_c.shape[0], 6, 1, -1)
    sa, ca, ga, sb, cb, gb = (mod[:, 0], mod[:, 1], mod[:, 2], mod[:, 3], mod[:, 4], mod[:, 5])
    ga = (2 * (ga >= 0) - 1) * jnp.maximum(jnp.abs(ga), 0.25)
    gb = (2 * (gb >= 0) - 1) * jnp.maximum(jnp.abs(gb), 0.25)
    h = _layernorm(x, axis=-1) * (1 + ca) + sa
    x = x + ga * _L0_attn_ref(h, L0_attn_Wq, L0_attn_Wkv_down, L0_attn_Wk_up, L0_attn_Wv_up, L0_attn_Wout)
    h = _layernorm(x, axis=-1) * (1 + cb) + sb
    x = x + gb * _L0_ffn_ref(h, L0_ffn_sg_w, L0_ffn_su_w, L0_ffn_sd_w, L0_ffn_router_w, L0_ffn_routing_bias, L0_ffn_wg, L0_ffn_wu, L0_ffn_wd)
    mod = (_silu(L1_c) @ L1_wmod).reshape(L1_c.shape[0], 6, 1, -1)
    sa, ca, ga, sb, cb, gb = (mod[:, 0], mod[:, 1], mod[:, 2], mod[:, 3], mod[:, 4], mod[:, 5])
    ga = (2 * (ga >= 0) - 1) * jnp.maximum(jnp.abs(ga), 0.25)
    gb = (2 * (gb >= 0) - 1) * jnp.maximum(jnp.abs(gb), 0.25)
    h = _layernorm(x, axis=-1) * (1 + ca) + sa
    x = x + ga * _L1_attn_ref(h, L1_attn_W_z, L1_attn_W_params, L1_attn_conv_w, L1_attn_W_dt, L1_attn_b_dt, L1_attn_A_log, L1_attn_D, L1_attn_W_out)
    h = _layernorm(x, axis=-1) * (1 + cb) + sb
    x = x + gb * _L1_ffn_ref(h, L1_ffn_W_r, L1_ffn_W_k, L1_ffn_W_v, L1_ffn_mu_r, L1_ffn_mu_k)
    return x

_drawn_inputs = setup_inputs


def setup_inputs(seed=0):
    import zlib

    import numpy as np

    out = dict(_drawn_inputs(seed))
    spreads = {'L0_ffn_routing_bias': (0.0, 0.8),
     'L1_attn_b_dt': (-6.907255172729492, 0.6),
     'L1_attn_D': (1.0, 0.6)}
    factors = {'L0_ffn_sg_w': 8.0,
     'L0_ffn_su_w': 8.0,
     'L0_ffn_sd_w': 8.0,
     'L0_ffn_router_w': 8.0,
     'L0_ffn_wg': 8.0,
     'L0_ffn_wu': 8.0,
     'L0_ffn_wd': 8.0,
     'L1_attn_W_params': 3.786,
     'L1_attn_W_dt': 8.0,
     'L1_attn_A_log': 5.892,
     'L1_ffn_W_r': 8.0,
     'L1_ffn_W_k': 3.003,
     'L1_ffn_W_v': 2.774,
     'L1_ffn_mu_r': 8.0,
     'L1_ffn_mu_k': 4.684}
    for name, (base, spread) in spreads.items():
        noise = np.random.default_rng([zlib.crc32(name.encode()), seed]).standard_normal(out[name].shape)
        drawn = base * np.exp(spread * noise) if base else spread * noise
        out[name] = jnp.asarray(drawn.astype(out[name].dtype))
    for name, factor in factors.items():
        out[name] = (out[name] * factor).astype(out[name].dtype)
    return out
```

```python
from contextlib import ExitStack

import concourse.bass as bass
from concourse import mybir

P = 128
SEQ = 256
NSEQ = 32
TOK = NSEQ * SEQ
PAD = 2
HEADS = 16
LD = 32
HD = 64
PAIRS = HEADS // 2
GROUPS = HEADS // 4
NEXP = 8
NALL = NEXP + 1
NST = 16
RDT = 64
TAPS = 4
NEG = -1.0e30
EPS = 1e-5

F32 = mybir.dt.float32
F32R = mybir.dt.float32r
BF16 = mybir.dt.bfloat16
ACT = mybir.ActivationFunctionType
ALU = mybir.AluOpType
AX = mybir.AxisListType.X
ds = bass.ds

SH_A, SC_A, GA, SH_B, SC_B, GB = range(6)


class Shared:
    pass


def constants_and_modulation(nc, ctx, w, S):
    def sb(name, shape, dt=F32):
        return ctx.enter_context(nc.sbuf_tensor(name, shape, dt))

    S.X = sb("X", [P, TOK + PAD * SEQ])
    S.mod = [sb("mod0", [P, 6, NSEQ + PAD]), sb("mod1", [P, 6, NSEQ + PAD])]
    S.meanw = sb("meanw", [P, P])
    S.ident = sb("ident", [P, P])
    S.identb = sb("identb", [P, P], BF16)
    S.eps = sb("eps", [P, 1])
    S.spare = sb("spare", [P, 8])

    with ExitStack() as loc:
        def lsb(name, shape, dt=F32):
            return loc.enter_context(nc.sbuf_tensor(name, shape, dt))

        cT = [lsb("cT0", [P, NSEQ]), lsb("cT1", [P, NSEQ])]
        wmod = [lsb("wm0", [P, 6, P]), lsb("wm1", [P, 6, P])]
        sc = [lsb("siluc0", [P, NSEQ]), lsb("siluc1", [P, NSEQ])]
        gpos = lsb("gpos", [P, NSEQ])
        gneg = lsb("gneg", [P, NSEQ])
        ps = loc.enter_context(nc.psum_tensor("ps_mod", [P, 2, 512], F32))
        sem = lambda n: loc.enter_context(nc.semaphore(n))
        loaded, x_loaded, silu_done, mod_done, filled, gate_step, built = map(
            sem, ["loaded", "x_loaded", "silu_done", "mod_done", "filled", "gate_step", "built"])
        with nc.Block() as block:

            @block.sync
            def _(sp):
                for l in range(2):
                    sp.dma_start(cT[l][:], w[f"c{l}"]).then_inc(loaded, 16)
                    sp.dma_start(wmod[l][:], w[f"wmod{l}"]).then_inc(loaded, 16)
                sp.dma_start(S.X[:, 0:TOK], w["x"]).then_inc(x_loaded, 16)
                sp.wait_ge(x_loaded, 16)

            @block.scalar
            def _(act):
                act.wait_ge(loaded, 64)
                for l in range(2):
                    nc.scalar.activation(sc[l][:], cT[l][:], ACT.Silu).then_inc(silu_done, 1)

            @block.tensor
            def _(pe):
                for l in range(2):
                    pe.wait_ge(silu_done, l + 1)
                    for r in range(6):
                        last = nc.tensor.matmul(ps[:, l, r * NSEQ:(r + 1) * NSEQ], wmod[l][:, r, :], sc[l][:],
                                                start=(r == 0), stop=(r == 5))
                    last.then_inc(mod_done, 1)

            @block.gpsimd
            def _(pool):
                nc.gpsimd.memset(S.meanw[:], 1.0 / P)
                nc.gpsimd.memset(S.eps[:], EPS)
                nc.gpsimd.memset(S.X[:, TOK:], 0.0)
                for l in range(2):
                    nc.gpsimd.memset(S.mod[l][:, :, NSEQ:], 0.0)
                nc.gpsimd.memset(S.ident[:], 0.0).then_inc(filled, 1)
                pool.wait_ge(filled, 1)
                nc.gpsimd.affine_select(out=S.ident[:], in_=S.ident[:], compare_op=ALU.not_equal, fill=1.0,
                                        base=0, pattern=[[-1, P]], channel_multiplier=1).then_inc(filled, 1)
                pool.wait_ge(filled, 2)
                nc.gpsimd.tensor_copy(S.identb[:], S.ident[:])

            @block.vector
            def _(dve):
                n = 0
                for l in range(2):
                    dve.wait_ge(mod_done, l + 1)
                    for r in range(6):
                        row = ps[:, l, r * NSEQ:(r + 1) * NSEQ]
                        out = S.mod[l][:, r, 0:NSEQ]
                        if r in (SH_A, SH_B):
                            nc.vector.tensor_copy(out, row)
                        elif r in (SC_A, SC_B):
                            nc.vector.tensor_scalar(out, row, 1.0, None, ALU.add)
                        else:
                            nc.vector.tensor_scalar(gpos[:], row, 0.25, None, ALU.max)
                            nc.vector.tensor_scalar(gneg[:], row, -0.25, None, ALU.min).then_inc(gate_step, 1)
                            dve.wait_ge(gate_step, 3 * n + 1)
                            nc.vector.scalar_tensor_tensor(gpos[:], row, 0.0, gpos[:], ALU.is_ge, ALU.mult)
                            nc.vector.scalar_tensor_tensor(gneg[:], row, 0.0, gneg[:], ALU.is_lt, ALU.mult
                                                           ).then_inc(gate_step, 1)
                            dve.wait_ge(gate_step, 3 * n + 2)
                            nc.vector.tensor_tensor(out, gpos[:], gneg[:], ALU.add).then_inc(gate_step, 1)
                            n += 1
                            dve.wait_ge(gate_step, 3 * n)


def attention(nc, w, S):
    with ExitStack() as ctx:
        def sb(name, shape, dt=F32):
            return ctx.enter_context(nc.sbuf_tensor(name, shape, dt))

        def pb(name, n):
            return ctx.enter_context(nc.psum_tensor(name, [P, n * 512], F32))

        wq = sb("wq", [HD, HEADS, P])
        wku = sb("wku", [HD, HEADS, LD])
        wvu = sb("wvu", [HD, HEADS, LD])
        wo = sb("wo", [HD, HEADS, P])
        wlat = sb("wlat", [P, 4, LD])
        wqk = sb("wqk", [P, HEADS, 4, LD])
        wvo = sb("wvo", [P, GROUPS, P])
        mask_s = sb("mask_s", [P, P], BF16)
        mask_t = sb("mask_t", [P, P], BF16)
        sel0 = sb("sel0", [2 * HEADS, HEADS, P])
        sel = sb("sel", [2 * HEADS, HEADS, P], F32R)
        ones = sb("ones", [P, LD])

        xc = sb("xc", [P, SEQ])
        sq = sb("sq", [P, SEQ])
        lnv = sb("lnv", [P, SEQ])
        rstd = sb("rstd", [P, SEQ])
        H = sb("H", [P, 2, SEQ])
        lat = sb("lat", [P, 2, SEQ], F32R)
        lat_tok = sb("lat_tok", [P, 2, 2, LD])
        Q = sb("Q", [P, 2, HEADS, SEQ], F32R)
        mx = sb("mx", [P, 2, HEADS])
        mhl = sb("mhl", [P, 2, 2, HEADS])
        nm = sb("nm", [2 * HEADS, SEQ], F32R)
        prob = sb("prob", [P, 4, 768])
        lden = sb("lden", [P, SEQ])
        rden = sb("rden", [P, SEQ])
        cn = sb("cn", [P, GROUPS, SEQ])

        psS, psT = pb("psS", 2), pb("psT", 2)
        psQ, psC, psM, psY = pb("psQ", 1), pb("psC", 1), pb("psM", 1), pb("psY", 1)

        with ExitStack() as pre:
            sem = lambda n: pre.enter_context(nc.semaphore(n))
            loaded, made, filled, copied = map(sem, ["a_loaded", "a_made", "a_filled", "a_copied"])
            with nc.Block() as block:

                @block.sync
                def _(sp):
                    for t, name in ((wq, "wqT"), (wku, "wkuT"), (wvu, "wvuT"), (wo, "wo")):
                        sp.dma_start(t[:], w[name]).then_inc(loaded, 16)
                    for r in range(4):
                        sp.dma_start(wlat[:, r, :], w["wlat"]).then_inc(loaded, 16)
                    sp.wait_ge(loaded, 128)

                @block.gpsimd
                def _(pool):
                    nc.gpsimd.memset(ones[:], 1.0)
                    nc.gpsimd.memset(sel0[:], 0.0)
                    nc.gpsimd.memset(mask_s[:], 0.0)
                    nc.gpsimd.memset(mask_t[:], 0.0).then_inc(filled, 1)
                    pool.wait_ge(filled, 1)
                    nc.gpsimd.affine_select(out=sel0[:], in_=sel0[:], compare_op=ALU.not_equal, fill=1.0,
                                            base=0, pattern=[[-1, HEADS], [0, P]], channel_multiplier=1
                                            ).then_inc(filled, 1)
                    nc.gpsimd.affine_select(out=mask_s[:], in_=mask_s[:], compare_op=ALU.is_ge, fill=NEG,
                                            base=0, pattern=[[-1, P]], channel_multiplier=1)
                    nc.gpsimd.affine_select(out=mask_t[:], in_=mask_t[:], compare_op=ALU.is_ge, fill=NEG,
                                            base=0, pattern=[[1, P]], channel_multiplier=-1)
                    pool.wait_ge(filled, 2)
                    nc.gpsimd.affine_select(out=sel0[:], in_=sel0[:], compare_op=ALU.not_equal, fill=1.0,
                                            base=-HEADS, pattern=[[-1, HEADS], [0, P]], channel_multiplier=1
                                            ).then_inc(filled, 1)

                @block.tensor
                def _(pe):
                    pe.wait_ge(loaded, 128)
                    for h in range(HEADS):
                        last = nc.tensor.matmul(psS[:, h * LD:(h + 1) * LD], wq[:, h, :], wku[:, h, :],
                                                start=(h == 0), stop=(h == HEADS - 1))
                    for h in range(HEADS):
                        g, q = divmod(h, 4)
                        last = nc.tensor.matmul(psT[LD * q:LD * (q + 1), g * P:(g + 1) * P], wvu[:, h, :],
                                                wo[:, h, :], start=(g == 0), stop=(g == GROUPS - 1))
                    last.then_inc(made, 1)

                @block.vector
                def _(dve):
                    dve.wait_ge(made, 1)
                    for r in range(4):
                        nc.vector.tensor_scalar(wqk[:, :, r, :], psS[:, 0:512].rearrange("p (h c) -> p h c", h=HEADS),
                                                HD ** -0.5, None, ALU.mult)
                    nc.vector.tensor_copy(wvo[:], psT[:, 0:512].rearrange("p (g c) -> p g c", g=GROUPS))
                    dve.wait_ge(filled, 3)
                    nc.vector.tensor_copy(sel[:], sel0[:]).then_inc(copied, 1)

        names = ["mean_done", "xc_done", "sq_done", "var_done", "lnv_done", "rstd_done", "xn_done", "h_done",
                 "lat_done", "lat_hi", "lat_lo", "q_done", "q_hi", "q_lo", "s_done", "max_done", "mh_done",
                 "mhl_done", "mt_done", "nm_done", "st_done", "exp_done", "pv_done", "lden_done", "rden_done",
                 "ctx_done", "y_done", "x_done"]
        (mean_done, xc_done, sq_done, var_done, lnv_done, rstd_done, xn_done, h_done, lat_done, lat_hi, lat_lo,
         q_done, q_hi, q_lo, s_done, max_done, mh_done, mhl_done, mt_done, nm_done, st_done, exp_done, pv_done,
         lden_done, rden_done, ctx_done, y_done, x_done) = [ctx.enter_context(nc.semaphore("a_" + n)) for n in names]

        EXP0, PV0, CTX0, X0 = 1, 2, 1, 1
        mod = S.mod[0]

        with nc.Block() as block:

            @block.tensor
            def _(pe):
                def mean(n, first=False):
                    if not first:
                        pe.wait_ge(lat_lo, n)
                    nc.tensor.matmul(psM[:, 0:SEQ], S.meanw[:], S.X[:, ds(n * SEQ, SEQ)],
                                     start=True, stop=True).then_inc(mean_done, 1)

                def var(n):
                    pe.wait_ge(sq_done, n + 1)
                    nc.tensor.matmul(psM[:, 0:SEQ], S.meanw[:], sq[:], start=True, stop=True).then_inc(var_done, 1)

                def latent(n, par):
                    pe.wait_ge(h_done, n + 1)
                    nc.tensor.matmul(psM[:, 0:SEQ], wlat[:].rearrange("p r c -> p (r c)"), H[:, par, :],
                                     start=True, stop=False)
                    for kb in range(2):
                        last = nc.tensor.matmul(psM[:, SEQ + kb * LD:SEQ + (kb + 1) * LD],
                                                H[:, par, kb * P:(kb + 1) * P], wlat[:, 0, :],
                                                start=False, stop=(kb == 1))
                    last.then_inc(lat_done, 1)

                def query(n, par, p, first=False):
                    if not (first and p == 0):
                        pe.wait_ge(q_lo, n * PAIRS + p)
                    if p == 0:
                        pe.wait_ge(h_done, n + 1)
                        if not first:
                            pe.wait_ge(nm_done, n)
                    for k in range(2):
                        last = nc.tensor.matmul(psQ[:, k * SEQ:(k + 1) * SEQ],
                                                wqk[:, 2 * p + k, :, :].rearrange("p r c -> p (r c)"),
                                                H[:, par, :], start=(k == 0), stop=(k == 1))
                    last.then_inc(q_done, 1)

                def scores(n, par, p, first=False):
                    pe.wait_ge(q_lo, n * PAIRS + (p + 1))
                    if not (first and p == 0):
                        pe.wait_ge(max_done, n * PAIRS + p)
                    if p == 0:
                        pe.wait_ge(lat_lo, n + 1)
                    for k in range(2):
                        h, wide = 2 * p + k, 512 * k
                        near = 256 + 128 * k
                        if k == 1:
                            nc.tensor.matmul(psS[:, near:near + P], Q[:, par, h, 0:P], lat[:, par, 0:P],
                                             start=False, stop=False)
                            nc.tensor.matmul(psS[:, near:near + P], S.identb[:], mask_s[:], start=False, stop=True)
                        nc.tensor.matmul(psS[:, wide:wide + SEQ], Q[:, par, h, P:SEQ], lat[:, par, :],
                                         start=True, stop=False)
                        last = nc.tensor.matmul(psS[:, wide + P:wide + SEQ], S.identb[:], mask_s[:],
                                                start=False, stop=(k == 1))
                        if k == 0:
                            nc.tensor.matmul(psS[:, near:near + P], Q[:, par, h, 0:P], lat[:, par, 0:P],
                                             start=False, stop=False)
                            nc.tensor.matmul(psS[:, near:near + P], S.identb[:], mask_s[:], start=False, stop=False)
                    last.then_inc(s_done, 1)

                def scores_t(n, par, p):
                    if p == 0:
                        pe.wait_ge(nm_done, n + 1)
                    pe.wait_ge(exp_done, n * PAIRS + (p + EXP0))
                    for k in range(2):
                        h, wide = 2 * p + k, 512 * k
                        near = 256 + 128 * k

                        def far_keys(stop):
                            nc.tensor.matmul(psT[:, near:near + P], lat[:, par, P:SEQ], Q[:, par, h, P:SEQ],
                                             start=False, stop=False)
                            nc.tensor.matmul(psT[:, near:near + P], sel[:, h, :], nm[:, P:SEQ],
                                             start=False, stop=False)
                            nc.tensor.matmul(psT[:, near:near + P], S.identb[:], mask_t[:], start=False, stop=stop)

                        if k == 1:
                            far_keys(True)
                        nc.tensor.matmul(psT[:, wide:wide + SEQ], lat[:, par, 0:P], Q[:, par, h, :],
                                         start=True, stop=False)
                        nc.tensor.matmul(psT[:, wide:wide + SEQ], sel[:, h, :], nm[:], start=False, stop=False)
                        last = nc.tensor.matmul(psT[:, wide:wide + P], S.identb[:], mask_t[:],
                                                start=False, stop=(k == 1))
                        if k == 0:
                            far_keys(False)
                    last.then_inc(st_done, 1)

                def values(n, par, g):
                    pe.wait_ge(exp_done, n * PAIRS + (2 * g + 2 + EXP0))
                    pe.wait_ge(ctx_done, n * GROUPS + (g + CTX0))
                    for off, kb in ((0, 0), (0, 1), (SEQ, 0), (SEQ, 1)):
                        for q in range(4):
                            k = q % 2
                            at, cols = ((512 * k, SEQ), (256 + 128 * k, P))[kb]
                            first = off + SEQ - cols
                            last = nc.tensor.matmul(
                                psC[LD * q:LD * (q + 1), first:off + SEQ],
                                lat_tok[:, par, kb, :] if off == 0 else ones[:],
                                prob[:, (2 * g + q // 2) % 4, at:at + cols],
                                start=(off == 0 and kb == 0), stop=(off == SEQ and kb == 1))
                    last.then_inc(pv_done, 1)

                def project(n, g):
                    if g == 0:
                        pe.wait_ge(x_done, n + X0)
                    pe.wait_ge(ctx_done, n * GROUPS + (g + 1 + CTX0))
                    last = nc.tensor.matmul(psY[:, 0:SEQ], wvo[:, g, :], cn[:, g, :],
                                            start=(g == 0), stop=(g == GROUPS - 1))
                    if g == GROUPS - 1:
                        last.then_inc(y_done, 1)

                def max_t(n):
                    pe.wait_ge(mhl_done, n + 1)
                    pe.wait_ge(q_lo, n * PAIRS + PAIRS)
                    for qb in range(2):
                        last = nc.tensor.transpose(psQ[0:2 * HEADS, qb * P:(qb + 1) * P],
                                                   mhl[:, qb, :, :].rearrange("p a h -> p (a h)"), S.ident[:])
                    last.then_inc(mt_done, 1)

                mean(0, first=True)
                var(0)
                latent(0, 0)
                mean(1)
                for p in range(PAIRS):
                    query(0, 0, p, first=True)
                    if p > 0:
                        scores(0, 0, p - 1, first=True)
                    if p == 3:
                        var(1)
                scores(0, 0, PAIRS - 1, first=True)
                latent(1, 1)
                max_t(0)
                with nc.tensor.Fori(0, NSEQ // 2) as j:
                    for par in range(2):
                        n = j * 2 + par
                        for p in range(PAIRS):
                            query(n + 1, 1 - par, p)
                            if p > 0:
                                scores(n + 1, 1 - par, p - 1)
                            scores_t(n, par, p)
                            if p >= 2 and p % 2 == 0:
                                values(n, par, p // 2 - 1)
                            if p == 1:
                                mean(n + 2)
                            if p == 4:
                                var(n + 2)
                            if p in (4, 6):
                                project(n, p // 2 - 2)
                        scores(n + 1, 1 - par, PAIRS - 1)
                        values(n, par, GROUPS - 1)
                        latent(n + 2, par)
                        project(n, 2)
                        max_t(n + 1)
                        project(n, 3)

            @block.scalar
            def _(act):
                def square(n):
                    act.wait_ge(xc_done, n + 1)
                    nc.scalar.activation(sq[:], xc[:], ACT.Square).then_inc(sq_done, 1)

                def inv_std(n):
                    act.wait_ge(var_done, n + 1)
                    nc.scalar.activation(lnv[:], psM[:, 0:SEQ], ACT.Ln, bias=S.eps[:, 0:1]).then_inc(lnv_done, 1)
                    act.wait_ge(lnv_done, n + 1)
                    nc.scalar.activation(rstd[:], lnv[:], ACT.Exp, scale=-0.5).then_inc(rstd_done, 1)

                def latent_hi(n, par):
                    act.wait_ge(lat_done, n + 1)
                    nc.scalar.copy(lat[:, par, :], psM[:, 0:SEQ]).then_inc(lat_hi, 1)

                def query_hi(n, par, p):
                    act.wait_ge(q_done, n * PAIRS + (p + 1))
                    nc.scalar.copy(Q[:, par, 2 * p:2 * p + 2, :], psQ[:, :].rearrange("p (h q) -> p h q", h=2)
                                   ).then_inc(q_hi, 1)

                def max_copy(n):
                    act.wait_ge(mt_done, n + 1)
                    nc.scalar.copy(nm[:], psQ[0:2 * HEADS, 0:SEQ]).then_inc(nm_done, 1)

                def softmax_exp(n, p):
                    act.wait_ge(st_done, n * PAIRS + (p + 1))
                    if p % 2 == 0:
                        act.wait_ge(pv_done, n * GROUPS + (p // 2 - 1 + PV0))
                    nc.scalar.activation(prob[:, p % 4, :], psT[:, 0:768], ACT.Exp).then_inc(exp_done, 1)

                def inv_den(n, g):
                    act.wait_ge(pv_done, n * GROUPS + (g + 1 + PV0))
                    nc.scalar.activation(lden[:], psC[:, SEQ:512], ACT.Ln).then_inc(lden_done, 1)
                    act.wait_ge(lden_done, n * GROUPS + (g + 1))
                    nc.scalar.activation(rden[:], lden[:], ACT.Exp, scale=-1.0).then_inc(rden_done, 1)

                nc.scalar.preload_act_table_set("natural_log_exp_and_others")
                square(0)
                inv_std(0)
                latent_hi(0, 0)
                square(1)
                for p in range(PAIRS):
                    query_hi(0, 0, p)
                    if p == 4:
                        inv_std(1)
                latent_hi(1, 1)
                max_copy(0)
                nc.scalar.copy(S.spare[:, 4:5], S.eps[:, 0:1]).then_inc(exp_done, EXP0)
                with nc.scalar.Fori(0, NSEQ // 2) as j:
                    for par in range(2):
                        n = j * 2 + par
                        for p in range(PAIRS):
                            query_hi(n + 1, 1 - par, p)
                            softmax_exp(n, p)
                            if p == 2:
                                square(n + 2)
                            if p == 5:
                                inv_std(n + 2)
                            if p >= 3 and p % 2 == 1:
                                inv_den(n, (p - 3) // 2)
                        inv_den(n, GROUPS - 1)
                        latent_hi(n + 2, par)
                        max_copy(n + 1)

            @block.vector
            def _(dve):
                def center(n):
                    dve.wait_ge(mean_done, n + 1)
                    nc.vector.tensor_tensor(xc[:], S.X[:, ds(n * SEQ, SEQ)], psM[:, 0:SEQ], ALU.subtract
                                            ).then_inc(xc_done, 1)

                def normalize(n, par):
                    dve.wait_ge(rstd_done, n + 1)
                    nc.vector.tensor_tensor(xc[:], xc[:], rstd[:], ALU.mult).then_inc(xn_done, 1)
                    dve.wait_ge(xn_done, n + 1)
                    nc.vector.tensor_scalar(H[:, par, :], xc[:], mod[:, SC_A, ds(n, 1)], mod[:, SH_A, ds(n, 1)],
                                            ALU.mult, ALU.add).then_inc(h_done, 1)

                def latent_lo(n, par):
                    dve.wait_ge(lat_hi, n + 1)
                    for r in (1, 3):
                        rows = slice(LD * r, LD * (r + 1))
                        nc.vector.tensor_tensor(lat[rows, par, :], psM[rows, 0:SEQ], lat[rows, par, :], ALU.subtract)
                    nc.vector.tensor_copy(lat_tok[:, par, :, :],
                                          psM[:, SEQ:SEQ + 2 * LD].rearrange("p (k c) -> p k c", k=2)
                                          ).then_inc(lat_lo, 1)

                def query_lo(n, par, p):
                    dve.wait_ge(q_hi, n * PAIRS + (p + 1))
                    half = slice(2 * LD, 4 * LD)
                    nc.vector.tensor_tensor(Q[half, par, 2 * p:2 * p + 2, :],
                                            psQ[half, :].rearrange("p (h q) -> p h q", h=2),
                                            Q[half, par, 2 * p:2 * p + 2, :], ALU.subtract).then_inc(q_lo, 1)

                def maximum(n, p):
                    dve.wait_ge(s_done, n * PAIRS + (p + 1))
                    nc.vector.tensor_reduce(mx[:, 1, 2 * p:2 * p + 2],
                                            psS[:, :].rearrange("p (h q) -> p h q", h=2)[:, :, 0:SEQ], AX, ALU.max)
                    nc.vector.tensor_reduce(mx[:, 0, 2 * p:2 * p + 2],
                                            psS[:, 256:512].rearrange("p (h q) -> p h q", h=2), AX, ALU.max
                                            ).then_inc(max_done, 1)

                def max_split(n):
                    dve.wait_ge(max_done, n * PAIRS + PAIRS)
                    nc.vector.tensor_scalar(mhl[:, :, 0, :].bitcast(F32R), mx[:], -1.0, None, ALU.mult
                                            ).then_inc(mh_done, 1)
                    dve.wait_ge(mh_done, n + 1)
                    nc.vector.scalar_tensor_tensor(mhl[:, :, 1, :], mx[:], -1.0, mhl[:, :, 0, :],
                                                   ALU.mult, ALU.subtract).then_inc(mhl_done, 1)

                def context(n, g):
                    dve.wait_ge(rden_done, n * GROUPS + (g + 1))
                    nc.vector.tensor_tensor(cn[:, g, :], psC[:, 0:SEQ], rden[:], ALU.mult).then_inc(ctx_done, 1)

                def residual(n):
                    dve.wait_ge(y_done, n + 1)
                    x = S.X[:, ds(n * SEQ, SEQ)]
                    nc.vector.scalar_tensor_tensor(x, psY[:, 0:SEQ], mod[:, GA, ds(n, 1)], x, ALU.mult, ALU.add
                                                   ).then_inc(x_done, 1)

                nc.vector.memset(S.spare[:, 0:1], 0.0).then_inc(pv_done, PV0)
                nc.vector.memset(S.spare[:, 1:2], 0.0).then_inc(ctx_done, CTX0)
                nc.vector.memset(S.spare[:, 2:3], 0.0).then_inc(x_done, X0)
                center(0)
                normalize(0, 0)
                latent_lo(0, 0)
                center(1)
                for p in range(PAIRS):
                    query_lo(0, 0, p)
                    if p > 0:
                        maximum(0, p - 1)
                    if p == 5:
                        normalize(1, 1)
                maximum(0, PAIRS - 1)
                max_split(0)
                latent_lo(1, 1)
                with nc.vector.Fori(0, NSEQ // 2) as j:
                    for par in range(2):
                        n = j * 2 + par
                        for p in range(PAIRS):
                            query_lo(n + 1, 1 - par, p)
                            if p > 0:
                                maximum(n + 1, p - 1)
                            if p == 2:
                                center(n + 2)
                            if p == 6:
                                normalize(n + 2, par)
                            if p >= 3 and p % 2 == 1:
                                context(n, (p - 3) // 2)
                        maximum(n + 1, PAIRS - 1)
                        max_split(n + 1)
                        context(n, GROUPS - 1)
                        latent_lo(n + 2, par)
                        residual(n)


MT = 512
NT = TOK // MT
SPT = MT // SEQ
UNITS = 2 * NALL
LEAD = 3
SUB = MT // P


def moe(nc, w, S):
    with ExitStack() as ctx:
        def sb(name, shape, dt=F32):
            return ctx.enter_context(nc.sbuf_tensor(name, shape, dt))

        def pb(name, n):
            return ctx.enter_context(nc.psum_tensor(name, [P, n, 512], F32))

        WG = [sb(f"WG{i}", [P, NALL, 2, P], F32R) for i in range(2)]
        WU = [sb(f"WU{i}", [P, NALL, 2, P], F32R) for i in range(2)]
        WD = sb("WD", [P, NALL, 2, P])
        wr = sb("wr_m", [P, NEXP])
        bias = sb("bias_m", [P, SUB, NEXP])
        tri = sb("tri", [P, NEXP, NEXP])
        sel0 = sb("sel0_m", [2 * NALL, NALL, P])
        sel = sb("sel_m", [2 * NALL, NALL, P], F32R)

        xc = sb("xc_m", [P, MT])
        sq = sb("sq_m", [P, MT])
        lnv = sb("lnv_m", [P, MT])
        rstd = sb("rstd_m", [P, MT])
        H = sb("H_m", [P, 2, MT])
        Hh = sb("Hh_m", [P, 2, MT], F32R)
        Hl = sb("Hl_m", [P, 2, MT], F32R)
        lg = sb("lg", [P, SUB, NEXP])
        pr = sb("pr", [P, SUB, NEXP])
        beats = sb("beats", [P, SUB, NEXP, NEXP])
        ties = sb("ties", [P, SUB, NEXP, NEXP])
        rank = sb("rank", [P, SUB, NEXP])
        pick = sb("pick", [P, SUB, NEXP])
        psum2 = sb("psum2", [P, SUB])
        wt = sb("wt", [P, SUB, NEXP])
        whl = sb("whl", [P, SUB, 2, NALL])
        wT = sb("wT", [2 * NALL, 2, MT], F32R)
        sg = sb("sg", [P, 2, MT])
        tt = sb("tt", [P, 2, MT])
        wbs = sb("wbs", [P, 2, MT])
        tw = sb("tw", [P, 4, MT])

        psG, psU, psY = pb("psG", 2), pb("psU", 2), pb("psY_m", 2)
        psW, psM = pb("psW", 1), pb("psM_m", 1)

        with ExitStack() as pre:
            sem = lambda n: pre.enter_context(nc.semaphore(n))
            loaded, high, filled, low = map(sem, ["m_loaded", "m_high", "m_filled", "m_low"])
            raw = [pre.enter_context(nc.sbuf_tensor(n, [P, NALL, 2, P], F32)) for n in ("rawG", "rawU")]
            with nc.Block() as block:

                @block.sync
                def _(sp):
                    for t, routed, shared in ((raw[0], "wg", "sg"), (raw[1], "wu", "su"), (WD, "wd", "sd")):
                        if routed == "wd":
                            sp.dma_start(t[:, 0:NEXP, :, :], w[routed]).then_inc(loaded, 16)
                            sp.dma_start(t[:, NEXP, :, :], w[shared]).then_inc(loaded, 16)
                        else:
                            sp.dma_start(t[:, 0:NEXP, :, :].rearrange("p e a i -> p e (a i)"), w[routed]
                                         ).then_inc(loaded, 16)
                            sp.dma_start(t[:, NEXP, :, :].rearrange("p a i -> p (a i)"), w[shared]
                                         ).then_inc(loaded, 16)
                    sp.dma_start(wr[:], w["router"]).then_inc(loaded, 16)
                    for s in range(SUB):
                        sp.dma_start(bias[:, s, :], w["rbias"].to_broadcast([P, NEXP])).then_inc(loaded, 16)
                    sp.wait_ge(loaded, 16 * (7 + SUB))

                @block.gpsimd
                def _(pool):
                    nc.gpsimd.memset(tri[:], 1.0)
                    nc.gpsimd.memset(whl[:, :, 0, NEXP], 1.0)
                    nc.gpsimd.memset(whl[:, :, 1, NEXP], 0.0)
                    nc.gpsimd.memset(sel0[:], 0.0).then_inc(filled, 1)
                    pool.wait_ge(filled, 1)
                    nc.gpsimd.affine_select(out=tri[:], in_=tri[:], compare_op=ALU.is_ge, fill=0.0, base=-1,
                                            pattern=[[1, NEXP], [-1, NEXP]], channel_multiplier=0)
                    nc.gpsimd.affine_select(out=sel0[:], in_=sel0[:], compare_op=ALU.not_equal, fill=1.0, base=0,
                                            pattern=[[-1, NALL], [0, P]], channel_multiplier=1).then_inc(filled, 1)
                    pool.wait_ge(filled, 2)
                    nc.gpsimd.affine_select(out=sel0[:], in_=sel0[:], compare_op=ALU.not_equal, fill=1.0,
                                            base=-NALL, pattern=[[-1, NALL], [0, P]], channel_multiplier=1
                                            ).then_inc(filled, 1)

                @block.scalar
                def _(act):
                    act.wait_ge(loaded, 16 * (7 + SUB))
                    for t, out in zip(raw, (WG, WU)):
                        nc.scalar.copy(out[0][:], t[:]).then_inc(high, 1)

                @block.vector
                def _(dve):
                    for n, (t, out) in enumerate(zip(raw, (WG, WU))):
                        dve.wait_ge(high, n + 1)
                        nc.vector.tensor_tensor(out[1][:], t[:], out[0][:], ALU.subtract)
                    dve.wait_ge(filled, 3)
                    nc.vector.tensor_copy(sel[:], sel0[:]).then_inc(low, 1)

        names = ["mean_done", "xc_done", "sq_done", "var_done", "lnv_done", "rstd_done", "xn_done", "h_done",
                 "hh_done", "hl_done", "lgp_done", "lg_done", "pr_done", "route", "wh_done", "whl_done", "wtp_done", "wt_done",
                 "gu_done", "silu_done", "t_done", "wb_done", "wbs_done", "tw_done",
                 "down_done", "x_done"]
        (mean_done, xc_done, sq_done, var_done, lnv_done, rstd_done, xn_done, h_done, hh_done, hl_done, lgp_done,
         lg_done, pr_done, route, wh_done, whl_done, wtp_done, wt_done, gu_done, silu_done, t_done, wb_done, wbs_done,
         tw_done, down_done, x_done) = [ctx.enter_context(nc.semaphore("m_" + n)) for n in names]
        TW0, DN0, X0 = 4, 4, 2
        ROUTE = 8
        mod = S.mod[0]

        def ahead(par, k, by):
            return ((0, par, k + by) if k + by < UNITS else (1, 1 - par, k + by - UNITS))

        with nc.Block() as block:

            @block.tensor
            def _(pe):
                def mean(n, first=False):
                    if not first:
                        pe.wait_ge(wt_done, n)
                    nc.tensor.matmul(psM[:, 0, :], S.meanw[:], S.X[:, ds(n * MT, MT)],
                                     start=True, stop=True).then_inc(mean_done, 1)

                def var(n):
                    pe.wait_ge(sq_done, n + 1)
                    nc.tensor.matmul(psM[:, 0, :], S.meanw[:], sq[:], start=True, stop=True).then_inc(var_done, 1)

                def logits(n, par):
                    pe.wait_ge(h_done, n + 1)
                    for s in range(SUB):
                        last = nc.tensor.matmul(psM[:, 0, s * NEXP:(s + 1) * NEXP], H[:, par, s * P:(s + 1) * P],
                                                wr[:], start=(s == 0), stop=(s == SUB - 1))
                    last.then_inc(lgp_done, 1)

                def weights_t(n):
                    pe.wait_ge(whl_done, n + 1)
                    for s in range(SUB):
                        last = nc.tensor.transpose(psM[0:2 * NALL, 0, s * P:(s + 1) * P],
                                                   whl[:, s, :, :].rearrange("p a e -> p (a e)"), S.ident[:])
                    last.then_inc(wtp_done, 1)

                def up(n, par, k, first=False):
                    e, half = divmod(k, 2)
                    u = par * UNITS + k
                    if k == 0:
                        pe.wait_ge(hl_done, n + 1)
                        pe.wait_ge(wt_done, n + 1)
                    if not (first and k < 2):
                        pe.wait_ge(silu_done, n * UNITS + (k - 1))
                        pe.wait_ge(t_done, n * UNITS + (k - 1))
                    for W, bank in ((WG, psG), (WU, psU)):
                        nc.tensor.matmul(bank[:, u % 2, :], W[0][:, e, half, :], Hh[:, par, :], start=True, stop=False)
                        nc.tensor.matmul(bank[:, u % 2, :], W[0][:, e, half, :], Hl[:, par, :], start=False, stop=False)
                        last = nc.tensor.matmul(bank[:, u % 2, :], W[1][:, e, half, :], Hh[:, par, :],
                                                start=False, stop=True)
                    last.then_inc(gu_done, 1)
                    if half == 0:
                        if not (first and k == 0):
                            pe.wait_ge(wbs_done, n * NALL + e)
                        nc.tensor.matmul(psW[:, 0, :], sel[:, e, :], wT[:, par, :], start=True, stop=True
                                         ).then_inc(wb_done, 1)

                def down(n, par, k):
                    e, half = divmod(k, 2)
                    u = par * UNITS + k
                    pe.wait_ge(tw_done, n * UNITS + (k + 1 + TW0))
                    if k == 0:
                        pe.wait_ge(x_done, n + (X0 - 1))
                    nc.tensor.matmul(psY[:, par, :], WD[:, e, half, :], tw[:, u % 4, :], start=(k == 0),
                                     stop=(k == UNITS - 1)).then_inc(down_done, 1)

                mean(0, first=True)
                var(0)
                logits(0, 0)
                weights_t(0)
                for k in range(LEAD):
                    up(0, 0, k, first=True)
                with nc.tensor.Fori(0, NT // 2) as j:
                    for par in range(2):
                        n = j * 2 + par
                        for k in range(UNITS):
                            on, upar, uk = ahead(par, k, LEAD)
                            up(n + on, upar, uk)
                            down(n, par, k)
                            if k == 1:
                                mean(n + 1)
                            if k == 3:
                                var(n + 1)
                            if k == 6:
                                logits(n + 1, 1 - par)
                            if k == 12:
                                weights_t(n + 1)

            @block.scalar
            def _(act):
                def square(n):
                    act.wait_ge(xc_done, n + 1)
                    nc.scalar.activation(sq[:], xc[:], ACT.Square).then_inc(sq_done, 1)

                def inv_std(n):
                    act.wait_ge(var_done, n + 1)
                    nc.scalar.activation(lnv[:], psM[:, 0, :], ACT.Ln, bias=S.eps[:, 0:1]).then_inc(lnv_done, 1)
                    act.wait_ge(lnv_done, n + 1)
                    nc.scalar.activation(rstd[:], lnv[:], ACT.Exp, scale=-0.5).then_inc(rstd_done, 1)

                def high_h(n, par):
                    act.wait_ge(h_done, n + 1)
                    nc.scalar.copy(Hh[:, par, :], H[:, par, :]).then_inc(hh_done, 1)

                def probabilities(n):
                    act.wait_ge(lg_done, n + 1)
                    nc.scalar.activation(pr[:], lg[:], ACT.Sigmoid).then_inc(pr_done, 1)

                def weights_copy(n, par):
                    act.wait_ge(wtp_done, n + 1)
                    nc.scalar.copy(wT[:, par, :], psM[0:2 * NALL, 0, :]).then_inc(wt_done, 1)

                def silu(n, par, k):
                    u = par * UNITS + k
                    act.wait_ge(gu_done, n * UNITS + (k + 1))
                    nc.scalar.activation(sg[:, u % 2, :], psG[:, u % 2, :], ACT.Silu).then_inc(silu_done, 1)
                    if k % 2 == 0:
                        e = k // 2
                        act.wait_ge(wb_done, n * NALL + (e + 1))
                        act.wait_ge(tw_done, n * UNITS + (2 * e - 2 + TW0))
                        nc.scalar.copy(wbs[:, (par * NALL + e) % 2, :], psW[:, 0, :]).then_inc(wbs_done, 1)

                square(0)
                inv_std(0)
                high_h(0, 0)
                probabilities(0)
                weights_copy(0, 0)
                for k in range(LEAD):
                    silu(0, 0, k)
                with nc.scalar.Fori(0, NT // 2) as j:
                    for par in range(2):
                        n = j * 2 + par
                        for k in range(UNITS):
                            on, upar, uk = ahead(par, k, LEAD)
                            silu(n + on, upar, uk)
                            if k == 2:
                                square(n + 1)
                            if k == 4:
                                inv_std(n + 1)
                            if k == 6:
                                high_h(n + 1, 1 - par)
                            if k == 8:
                                probabilities(n + 1)
                            if k == 13:
                                weights_copy(n + 1, 1 - par)

            @block.gpsimd
            def _(pool):
                def weigh(n, par, k):
                    u = par * UNITS + k
                    e = k // 2
                    pool.wait_ge(t_done, n * UNITS + (k + 1))
                    pool.wait_ge(wbs_done, n * NALL + (e + 1))
                    pool.wait_ge(down_done, n * UNITS + (k - 3 + DN0))
                    nc.gpsimd.tensor_tensor(tw[:, u % 4, :], tt[:, u % 2, :], wbs[:, (par * NALL + e) % 2, :],
                                            ALU.mult).then_inc(tw_done, 1)

                nc.gpsimd.memset(S.spare[:, 3:4], 0.0).then_inc(tw_done, TW0)
                for k in range(2):
                    weigh(0, 0, k)
                with nc.gpsimd.Fori(0, NT // 2) as j:
                    for par in range(2):
                        n = j * 2 + par
                        for k in range(UNITS):
                            on, upar, uk = ahead(par, k, 2)
                            weigh(n + on, upar, uk)

            @block.vector
            def _(dve):
                def center(n):
                    dve.wait_ge(mean_done, n + 1)
                    nc.vector.tensor_tensor(xc[:], S.X[:, ds(n * MT, MT)], psM[:, 0, :], ALU.subtract
                                            ).then_inc(xc_done, 1)

                def normalize(n, par):
                    dve.wait_ge(rstd_done, n + 1)
                    nc.vector.tensor_tensor(xc[:], xc[:], rstd[:], ALU.mult).then_inc(xn_done, 1)
                    dve.wait_ge(xn_done, n + 1)
                    for s in range(SPT):
                        cols = slice(s * SEQ, (s + 1) * SEQ)
                        last = nc.vector.tensor_scalar(H[:, par, cols], xc[:, cols], mod[:, SC_B, ds(n * SPT + s, 1)],
                                                       mod[:, SH_B, ds(n * SPT + s, 1)], ALU.mult, ALU.add)
                    last.then_inc(h_done, 1)

                def low_h(n, par):
                    dve.wait_ge(hh_done, n + 1)
                    nc.vector.tensor_tensor(Hl[:, par, :], H[:, par, :], Hh[:, par, :], ALU.subtract
                                            ).then_inc(hl_done, 1)

                def add_bias(n):
                    dve.wait_ge(lgp_done, n + 1)
                    nc.vector.tensor_tensor(lg[:], psM[:, 0, 0:SUB * NEXP].rearrange("p (s e) -> p s e", s=SUB),
                                            bias[:], ALU.add).then_inc(lg_done, 1)

                def choose(n):
                    dve.wait_ge(pr_done, n + 1)
                    step = [0]

                    def after(ins):
                        step[0] += 1
                        ins.then_inc(route, 1)
                        dve.wait_ge(route, n * ROUTE + step[0])

                    big = [P, SUB, NEXP, NEXP]
                    other = pr[:].unsqueeze(2).broadcast_to(big)
                    own = pr[:].unsqueeze(3).broadcast_to(big)
                    nc.vector.tensor_tensor(beats[:], other, own, ALU.is_gt)
                    after(nc.vector.tensor_tensor(ties[:], other, own, ALU.is_equal))
                    after(nc.vector.tensor_tensor(ties[:], ties[:], tri[:].unsqueeze(1).broadcast_to(big), ALU.mult))
                    after(nc.vector.tensor_tensor(beats[:], beats[:], ties[:], ALU.add))
                    after(nc.vector.tensor_reduce(rank[:], beats[:], AX, ALU.add))
                    after(nc.vector.scalar_tensor_tensor(pick[:], rank[:], 1.5, pr[:], ALU.is_lt, ALU.mult))
                    after(nc.vector.tensor_reduce(psum2[:], pick[:], AX, ALU.add))
                    after(nc.vector.reciprocal(psum2[:], psum2[:]))
                    after(nc.vector.tensor_tensor(wt[:], pick[:], psum2[:].unsqueeze(2).broadcast_to([P, SUB, NEXP]),
                                                  ALU.mult))
                    assert step[0] == ROUTE
                    split(n)

                def split(n):
                    nc.vector.tensor_copy(whl[:, :, 0, 0:NEXP].bitcast(F32R), wt[:]).then_inc(wh_done, 1)
                    dve.wait_ge(wh_done, n + 1)
                    nc.vector.tensor_tensor(whl[:, :, 1, 0:NEXP], wt[:], whl[:, :, 0, 0:NEXP], ALU.subtract
                                            ).then_inc(whl_done, 1)

                def gate_up(n, par, k):
                    u = par * UNITS + k
                    dve.wait_ge(silu_done, n * UNITS + (k + 1))
                    dve.wait_ge(tw_done, n * UNITS + (k - 1 + TW0))
                    nc.vector.tensor_tensor(tt[:, u % 2, :], sg[:, u % 2, :], psU[:, u % 2, :], ALU.mult
                                            ).then_inc(t_done, 1)

                def residual(n, par):
                    dve.wait_ge(down_done, n * UNITS + (UNITS + DN0))
                    for s in range(SPT):
                        x = S.X[:, ds((n * SPT + s) * SEQ, SEQ)]
                        last = nc.vector.scalar_tensor_tensor(x, psY[:, par, s * SEQ:(s + 1) * SEQ],
                                                              mod[:, GB, ds(n * SPT + s, 1)], x, ALU.mult, ALU.add)
                    last.then_inc(x_done, 1)

                nc.vector.memset(S.spare[:, 1:2], 0.0).then_inc(down_done, DN0)
                nc.vector.memset(S.spare[:, 2:3], 0.0).then_inc(x_done, X0)
                center(0)
                normalize(0, 0)
                low_h(0, 0)
                add_bias(0)
                choose(0)
                for k in range(2):
                    gate_up(0, 0, k)
                with nc.vector.Fori(0, NT // 2) as j:
                    for par in range(2):
                        n = j * 2 + par
                        for k in range(UNITS):
                            on, upar, uk = ahead(par, k, 2)
                            gate_up(n + on, upar, uk)
                            if k == 2:
                                center(n + 1)
                            if k == 5:
                                normalize(n + 1, 1 - par)
                            if k == 7:
                                low_h(n + 1, 1 - par)
                                add_bias(n + 1)
                            if k == 10:
                                choose(n + 1)
                        residual(n, par)


ROW = SEQ + 1
SMALL_E = 0.03
SMALL = 1e-5


def mamba(nc, w, S):
    with ExitStack() as ctx:
        def sb(name, shape, dt=F32):
            return ctx.enter_context(nc.sbuf_tensor(name, shape, dt))

        def pb(name, n):
            return ctx.enter_context(nc.psum_tensor(name, [P, n, 512], F32))

        wz = sb("wz", [P, P])
        wdd = sb("wdd", [P, RDT])
        wc = sb("wc", [P, 4, NST])
        wdt = sb("wdt", [RDT, P])
        wout = sb("wout_s", [P, P])
        conv = sb("conv", [P, TAPS])
        bdt = sb("bdt", [P, 1])
        dskip = sb("dskip", [P, 1])
        negA = sb("negA", [P, NST])
        is_small = sb("is_small", [P, NST])
        is_large = sb("is_large", [P, NST])
        cst = sb("cst", [P, NST])
        diag = sb("diag", [P, NST, P])
        csT = [sb(f"csT{i}", [4 * NST, P], F32R) for i in range(2)]
        sel = sb("sel_s", [4 * NST, NST, P], F32R)
        any_small = sb("any_small", [P, 1], mybir.dt.int32)

        xc = sb("xc_s", [P, MT])
        sq = sb("sq_s", [P, MT])
        lnv = sb("lnv_s", [P, MT])
        rstd = sb("rstd_s", [P, MT])
        H = sb("H_s", [P, SPT, TAPS - 1 + SEQ])
        acc = sb("acc_s", [P, 2, SPT, SEQ])
        U = sb("U_s", [P, 2, SPT, SEQ])
        sz = sb("sz_s", [P, 2, MT])
        dtx = sb("dtx", [P, 2, SPT, ROW + 1])
        dd = sb("dd", [P, 3, SPT * ROW])
        wx = sb("wx", [P, SPT, ROW])
        part = sb("part_s", [P, SPT * ROW])
        Ch = sb("Ch", [4 * NST, 2, MT], F32R)
        dtu = sb("dtu", [RDT, MT])
        A = sb("A_s", [P, 2, SPT, ROW])
        K = sb("K_s", [P, 4, SPT, ROW])
        M = sb("M_s", [P, 3, MT])
        ex = sb("ex", [P, MT])
        rx = sb("rx", [P, MT])
        big = sb("big", [P, MT])
        tiny = sb("tiny", [P, MT])
        one = sb("one", [P, 1])
        coef = sb("coef", [P, 4])
        g1 = sb("g1", [P, MT])
        yo = sb("yo", [P, MT])

        psM, psZ, psC, psY, psG, psO = (pb("psM_s", 1), pb("psZ_s", 1), pb("psC_s", 2), pb("psY_s", 1),
                                        pb("psG_s", 1), pb("psO_s", 1))

        with ExitStack() as pre:
            sem = lambda n: pre.enter_context(nc.semaphore(n))
            loaded, expd, vstep, made, filled = map(sem, ["s_loaded", "s_expd", "s_vstep", "s_made", "s_filled"])
            alog = pre.enter_context(nc.sbuf_tensor("alog", [P, NST], F32))
            ea = pre.enter_context(nc.sbuf_tensor("ea", [P, NST], F32))
            den = pre.enter_context(nc.sbuf_tensor("den_s", [P, NST], F32))
            cs4 = pre.enter_context(nc.sbuf_tensor("cs4", [P, 4, NST], F32))
            sel0 = pre.enter_context(nc.sbuf_tensor("sel0_s", [4 * NST, NST, P], F32))
            onesq = pre.enter_context(nc.sbuf_tensor("onesq", [P, P], F32))
            some = pre.enter_context(nc.sbuf_tensor("some", [P, 1], F32))
            with nc.Block() as block:

                @block.sync
                def _(sp):
                    sp.wait_ge(filled, 1)
                    for t, src in ((wz[:], w["wz"]), (wdd[:], w["wpar"][:, 0:RDT]),
                                   (wc[:, 0, :], w["wpar"][:, RDT + NST:RDT + 2 * NST]),
                                   (wc[:, 2, :], w["wpar"][:, RDT + NST:RDT + 2 * NST]),
                                   (wdt[:], w["wdt"]), (wout[:], w["wout"]), (conv[:], w["conv"]),
                                   (bdt[:], w["bdt"]), (dskip[:], w["dskip"]), (alog[:], w["alog"])):
                        sp.dma_start(t, src).then_inc(loaded, 16)
                    sp.wait_ge(loaded, 160)

                @block.gpsimd
                def _(pool):
                    nc.gpsimd.memset(wc[:], 0.0).then_inc(filled, 1)
                    nc.gpsimd.memset(onesq[:], 1.0)
                    nc.gpsimd.memset(one[:], 1.0)
                    for i, c in enumerate((-1 / 4, 1 / 3, -1 / 2, 1.0)):
                        nc.gpsimd.memset(coef[:, i:i + 1], c)
                    nc.gpsimd.memset(cs4[:], 0.0)
                    nc.gpsimd.memset(H[:, :, 0:TAPS - 1], 0.0)
                    nc.gpsimd.memset(wx[:, :, 0:1], 0.0)
                    for par in range(2):
                        nc.gpsimd.memset(A[:, par, :, 0:1], 0.0)
                        nc.gpsimd.memset(dd[:, par, :].rearrange("p (s t) -> p s t", s=SPT)[:, :, 1:2], 0.0)
                    nc.gpsimd.memset(sel0[:], 0.0).then_inc(filled, 1)
                    pool.wait_ge(filled, 2)
                    nc.gpsimd.affine_select(out=sel0[:], in_=sel0[:], compare_op=ALU.not_equal, fill=1.0, base=0,
                                            pattern=[[-1, NST], [0, P]], channel_multiplier=1).then_inc(filled, 1)
                    pool.wait_ge(filled, 3)
                    nc.gpsimd.affine_select(out=sel0[:], in_=sel0[:], compare_op=ALU.not_equal, fill=1.0,
                                            base=-2 * NST, pattern=[[-1, NST], [0, P]], channel_multiplier=1
                                            ).then_inc(filled, 1)

                @block.scalar
                def _(act):
                    act.wait_ge(loaded, 160)
                    nc.scalar.activation(ea[:], alog[:], ACT.Exp).then_inc(expd, 1)

                @block.vector
                def _(dve):
                    n = [0]

                    def after(ins):
                        n[0] += 1
                        ins.then_inc(vstep, 1)
                        dve.wait_ge(vstep, n[0])

                    dve.wait_ge(expd, 1)
                    dve.wait_ge(filled, 4)
                    nc.vector.tensor_scalar(negA[:], ea[:], -1.0, None, ALU.mult)
                    nc.vector.tensor_scalar(is_small[:], ea[:], SMALL, None, ALU.is_lt)
                    after(nc.vector.tensor_scalar(is_large[:], ea[:], SMALL, None, ALU.is_ge))
                    after(nc.vector.scalar_tensor_tensor(den[:], negA[:], 1e-10, is_large[:], ALU.add, ALU.mult))
                    after(nc.vector.tensor_tensor(den[:], den[:], is_small[:], ALU.add))
                    after(nc.vector.reciprocal(cst[:], den[:]))
                    for r in (0, 2):
                        nc.vector.tensor_tensor(cs4[:, r, :], cst[:], is_large[:], ALU.mult)
                    for k in range(NST):
                        last = nc.vector.tensor_scalar(diag[:, k, :], S.ident[:], cst[:, k:k + 1], None, ALU.mult)
                    after(last)
                    nc.vector.tensor_copy(sel[:], sel0[:])
                    dve.wait_ge(made, 1)
                    after(nc.vector.tensor_copy(csT[0][:], psM[0:4 * NST, 0, 0:P]))
                    nc.vector.tensor_tensor(csT[1][:], psM[0:4 * NST, 0, 0:P], csT[0][:], ALU.subtract)
                    after(nc.vector.tensor_reduce(some[:], psZ[:, 0, 0:NST], AX, ALU.max))
                    after(nc.vector.tensor_scalar(any_small[:], some[:], 0.5, None, ALU.is_gt))

                @block.tensor
                def _(pe):
                    pe.wait_ge(vstep, 5)
                    nc.tensor.transpose(psM[0:4 * NST, 0, 0:P], cs4[:].rearrange("p r n -> p (r n)"), S.ident[:])
                    nc.tensor.matmul(psZ[:, 0, 0:NST], onesq[:], is_small[:], start=True, stop=True).then_inc(made, 1)

        names = ["mean_done", "xc_done", "sq_done", "var_done", "lnv_done", "rstd_done", "xn_done", "h_done",
                 "z_done", "c_done", "chi_done", "clo_done", "dtu_done", "dtuc_done", "dt_done", "ax_done", "conv_step",
                 "conv_done", "sz_done", "u_done", "e_done", "big_done", "x_read", "series", "blend_done", "dtx_done", "dd_done", "w_done",
                 "a_done", "cb_done", "k_done", "m_done", "acc_done", "g_done", "fin_step", "yo_done",
                 "o_done", "x_done", "small_step"]
        (mean_done, xc_done, sq_done, var_done, lnv_done, rstd_done, xn_done, h_done,
         z_done, c_done, chi_done, clo_done, dtu_done, dtuc_done, dt_done, ax_done, conv_step,
         conv_done, sz_done, u_done, e_done, big_done, x_read, series, blend_done, dtx_done, dd_done, w_done,
         a_done, cb_done, k_done, m_done, acc_done, g_done, fin_step, yo_done,
         o_done, x_done, small_step) = [ctx.enter_context(nc.semaphore("s_" + n)) for n in names]
        K0, M0, AC0, X0, F0 = 2, 4, 3, 1, 3
        SERIES = 9
        mod = S.mod[1]

        with nc.Block() as block:

            @block.tensor
            def _(pe):
                def mean(n, first=False):
                    if not first:
                        pe.wait_ge(x_read, n)
                    nc.tensor.matmul(psM[:, 0, :], S.meanw[:], S.X[:, ds(n * MT, MT)],
                                     start=True, stop=True).then_inc(mean_done, 1)

                def var(n):
                    pe.wait_ge(sq_done, n + 1)
                    nc.tensor.matmul(psM[:, 0, :], S.meanw[:], sq[:], start=True, stop=True).then_inc(var_done, 1)

                h = H[:, :, TAPS - 1:]

                def z_and_c(n, first=False):
                    pe.wait_ge(h_done, n + 1)
                    nc.tensor.matmul(psM[0:4 * NST, 0, :], wc[:].rearrange("p r n -> p (r n)"), h,
                                     start=True, stop=True).then_inc(c_done, 1)
                    if not first:
                        pe.wait_ge(sz_done, n)
                    nc.tensor.matmul(psZ[:, 0, :], wz[:], h, start=True, stop=True).then_inc(z_done, 1)

                def dt_down(n):
                    pe.wait_ge(clo_done, n + 1)
                    nc.tensor.matmul(psM[0:RDT, 0, :], wdd[:], h, start=True, stop=True).then_inc(dtu_done, 1)

                def dt_up(n):
                    pe.wait_ge(dtuc_done, n + 1)
                    nc.tensor.matmul(psM[:, 0, :], wdt[:], dtu[:], start=True, stop=True).then_inc(dt_done, 1)

                def spread_c(n, par, k):
                    pe.wait_ge(m_done, n * NST + (k - 1 + M0))
                    nc.tensor.matmul(psC[:, k % 2, :], sel[:, k, :], Ch[:, par, :], start=True, stop=True
                                     ).then_inc(cb_done, 1)

                def sum_c(n, par):
                    pe.wait_ge(fin_step, n * 3 + (1 - 3 + F0))
                    nc.tensor.matmul(psG[:, 0, :], csT[0][:], Ch[:, par, :], start=True, stop=False)
                    nc.tensor.matmul(psG[:, 0, :], csT[1][:], Ch[:, par, :], start=False, stop=True
                                     ).then_inc(g_done, 1)

                def accumulate(n, k):
                    pe.wait_ge(m_done, n * NST + (k + 1 + M0))
                    if k == 0:
                        pe.wait_ge(fin_step, n * 3 + F0)
                    nc.tensor.matmul(psY[:, 0, :], diag[:, k, :], M[:, k % 3, :], start=(k == 0), stop=(k == NST - 1)
                                     ).then_inc(acc_done, 1)

                def project(n):
                    pe.wait_ge(yo_done, n + 1)
                    pe.wait_ge(x_done, n + X0)
                    nc.tensor.matmul(psO[:, 0, :], wout[:], yo[:], start=True, stop=True).then_inc(o_done, 1)

                mean(0, first=True)
                var(0)
                z_and_c(0, first=True)
                dt_down(0)
                dt_up(0)
                with nc.tensor.Fori(0, NT // 2) as j:
                    for par in range(2):
                        n = j * 2 + par
                        pe.wait_ge(clo_done, n + 1)
                        sum_c(n, par)
                        spread_c(n, par, 0)
                        for k in range(NST):
                            if k + 1 < NST:
                                spread_c(n, par, k + 1)
                            if k >= 1:
                                accumulate(n, k - 1)
                            if k == 0:
                                mean(n + 1)
                            if k == 2:
                                var(n + 1)
                            if k == 5:
                                z_and_c(n + 1)
                            if k == 7:
                                dt_down(n + 1)
                            if k == 8:
                                dt_up(n + 1)
                        accumulate(n, NST - 1)
                        project(n)

            @block.scalar
            def _(act):
                def square(n):
                    act.wait_ge(xc_done, n + 1)
                    nc.scalar.activation(sq[:], xc[:], ACT.Square).then_inc(sq_done, 1)

                def inv_std(n):
                    act.wait_ge(var_done, n + 1)
                    nc.scalar.activation(lnv[:], psM[:, 0, :], ACT.Ln, bias=S.eps[:, 0:1]).then_inc(lnv_done, 1)
                    act.wait_ge(lnv_done, n + 1)
                    nc.scalar.activation(rstd[:], lnv[:], ACT.Exp, scale=-0.5).then_inc(rstd_done, 1)

                def c_high(n, par):
                    act.wait_ge(c_done, n + 1)
                    nc.scalar.copy(Ch[:, par, :], psM[0:4 * NST, 0, :]).then_inc(chi_done, 1)

                def dt_copy(n):
                    act.wait_ge(dtu_done, n + 1)
                    nc.scalar.copy(dtu[:], psM[0:RDT, 0, :]).then_inc(dtuc_done, 1)

                def softplus(n):
                    act.wait_ge(dt_done, n + 1)
                    nc.scalar.activation(ex[:], psM[:, 0, :], ACT.Abs, bias=bdt[:, 0:1]).then_inc(ax_done, 1)
                    nc.scalar.activation(rx[:], psM[:, 0, :], ACT.Relu, bias=bdt[:, 0:1]).then_inc(x_read, 1)
                    act.wait_ge(ax_done, n + 1)
                    nc.scalar.activation(ex[:], ex[:], ACT.Exp, scale=-1.0).then_inc(e_done, 1)
                    act.wait_ge(e_done, n + 1)
                    nc.scalar.activation(big[:], ex[:], ACT.Ln, bias=one[:, 0:1]).then_inc(big_done, 1)

                def activations(n, par):
                    act.wait_ge(z_done, n + 1)
                    nc.scalar.activation(sz[:, par, :], psZ[:, 0, :], ACT.Silu).then_inc(sz_done, 1)
                    act.wait_ge(conv_done, n + 1)
                    nc.scalar.activation(U[:, par, :, :], acc[:, 1, :, :], ACT.Silu).then_inc(u_done, 1)
                    nc.scalar.preload_act_table_set("natural_log_exp_and_others")

                def decay(n, par, k):
                    if k == 0:
                        act.wait_ge(dtx_done, n + 1)
                    act.wait_ge(k_done, n * NST + (k - 1 + K0))
                    if k >= 0:
                        nc.scalar.activation(A[:, k % 2, :, 1:ROW], dtx[:, par, :, 1:ROW], ACT.Exp,
                                             scale=negA[:, k:k + 1]).then_inc(a_done, 1)

                nc.scalar.preload_act_table_set("natural_log_exp_and_others")
                square(0)
                inv_std(0)
                c_high(0, 0)
                dt_copy(0)
                softplus(0)
                activations(0, 0)
                with nc.scalar.Fori(0, NT // 2) as j:
                    for par in range(2):
                        n = j * 2 + par
                        for k in range(NST):
                            decay(n, par, k)
                            if k == 2:
                                square(n + 1)
                            if k == 4:
                                inv_std(n + 1)
                            if k == 6:
                                c_high(n + 1, 1 - par)
                            if k == 8:
                                dt_copy(n + 1)
                            if k == 9:
                                softplus(n + 1)
                            if k == 13:
                                activations(n + 1, 1 - par)

            @block.gpsimd
            def _(pool):
                def inputs(n, par):
                    pool.wait_ge(u_done, n + 1)
                    d = dd[:, par, :].rearrange("p (s t) -> p s t", s=SPT)
                    nc.gpsimd.tensor_tensor(d[:, :, 2:ROW], U[:, par, :, 1:SEQ], U[:, par, :, 0:SEQ - 1],
                                            ALU.subtract)
                    nc.gpsimd.tensor_copy(d[:, :, 0:1], U[:, par, :, 0:1]).then_inc(dd_done, 1)

                def small_log(n):
                    pool.wait_ge(e_done, n + 1)
                    coefs = [coef[:, i:i + 1].broadcast_to([P, MT]) for i in range(4)]
                    nc.gpsimd.tensor_tensor(tiny[:], ex[:], coefs[0], ALU.mult).then_inc(series, 1)
                    for i in range(3):
                        pool.wait_ge(series, n * SERIES + (2 * i + 1))
                        nc.gpsimd.tensor_tensor(tiny[:], tiny[:], coefs[i + 1], ALU.add).then_inc(series, 1)
                        pool.wait_ge(series, n * SERIES + (2 * i + 2))
                        nc.gpsimd.tensor_tensor(tiny[:], tiny[:], ex[:], ALU.mult).then_inc(series, 1)
                    pool.wait_ge(series, n * SERIES + 7)
                    pool.wait_ge(big_done, n + 1)
                    nc.gpsimd.tensor_tensor(big[:], big[:], tiny[:], ALU.subtract).then_inc(series, 1)
                    pool.wait_ge(x_read, n + 1)
                    nc.gpsimd.tensor_tensor(rx[:], rx[:], tiny[:], ALU.add).then_inc(series, 1)

                def dt_out(n, par):
                    pool.wait_ge(blend_done, n + 1)
                    s3 = lambda a: a[:].rearrange("p (s t) -> p s t", s=SPT)
                    nc.gpsimd.tensor_tensor(dtx[:, par, :, 2:2 + SEQ], s3(rx), s3(big), ALU.add)
                    nc.gpsimd.tensor_tensor(dtx[:, par, :, 1:2], s3(rx)[:, :, 0:1], s3(big)[:, :, 0:1], ALU.add
                                            ).then_inc(dtx_done, 1)

                small_log(0)
                dt_out(0, 0)
                inputs(0, 0)
                with nc.gpsimd.Fori(0, NT // 2) as j:
                    for par in range(2):
                        n = j * 2 + par
                        small_log(n + 1)
                        dt_out(n + 1, 1 - par)
                        inputs(n + 1, 1 - par)

            @block.vector
            def _(dve):
                small = nc.vector.value_load(any_small[0:1, 0:1], min_val=0, max_val=1)

                def center(n):
                    dve.wait_ge(mean_done, n + 1)
                    nc.vector.tensor_tensor(xc[:], S.X[:, ds(n * MT, MT)], psM[:, 0, :], ALU.subtract
                                            ).then_inc(xc_done, 1)

                def normalize(n):
                    dve.wait_ge(rstd_done, n + 1)
                    nc.vector.tensor_tensor(xc[:], xc[:], rstd[:], ALU.mult).then_inc(xn_done, 1)
                    dve.wait_ge(xn_done, n + 1)
                    for s in range(SPT):
                        last = nc.vector.tensor_scalar(H[:, s, TAPS - 1:], xc[:, s * SEQ:(s + 1) * SEQ],
                                                       mod[:, SC_A, ds(n * SPT + s, 1)],
                                                       mod[:, SH_A, ds(n * SPT + s, 1)], ALU.mult, ALU.add)
                    last.then_inc(h_done, 1)

                def c_low(n, par):
                    dve.wait_ge(chi_done, n + 1)
                    rows = slice(2 * NST, 4 * NST)
                    nc.vector.tensor_tensor(Ch[rows, par, :], psM[rows, 0, :], Ch[rows, par, :], ALU.subtract
                                            ).then_inc(clo_done, 1)

                def blend(n):
                    dve.wait_ge(series, n * SERIES + SERIES)
                    nc.vector.scalar_tensor_tensor(big[:], ex[:], SMALL_E, big[:], ALU.is_gt, ALU.mult
                                                   ).then_inc(blend_done, 1)

                def convolve(n, i):
                    if i == 0:
                        dve.wait_ge(h_done, n + 1)
                        nc.vector.tensor_scalar(acc[:, 0, :, :], H[:, :, TAPS - 1:], conv[:, TAPS - 1:TAPS], None,
                                                ALU.mult).then_inc(conv_step, 1)
                    else:
                        dve.wait_ge(conv_step, n * (TAPS - 1) + i)
                        t = TAPS - 1 - i
                        nc.vector.scalar_tensor_tensor(acc[:, i % 2, :, :], H[:, :, t:t + SEQ], conv[:, t:t + 1],
                                                       acc[:, 1 - i % 2, :, :], ALU.mult, ALU.add
                                                       ).then_inc(conv_done if i == TAPS - 1 else conv_step, 1)

                def scan(n, par, k):
                    with nc.vector.If(small):
                        if k == 0:
                            dve.wait_ge(dd_done, n + 1)
                            dve.wait_ge(dtx_done, n + 1)
                            nc.vector.tensor_tensor(wx[:, :, 2:ROW], dtx[:, par, :, 2:ROW], U[:, par, :, 0:SEQ - 1],
                                                    ALU.mult)
                            nc.vector.tensor_tensor(wx[:, :, 1:2], dtx[:, par, :, 1:2], U[:, par, :, 0:1], ALU.mult
                                                    ).then_inc(w_done, 1)
                            dve.wait_ge(w_done, n + 1)
                        dve.wait_ge(k_done, n * NST + (k + K0))
                        nc.vector.tensor_scalar(part[:], dd[:, par, :], is_large[:, k:k + 1], None, ALU.mult
                                                ).then_inc(small_step, 1)
                        dve.wait_ge(small_step, n * 2 * NST + (2 * k + 1))
                        nc.vector.scalar_tensor_tensor(dd[:, 2, :], wx[:].rearrange("p s t -> p (s t)"),
                                                       is_small[:, k:k + 1], part[:], ALU.mult, ALU.add
                                                       ).then_inc(small_step, 1)
                        dve.wait_ge(small_step, n * 2 * NST + (2 * k + 2))
                        nc.vector.memset(S.spare[:, 6:7], 0.0)
                    dve.wait_ge(a_done, n * NST + (k + 1))
                    if k == 0:
                        dve.wait_ge(dd_done, n + 1)
                    dve.wait_ge(m_done, n * NST + (k - 3 + M0))
                    at = small * ((2 - par) * SPT * ROW) + par * SPT * ROW
                    nc.vector.tensor_tensor_scan(K[:, k % 4, :, :].rearrange("p s t -> p (s t)"),
                                                 A[:, k % 2, :, :].rearrange("p s t -> p (s t)"),
                                                 dd[:].rearrange("p i t -> p (i t)")[:, ds(at, SPT * ROW)],
                                                 0.0, ALU.mult, ALU.add).then_inc(k_done, 1)

                def times_c(n, k):
                    dve.wait_ge(cb_done, n * NST + (k + 1))
                    dve.wait_ge(k_done, n * NST + (k + 1 + K0))
                    dve.wait_ge(acc_done, n * NST + (k - 2 + AC0))
                    nc.vector.tensor_tensor(M[:, k % 3, :].rearrange("p (s t) -> p s t", s=SPT), K[:, k % 4, :, 1:ROW],
                                            psC[:, k % 2, :].rearrange("p (s t) -> p s t", s=SPT), ALU.mult
                                            ).then_inc(m_done, 1)

                def gate_off(n, par):
                    dve.wait_ge(g_done, n + 1)
                    nc.vector.tensor_scalar(g1[:], psG[:, 0, :], -1.0, dskip[:, 0:1], ALU.mult, ALU.add
                                            ).then_inc(fin_step, 1)
                    dve.wait_ge(fin_step, n * 3 + 1 + F0)
                    nc.vector.tensor_tensor(g1[:], g1[:], U[:, par, :, :].rearrange("p s t -> p (s t)"), ALU.mult
                                            ).then_inc(fin_step, 1)

                def finish(n, par):
                    dve.wait_ge(acc_done, n * NST + (NST + AC0))
                    dve.wait_ge(fin_step, n * 3 + 2 + F0)
                    nc.vector.tensor_tensor(g1[:], psY[:, 0, :], g1[:], ALU.add).then_inc(fin_step, 1)
                    dve.wait_ge(fin_step, n * 3 + 3 + F0)
                    nc.vector.tensor_tensor(yo[:], g1[:], sz[:, par, :], ALU.mult).then_inc(yo_done, 1)

                def residual(n):
                    dve.wait_ge(o_done, n + 1)
                    for s in range(SPT):
                        x = S.X[:, ds((n * SPT + s) * SEQ, SEQ)]
                        last = nc.vector.scalar_tensor_tensor(x, psO[:, 0, s * SEQ:(s + 1) * SEQ],
                                                              mod[:, GA, ds(n * SPT + s, 1)], x, ALU.mult, ALU.add)
                    last.then_inc(x_done, 1)

                for i, (sem, count) in enumerate(((k_done, K0), (m_done, M0), (acc_done, AC0), (x_done, X0),
                                                  (fin_step, F0))):
                    nc.vector.memset(S.spare[:, i:i + 1], 0.0).then_inc(sem, count)
                center(0)
                normalize(0)
                c_low(0, 0)
                for i in range(TAPS):
                    convolve(0, i)
                blend(0)
                with nc.vector.Fori(0, NT // 2) as j:
                    for par in range(2):
                        n = j * 2 + par
                        scan(n, par, 0)
                        for k in range(NST):
                            if k + 1 < NST:
                                scan(n, par, k + 1)
                            times_c(n, k)
                            if k == 1:
                                center(n + 1)
                            if k == 2:
                                gate_off(n, par)
                            if k == 5:
                                normalize(n + 1)
                            if k == 7:
                                c_low(n + 1, 1 - par)
                            if 8 <= k < 8 + TAPS:
                                convolve(n + 1, k - 8)
                            if k == NST - 1:
                                blend(n + 1)
                        finish(n, par)
                        residual(n)


def rwkv(nc, w, S):
    with ExitStack() as ctx:
        def sb(name, shape, dt=F32):
            return ctx.enter_context(nc.sbuf_tensor(name, shape, dt))

        def pb(name):
            return ctx.enter_context(nc.psum_tensor(name, [P, 512], F32))

        wr, wk, wv = sb("wr_r", [P, P]), sb("wk_r", [P, P]), sb("wv_r", [P, P])
        mu = sb("mu", [P, 2])
        nmu = sb("nmu", [P, 2])
        xc = sb("xc_r", [P, MT])
        sq = sb("sq_r", [P, MT])
        lnv = sb("lnv_r", [P, MT])
        rstd = sb("rstd_r", [P, MT])
        H = sb("H_r", [P, SPT, 1 + SEQ])
        old = sb("old_r", [P, 2, SPT, SEQ])
        mix = sb("mix_r", [P, 2, SPT, SEQ])
        rs = sb("rs_r", [P, MT])
        kr = sb("kr_r", [P, MT])
        ks = sb("ks_r", [P, MT])
        ov = sb("ov_r", [P, MT])
        psM, psR, psK, psV = pb("psM_r"), pb("psR_r"), pb("psK_r"), pb("psV_r")

        with ExitStack() as pre:
            loaded = pre.enter_context(nc.semaphore("r_loaded"))
            with nc.Block() as block:

                @block.sync
                def _(sp):
                    for t, src in ((wr[:], "wr"), (wk[:], "wk"), (wv[:], "wv"), (mu[:, 0:1], "mur"), (mu[:, 1:2], "muk")):
                        sp.dma_start(t, w[src]).then_inc(loaded, 16)
                    sp.wait_ge(loaded, 80)

                @block.vector
                def _(dve):
                    nc.vector.memset(H[:, :, 0:1], 0.0)
                    dve.wait_ge(loaded, 80)
                    nc.vector.tensor_scalar(nmu[:], mu[:], -1.0, 1.0, ALU.mult, ALU.add)

        names = ["mean_done", "xc_done", "sq_done", "var_done", "lnv_done", "rstd_done", "xn_done", "h_done",
                 "old_done", "mix_done", "r_done", "k_done", "rs_done", "kr_done", "ks_done", "v_done", "ov_done",
                 "x_done"]
        (mean_done, xc_done, sq_done, var_done, lnv_done, rstd_done, xn_done, h_done, old_done, mix_done, r_done,
         k_done, rs_done, kr_done, ks_done, v_done, ov_done, x_done) = [
             ctx.enter_context(nc.semaphore("r_" + n)) for n in names]
        mod = S.mod[1]

        with nc.Block() as block:

            @block.tensor
            def _(pe):
                def mean(n):
                    nc.tensor.matmul(psM[:], S.meanw[:], S.X[:, ds(n * MT, MT)],
                                     start=True, stop=True).then_inc(mean_done, 1)

                def var(n):
                    pe.wait_ge(sq_done, n + 1)
                    nc.tensor.matmul(psM[:], S.meanw[:], sq[:], start=True, stop=True).then_inc(var_done, 1)

                def products(n, first=False):
                    pe.wait_ge(mix_done, n + 1)
                    if not first:
                        pe.wait_ge(rs_done, n)
                        pe.wait_ge(kr_done, n)
                    nc.tensor.matmul(psR[:], wr[:], mix[:, 0, :, :], start=True, stop=True).then_inc(r_done, 1)
                    nc.tensor.matmul(psK[:], wk[:], mix[:, 1, :, :], start=True, stop=True).then_inc(k_done, 1)

                def value(n):
                    pe.wait_ge(ks_done, n + 1)
                    nc.tensor.matmul(psV[:], wv[:], ks[:], start=True, stop=True).then_inc(v_done, 1)

                mean(0)
                var(0)
                products(0, first=True)
                pe.wait_ge(rstd_done, 1)
                mean(1)
                with nc.tensor.Fori(0, NT - 1) as n:
                    var(n + 1)
                    value(n)
                    products(n + 1)
                    mean(n + 2)
                value(NT - 1)

            @block.scalar
            def _(act):
                def square(n):
                    act.wait_ge(xc_done, n + 1)
                    nc.scalar.activation(sq[:], xc[:], ACT.Square).then_inc(sq_done, 1)

                def inv_std(n):
                    act.wait_ge(var_done, n + 1)
                    nc.scalar.activation(lnv[:], psM[:], ACT.Ln, bias=S.eps[:, 0:1]).then_inc(lnv_done, 1)
                    act.wait_ge(lnv_done, n + 1)
                    nc.scalar.activation(rstd[:], lnv[:], ACT.Exp, scale=-0.5).then_inc(rstd_done, 1)

                def predecessor(n):
                    act.wait_ge(h_done, n + 1)
                    for i in range(2):
                        last = nc.scalar.activation(old[:, i, :, :], H[:, :, 0:SEQ], ACT.Identity,
                                                    scale=nmu[:, i:i + 1])
                    last.then_inc(old_done, 1)

                def gates(n):
                    act.wait_ge(k_done, n + 1)
                    nc.scalar.activation(kr[:], psK[:], ACT.Relu).then_inc(kr_done, 1)
                    act.wait_ge(kr_done, n + 1)
                    nc.scalar.activation(ks[:], kr[:], ACT.Square).then_inc(ks_done, 1)
                    nc.scalar.activation(rs[:], psR[:], ACT.Sigmoid).then_inc(rs_done, 1)

                square(0)
                inv_std(0)
                predecessor(0)
                square(1)
                with nc.scalar.Fori(0, NT - 1) as n:
                    nc.scalar.preload_act_table_set("natural_log_exp_and_others")
                    inv_std(n + 1)
                    gates(n)
                    predecessor(n + 1)
                    square(n + 2)
                gates(NT - 1)

            @block.vector
            def _(dve):
                def center(n):
                    dve.wait_ge(mean_done, n + 1)
                    nc.vector.tensor_tensor(xc[:], S.X[:, ds(n * MT, MT)], psM[:], ALU.subtract).then_inc(xc_done, 1)

                def normalize(n):
                    dve.wait_ge(rstd_done, n + 1)
                    nc.vector.tensor_tensor(xc[:], xc[:], rstd[:], ALU.mult).then_inc(xn_done, 1)
                    dve.wait_ge(xn_done, n + 1)
                    for s in range(SPT):
                        last = nc.vector.tensor_scalar(H[:, s, 1:], xc[:, s * SEQ:(s + 1) * SEQ],
                                                       mod[:, SC_B, ds(n * SPT + s, 1)],
                                                       mod[:, SH_B, ds(n * SPT + s, 1)], ALU.mult, ALU.add)
                    last.then_inc(h_done, 1)

                def mixes(n, first=False):
                    dve.wait_ge(old_done, n + 1)
                    if not first:
                        dve.wait_ge(k_done, n)
                    for i in range(2):
                        last = nc.vector.scalar_tensor_tensor(mix[:, i, :, :], H[:, :, 1:], mu[:, i:i + 1],
                                                              old[:, i, :, :], ALU.mult, ALU.add)
                    last.then_inc(mix_done, 1)

                def residual(n):
                    dve.wait_ge(v_done, n + 1)
                    dve.wait_ge(rs_done, n + 1)
                    nc.vector.tensor_tensor(ov[:], rs[:], psV[:], ALU.mult).then_inc(ov_done, 1)
                    dve.wait_ge(ov_done, n + 1)
                    for s in range(SPT):
                        x = S.X[:, ds((n * SPT + s) * SEQ, SEQ)]
                        last = nc.vector.scalar_tensor_tensor(x, ov[:, s * SEQ:(s + 1) * SEQ],
                                                              mod[:, GB, ds(n * SPT + s, 1)], x, ALU.mult, ALU.add)
                    last.then_inc(x_done, 1)

                center(0)
                normalize(0)
                mixes(0, first=True)
                center(1)
                with nc.vector.Fori(0, NT - 1) as n:
                    normalize(n + 1)
                    residual(n)
                    mixes(n + 1)
                    center(n + 2)
                residual(NT - 1)


STAGES = [attention, moe, mamba, rwkv]

def store(nc, out, S):
    with ExitStack() as ctx:
        stored = ctx.enter_context(nc.semaphore("stored"))
        with nc.Block() as block:

            @block.sync
            def _(sp):
                sp.dma_start(out, S.X[:, 0:TOK]).then_inc(stored, 16)
                sp.wait_ge(stored, 16)

def build(nc, w, out, stages):
    S = Shared()
    with ExitStack() as ctx:
        constants_and_modulation(nc, ctx, w, S)
        for stage in stages:
            stage(nc, w, S)
        store(nc, out, S)

def layouts(inputs):
    import numpy as np

    i = {k: np.asarray(v) for k, v in inputs.items()}
    t = lambda a, *o: np.ascontiguousarray(a.transpose(*o))

    down = lambda a: np.ascontiguousarray(np.moveaxis(np.swapaxes(a, -1, -2).reshape(a.shape[:-2] + (2, P, P)), -2, 0))
    arrays = {
        "x": t(i["L0_attn_x_bld"].reshape(TOK, P), 1, 0),
        "c0": t(i["L0_c"], 1, 0), "c1": t(i["L1_c"], 1, 0),
        "wmod0": i["L0_wmod"].reshape(P, 6, P), "wmod1": i["L1_wmod"].reshape(P, 6, P),
        "wqT": t(i["L0_attn_Wq"], 2, 1, 0), "wkuT": t(i["L0_attn_Wk_up"], 2, 1, 0),
        "wvuT": t(i["L0_attn_Wv_up"], 2, 1, 0), "wo": t(i["L0_attn_Wout"], 1, 0, 2),
        "wlat": i["L0_attn_Wkv_down"],
        "sg": t(i["L0_ffn_sg_w"], 1, 0), "su": t(i["L0_ffn_su_w"], 1, 0), "sd": down(i["L0_ffn_sd_w"]),
        "wg": t(i["L0_ffn_wg"], 2, 0, 1), "wu": t(i["L0_ffn_wu"], 2, 0, 1), "wd": down(i["L0_ffn_wd"]),
        "router": t(i["L0_ffn_router_w"], 1, 0), "rbias": i["L0_ffn_routing_bias"].reshape(1, NEXP),
        "wz": t(i["L1_attn_W_z"], 1, 0), "wpar": t(i["L1_attn_W_params"], 1, 0),
        "conv": i["L1_attn_conv_w"].reshape(P, TAPS), "wdt": t(i["L1_attn_W_dt"], 1, 0),
        "bdt": i["L1_attn_b_dt"].reshape(P, 1), "alog": i["L1_attn_A_log"], "dskip": i["L1_attn_D"].reshape(P, 1),
        "wout": t(i["L1_attn_W_out"], 1, 0),
        "wr": t(i["L1_ffn_W_r"], 1, 0), "wk": t(i["L1_ffn_W_k"], 1, 0), "wv": t(i["L1_ffn_W_v"], 1, 0),
        "mur": i["L1_ffn_mu_r"].reshape(P, 1), "muk": i["L1_ffn_mu_k"].reshape(P, 1),
    }
    return arrays

def kernel(**inputs):
    import numpy as np
    import concourse.bacc as bacc
    from concourse.bass_utils import run_bass_kernel_spmd

    nc = bacc.Bacc("TRN2", target_bir_lowering=False, num_devices=1)
    arrays = layouts(inputs)
    w = {k: nc.dram_tensor("in_" + k, a.shape, mybir.dt.from_np(a.dtype), kind="ExternalInput").ap()
         for k, a in arrays.items()}
    out = nc.dram_tensor("out", [P, TOK], F32, kind="ExternalOutput").ap()
    build(nc, w, out, [attention, moe, mamba, rwkv])
    r = run_bass_kernel_spmd(nc, [{"in_" + k: a for k, a in arrays.items()}], core_ids=[0])
    xT = r.results[0]["out"]
    return np.ascontiguousarray(xT.transpose(1, 0)).reshape(NSEQ, SEQ, P)
```

```python
from contextlib import ExitStack

import concourse.bass as bass
from concourse import mybir

P = 128
SEQ = 256
NSEQ = 32
TOK = NSEQ * SEQ
PAD = 6
HEADS = 16
LD = 32
HD = 64
PAIRS = HEADS // 2
GROUPS = HEADS // 4
NEXP = 8
NALL = NEXP + 1
NST = 16
RDT = 64
TAPS = 4
NEG = -1.0e30
EPS = 1e-5

F32 = mybir.dt.float32
F32R = mybir.dt.float32r
BF16 = mybir.dt.bfloat16
ACT = mybir.ActivationFunctionType
ALU = mybir.AluOpType
AX = mybir.AxisListType.X
ds = bass.ds

SH_A, SC_A, GA, SH_B, SC_B, GB = range(6)


class Shared:
    pass


def constants_and_modulation(nc, ctx, w, S):
    def sb(name, shape, dt=F32):
        return ctx.enter_context(nc.sbuf_tensor(name, shape, dt))

    S.X = sb("X", [P, TOK + PAD * SEQ])
    S.mod = [sb("mod0", [P, 6, NSEQ + PAD]), sb("mod1", [P, 6, NSEQ + PAD])]
    S.meanw = sb("meanw", [P, P])
    S.center = sb("center", [P, P])
    S.ident = sb("ident", [P, P])
    S.identb = sb("identb", [P, P], BF16)
    S.eps = sb("eps", [P, 1])
    S.spare = sb("spare", [P, 8])

    with ExitStack() as loc:
        def lsb(name, shape, dt=F32):
            return loc.enter_context(nc.sbuf_tensor(name, shape, dt))

        cT = [lsb("cT0", [P, NSEQ]), lsb("cT1", [P, NSEQ])]
        wmod = [lsb("wm0", [P, 6, P]), lsb("wm1", [P, 6, P])]
        sc = [lsb("siluc0", [P, NSEQ]), lsb("siluc1", [P, NSEQ])]
        gpos = lsb("gpos", [P, NSEQ])
        gneg = lsb("gneg", [P, NSEQ])
        ps = loc.enter_context(nc.psum_tensor("ps_mod", [P, 2, 512], F32))
        sem = lambda n: loc.enter_context(nc.semaphore(n))
        loaded, x_loaded, silu_done, mod_done, filled, gate_step, built = map(
            sem, ["loaded", "x_loaded", "silu_done", "mod_done", "filled", "gate_step", "built"])
        with nc.Block() as block:

            @block.sync
            def _(sp):
                for l in range(2):
                    sp.dma_start(cT[l][:], w[f"c{l}"]).then_inc(loaded, 16)
                    sp.dma_start(wmod[l][:], w[f"wmod{l}"]).then_inc(loaded, 16)
                sp.dma_start(S.X[:, 0:TOK], w["x"]).then_inc(x_loaded, 16)
                sp.wait_ge(x_loaded, 16)

            @block.scalar
            def _(act):
                act.wait_ge(loaded, 64)
                for l in range(2):
                    nc.scalar.activation(sc[l][:], cT[l][:], ACT.Silu).then_inc(silu_done, 1)

            @block.tensor
            def _(pe):
                for l in range(2):
                    pe.wait_ge(silu_done, l + 1)
                    for r in range(6):
                        last = nc.tensor.matmul(ps[:, l, r * NSEQ:(r + 1) * NSEQ], wmod[l][:, r, :], sc[l][:],
                                                start=(r == 0), stop=(r == 5))
                    last.then_inc(mod_done, 1)

            @block.gpsimd
            def _(pool):
                nc.gpsimd.memset(S.meanw[:], 1.0 / P)
                nc.gpsimd.memset(S.eps[:], EPS)
                nc.gpsimd.memset(S.X[:, TOK:], 0.0)
                for l in range(2):
                    nc.gpsimd.memset(S.mod[l][:, :, NSEQ:], 0.0)
                nc.gpsimd.memset(S.ident[:], 0.0).then_inc(filled, 1)
                pool.wait_ge(filled, 1)
                nc.gpsimd.affine_select(out=S.ident[:], in_=S.ident[:], compare_op=ALU.not_equal, fill=1.0,
                                        base=0, pattern=[[-1, P]], channel_multiplier=1).then_inc(filled, 1)
                pool.wait_ge(filled, 2)
                nc.gpsimd.tensor_copy(S.identb[:], S.ident[:])

            @block.vector
            def _(dve):
                n = 0
                for l in range(2):
                    dve.wait_ge(mod_done, l + 1)
                    for r in range(6):
                        row = ps[:, l, r * NSEQ:(r + 1) * NSEQ]
                        out = S.mod[l][:, r, 0:NSEQ]
                        if r in (SH_A, SH_B):
                            nc.vector.tensor_copy(out, row)
                        elif r in (SC_A, SC_B):
                            nc.vector.tensor_scalar(out, row, 1.0, None, ALU.add)
                        else:
                            nc.vector.tensor_scalar(gpos[:], row, 0.25, None, ALU.max)
                            nc.vector.tensor_scalar(gneg[:], row, -0.25, None, ALU.min).then_inc(gate_step, 1)
                            dve.wait_ge(gate_step, 3 * n + 1)
                            nc.vector.scalar_tensor_tensor(gpos[:], row, 0.0, gpos[:], ALU.is_ge, ALU.mult)
                            nc.vector.scalar_tensor_tensor(gneg[:], row, 0.0, gneg[:], ALU.is_lt, ALU.mult
                                                           ).then_inc(gate_step, 1)
                            dve.wait_ge(gate_step, 3 * n + 2)
                            nc.vector.tensor_tensor(out, gpos[:], gneg[:], ALU.add).then_inc(gate_step, 1)
                            n += 1
                            dve.wait_ge(gate_step, 3 * n)
                dve.wait_ge(filled, 2)
                nc.vector.tensor_tensor(S.center[:], S.ident[:], S.meanw[:], ALU.subtract)


def attention(nc, w, S):
    with ExitStack() as ctx:
        def sb(name, shape, dt=F32):
            return ctx.enter_context(nc.sbuf_tensor(name, shape, dt))

        def pb(name, n):
            return ctx.enter_context(nc.psum_tensor(name, [P, n * 512], F32))

        wq = sb("wq", [HD, HEADS, P])
        wku = sb("wku", [HD, HEADS, LD])
        wvu = sb("wvu", [HD, HEADS, LD])
        wo = sb("wo", [HD, HEADS, P])
        wlat = sb("wlat", [P, 4, LD])
        wqk = sb("wqk", [P, HEADS, 4, LD])
        wvo = sb("wvo", [P, GROUPS, P])
        mask_s = sb("mask_s", [P, P], BF16)
        mask_t = sb("mask_t", [P, P], BF16)
        sel0 = sb("sel0", [2 * HEADS, HEADS, P])
        sel = sb("sel", [2 * HEADS, HEADS, P], F32R)
        ones = sb("ones", [P, LD])

        xc = sb("xc", [P, SEQ])
        sq = sb("sq", [P, SEQ])
        lnv = sb("lnv", [P, SEQ])
        rstd = sb("rstd", [P, SEQ])
        H = sb("H", [P, 2, SEQ])
        lat = sb("lat", [P, 2, SEQ], F32R)
        lat_tok = sb("lat_tok", [P, 2, 2, LD])
        Q = sb("Q", [P, 2, HEADS, SEQ], F32R)
        mx = sb("mx", [P, 2, HEADS])
        mhl = sb("mhl", [P, 2, 2, HEADS])
        nm = sb("nm", [2 * HEADS, SEQ], F32R)
        prob = sb("prob", [P, 4, 768])
        lden = sb("lden", [P, SEQ])
        rden = sb("rden", [P, SEQ])
        cn = sb("cn", [P, GROUPS, SEQ])

        psS, psT = pb("psS", 2), pb("psT", 2)
        psQ, psC, psM, psY = pb("psQ", 1), pb("psC", 1), pb("psM", 1), pb("psY", 1)

        with ExitStack() as pre:
            sem = lambda n: pre.enter_context(nc.semaphore(n))
            loaded, made, filled, copied = map(sem, ["a_loaded", "a_made", "a_filled", "a_copied"])
            with nc.Block() as block:

                @block.sync
                def _(sp):
                    for t, name in ((wq, "wqT"), (wku, "wkuT"), (wvu, "wvuT"), (wo, "wo")):
                        sp.dma_start(t[:], w[name]).then_inc(loaded, 16)
                    for r in range(4):
                        sp.dma_start(wlat[:, r, :], w["wlat"]).then_inc(loaded, 16)
                    sp.wait_ge(loaded, 128)

                @block.gpsimd
                def _(pool):
                    nc.gpsimd.memset(ones[:], 1.0)
                    nc.gpsimd.memset(sel0[:], 0.0)
                    nc.gpsimd.memset(mask_s[:], 0.0)
                    nc.gpsimd.memset(mask_t[:], 0.0).then_inc(filled, 1)
                    pool.wait_ge(filled, 1)
                    nc.gpsimd.affine_select(out=sel0[:], in_=sel0[:], compare_op=ALU.not_equal, fill=1.0,
                                            base=0, pattern=[[-1, HEADS], [0, P]], channel_multiplier=1
                                            ).then_inc(filled, 1)
                    nc.gpsimd.affine_select(out=mask_s[:], in_=mask_s[:], compare_op=ALU.is_ge, fill=NEG,
                                            base=0, pattern=[[-1, P]], channel_multiplier=1)
                    nc.gpsimd.affine_select(out=mask_t[:], in_=mask_t[:], compare_op=ALU.is_ge, fill=NEG,
                                            base=0, pattern=[[1, P]], channel_multiplier=-1)
                    pool.wait_ge(filled, 2)
                    nc.gpsimd.affine_select(out=sel0[:], in_=sel0[:], compare_op=ALU.not_equal, fill=1.0,
                                            base=-HEADS, pattern=[[-1, HEADS], [0, P]], channel_multiplier=1
                                            ).then_inc(filled, 1)

                @block.tensor
                def _(pe):
                    pe.wait_ge(loaded, 128)
                    for h in range(HEADS):
                        last = nc.tensor.matmul(psS[:, h * LD:(h + 1) * LD], wq[:, h, :], wku[:, h, :],
                                                start=(h == 0), stop=(h == HEADS - 1))
                    for h in range(HEADS):
                        g, q = divmod(h, 4)
                        last = nc.tensor.matmul(psT[LD * q:LD * (q + 1), g * P:(g + 1) * P], wvu[:, h, :],
                                                wo[:, h, :], start=(g == 0), stop=(g == GROUPS - 1))
                    last.then_inc(made, 1)

                @block.vector
                def _(dve):
                    dve.wait_ge(made, 1)
                    for r in range(4):
                        nc.vector.tensor_scalar(wqk[:, :, r, :], psS[:, 0:512].rearrange("p (h c) -> p h c", h=HEADS),
                                                HD ** -0.5, None, ALU.mult)
                    nc.vector.tensor_copy(wvo[:], psT[:, 0:512].rearrange("p (g c) -> p g c", g=GROUPS))
                    dve.wait_ge(filled, 3)
                    nc.vector.tensor_copy(sel[:], sel0[:]).then_inc(copied, 1)

        names = ["mean_done", "xc_done", "sq_done", "var_done", "lnv_done", "rstd_done", "xn_done", "h_done",
                 "lat_done", "lat_hi", "lat_lo", "q_done", "q_hi", "q_lo", "s_done", "max_done", "mh_done",
                 "mhl_done", "mt_done", "nm_done", "st_done", "exp_done", "pv_done", "lden_done", "rden_done",
                 "ctx_done", "y_done", "x_done"]
        (mean_done, xc_done, sq_done, var_done, lnv_done, rstd_done, xn_done, h_done, lat_done, lat_hi, lat_lo,
         q_done, q_hi, q_lo, s_done, max_done, mh_done, mhl_done, mt_done, nm_done, st_done, exp_done, pv_done,
         lden_done, rden_done, ctx_done, y_done, x_done) = [ctx.enter_context(nc.semaphore("a_" + n)) for n in names]

        EXP0, PV0, CTX0, X0 = 1, 2, 1, 1
        mod = S.mod[0]

        with nc.Block() as block:

            @block.tensor
            def _(pe):
                def mean(n, first=False):
                    if not first:
                        pe.wait_ge(lat_lo, n)
                    nc.tensor.matmul(psM[:, 0:SEQ], S.meanw[:], S.X[:, ds(n * SEQ, SEQ)],
                                     start=True, stop=True).then_inc(mean_done, 1)

                def var(n):
                    pe.wait_ge(sq_done, n + 1)
                    nc.tensor.matmul(psM[:, 0:SEQ], S.meanw[:], sq[:], start=True, stop=True).then_inc(var_done, 1)

                def latent(n, par):
                    pe.wait_ge(h_done, n + 1)
                    nc.tensor.matmul(psM[:, 0:SEQ], wlat[:].rearrange("p r c -> p (r c)"), H[:, par, :],
                                     start=True, stop=False)
                    for kb in range(2):
                        last = nc.tensor.matmul(psM[:, SEQ + kb * LD:SEQ + (kb + 1) * LD],
                                                H[:, par, kb * P:(kb + 1) * P], wlat[:, 0, :],
                                                start=False, stop=(kb == 1))
                    last.then_inc(lat_done, 1)

                def query(n, par, p, first=False):
                    if not (first and p == 0):
                        pe.wait_ge(q_lo, n * PAIRS + p)
                    if p == 0:
                        pe.wait_ge(h_done, n + 1)
                        if not first:
                            pe.wait_ge(nm_done, n)
                    for k in range(2):
                        last = nc.tensor.matmul(psQ[:, k * SEQ:(k + 1) * SEQ],
                                                wqk[:, 2 * p + k, :, :].rearrange("p r c -> p (r c)"),
                                                H[:, par, :], start=(k == 0), stop=(k == 1))
                    last.then_inc(q_done, 1)

                def scores(n, par, p, first=False):
                    pe.wait_ge(q_lo, n * PAIRS + (p + 1))
                    if not (first and p == 0):
                        pe.wait_ge(max_done, n * PAIRS + p)
                    if p == 0:
                        pe.wait_ge(lat_lo, n + 1)
                    for k in range(2):
                        h, wide = 2 * p + k, 512 * k
                        near = 256 + 128 * k
                        if k == 1:
                            nc.tensor.matmul(psS[:, near:near + P], Q[:, par, h, 0:P], lat[:, par, 0:P],
                                             start=False, stop=False)
                            nc.tensor.matmul(psS[:, near:near + P], S.identb[:], mask_s[:], start=False, stop=True)
                        nc.tensor.matmul(psS[:, wide:wide + SEQ], Q[:, par, h, P:SEQ], lat[:, par, :],
                                         start=True, stop=False)
                        last = nc.tensor.matmul(psS[:, wide + P:wide + SEQ], S.identb[:], mask_s[:],
                                                start=False, stop=(k == 1))
                        if k == 0:
                            nc.tensor.matmul(psS[:, near:near + P], Q[:, par, h, 0:P], lat[:, par, 0:P],
                                             start=False, stop=False)
                            nc.tensor.matmul(psS[:, near:near + P], S.identb[:], mask_s[:], start=False, stop=False)
                    last.then_inc(s_done, 1)

                def scores_t(n, par, p):
                    if p == 0:
                        pe.wait_ge(nm_done, n + 1)
                    pe.wait_ge(exp_done, n * PAIRS + (p + EXP0))
                    for k in range(2):
                        h, wide = 2 * p + k, 512 * k
                        near = 256 + 128 * k

                        def far_keys(stop):
                            nc.tensor.matmul(psT[:, near:near + P], lat[:, par, P:SEQ], Q[:, par, h, P:SEQ],
                                             start=False, stop=False)
                            nc.tensor.matmul(psT[:, near:near + P], sel[:, h, :], nm[:, P:SEQ],
                                             start=False, stop=False)
                            nc.tensor.matmul(psT[:, near:near + P], S.identb[:], mask_t[:], start=False, stop=stop)

                        if k == 1:
                            far_keys(True)
                        nc.tensor.matmul(psT[:, wide:wide + SEQ], lat[:, par, 0:P], Q[:, par, h, :],
                                         start=True, stop=False)
                        nc.tensor.matmul(psT[:, wide:wide + SEQ], sel[:, h, :], nm[:], start=False, stop=False)
                        last = nc.tensor.matmul(psT[:, wide:wide + P], S.identb[:], mask_t[:],
                                                start=False, stop=(k == 1))
                        if k == 0:
                            far_keys(False)
                    last.then_inc(st_done, 1)

                def values(n, par, g):
                    pe.wait_ge(exp_done, n * PAIRS + (2 * g + 2 + EXP0))
                    pe.wait_ge(ctx_done, n * GROUPS + (g + CTX0))
                    for off, kb in ((0, 0), (0, 1), (SEQ, 0), (SEQ, 1)):
                        for q in range(4):
                            k = q % 2
                            at, cols = ((512 * k, SEQ), (256 + 128 * k, P))[kb]
                            first = off + SEQ - cols
                            last = nc.tensor.matmul(
                                psC[LD * q:LD * (q + 1), first:off + SEQ],
                                lat_tok[:, par, kb, :] if off == 0 else ones[:],
                                prob[:, (2 * g + q // 2) % 4, at:at + cols],
                                start=(off == 0 and kb == 0), stop=(off == SEQ and kb == 1))
                    last.then_inc(pv_done, 1)

                def project(n, g):
                    if g == 0:
                        pe.wait_ge(x_done, n + X0)
                    pe.wait_ge(ctx_done, n * GROUPS + (g + 1 + CTX0))
                    last = nc.tensor.matmul(psY[:, 0:SEQ], wvo[:, g, :], cn[:, g, :],
                                            start=(g == 0), stop=(g == GROUPS - 1))
                    if g == GROUPS - 1:
                        last.then_inc(y_done, 1)

                def max_t(n):
                    pe.wait_ge(mhl_done, n + 1)
                    pe.wait_ge(q_lo, n * PAIRS + PAIRS)
                    for qb in range(2):
                        last = nc.tensor.transpose(psQ[0:2 * HEADS, qb * P:(qb + 1) * P],
                                                   mhl[:, qb, :, :].rearrange("p a h -> p (a h)"), S.ident[:])
                    last.then_inc(mt_done, 1)

                mean(0, first=True)
                var(0)
                latent(0, 0)
                mean(1)
                for p in range(PAIRS):
                    query(0, 0, p, first=True)
                    if p > 0:
                        scores(0, 0, p - 1, first=True)
                    if p == 3:
                        var(1)
                scores(0, 0, PAIRS - 1, first=True)
                latent(1, 1)
                max_t(0)
                with nc.tensor.Fori(0, NSEQ // 2) as j:
                    for par in range(2):
                        n = j * 2 + par
                        for p in range(PAIRS):
                            query(n + 1, 1 - par, p)
                            if p > 0:
                                scores(n + 1, 1 - par, p - 1)
                            scores_t(n, par, p)
                            if p >= 2 and p % 2 == 0:
                                values(n, par, p // 2 - 1)
                            if p == 1:
                                mean(n + 2)
                            if p == 4:
                                var(n + 2)
                            if p in (4, 6):
                                project(n, p // 2 - 2)
                        scores(n + 1, 1 - par, PAIRS - 1)
                        values(n, par, GROUPS - 1)
                        latent(n + 2, par)
                        project(n, 2)
                        max_t(n + 1)
                        project(n, 3)

            @block.scalar
            def _(act):
                def square(n):
                    act.wait_ge(xc_done, n + 1)
                    nc.scalar.activation(sq[:], xc[:], ACT.Square).then_inc(sq_done, 1)

                def inv_std(n):
                    act.wait_ge(var_done, n + 1)
                    nc.scalar.activation(lnv[:], psM[:, 0:SEQ], ACT.Ln, bias=S.eps[:, 0:1]).then_inc(lnv_done, 1)
                    act.wait_ge(lnv_done, n + 1)
                    nc.scalar.activation(rstd[:], lnv[:], ACT.Exp, scale=-0.5).then_inc(rstd_done, 1)

                def latent_hi(n, par):
                    act.wait_ge(lat_done, n + 1)
                    nc.scalar.copy(lat[:, par, :], psM[:, 0:SEQ]).then_inc(lat_hi, 1)

                def query_hi(n, par, p):
                    act.wait_ge(q_done, n * PAIRS + (p + 1))
                    nc.scalar.copy(Q[:, par, 2 * p:2 * p + 2, :], psQ[:, :].rearrange("p (h q) -> p h q", h=2)
                                   ).then_inc(q_hi, 1)

                def max_copy(n):
                    act.wait_ge(mt_done, n + 1)
                    nc.scalar.copy(nm[:], psQ[0:2 * HEADS, 0:SEQ]).then_inc(nm_done, 1)

                def softmax_exp(n, p):
                    act.wait_ge(st_done, n * PAIRS + (p + 1))
                    if p % 2 == 0:
                        act.wait_ge(pv_done, n * GROUPS + (p // 2 - 1 + PV0))
                    nc.scalar.activation(prob[:, p % 4, :], psT[:, 0:768], ACT.Exp).then_inc(exp_done, 1)

                def inv_den(n, g):
                    act.wait_ge(pv_done, n * GROUPS + (g + 1 + PV0))
                    nc.scalar.activation(lden[:], psC[:, SEQ:512], ACT.Ln).then_inc(lden_done, 1)
                    act.wait_ge(lden_done, n * GROUPS + (g + 1))
                    nc.scalar.activation(rden[:], lden[:], ACT.Exp, scale=-1.0).then_inc(rden_done, 1)

                nc.scalar.preload_act_table_set("natural_log_exp_and_others")
                square(0)
                inv_std(0)
                latent_hi(0, 0)
                square(1)
                for p in range(PAIRS):
                    query_hi(0, 0, p)
                    if p == 4:
                        inv_std(1)
                latent_hi(1, 1)
                max_copy(0)
                nc.scalar.copy(S.spare[:, 4:5], S.eps[:, 0:1]).then_inc(exp_done, EXP0)
                with nc.scalar.Fori(0, NSEQ // 2) as j:
                    for par in range(2):
                        n = j * 2 + par
                        for p in range(PAIRS):
                            query_hi(n + 1, 1 - par, p)
                            softmax_exp(n, p)
                            if p == 2:
                                square(n + 2)
                            if p == 5:
                                inv_std(n + 2)
                            if p >= 3 and p % 2 == 1:
                                inv_den(n, (p - 3) // 2)
                        inv_den(n, GROUPS - 1)
                        latent_hi(n + 2, par)
                        max_copy(n + 1)

            @block.vector
            def _(dve):
                def center(n):
                    dve.wait_ge(mean_done, n + 1)
                    nc.vector.tensor_tensor(xc[:], S.X[:, ds(n * SEQ, SEQ)], psM[:, 0:SEQ], ALU.subtract
                                            ).then_inc(xc_done, 1)

                def normalize(n, par):
                    dve.wait_ge(rstd_done, n + 1)
                    nc.vector.tensor_tensor(xc[:], xc[:], rstd[:], ALU.mult).then_inc(xn_done, 1)
                    dve.wait_ge(xn_done, n + 1)
                    nc.vector.tensor_scalar(H[:, par, :], xc[:], mod[:, SC_A, ds(n, 1)], mod[:, SH_A, ds(n, 1)],
                                            ALU.mult, ALU.add).then_inc(h_done, 1)

                def latent_lo(n, par):
                    dve.wait_ge(lat_hi, n + 1)
                    for r in (1, 3):
                        rows = slice(LD * r, LD * (r + 1))
                        nc.vector.tensor_tensor(lat[rows, par, :], psM[rows, 0:SEQ], lat[rows, par, :], ALU.subtract)
                    nc.vector.tensor_copy(lat_tok[:, par, :, :],
                                          psM[:, SEQ:SEQ + 2 * LD].rearrange("p (k c) -> p k c", k=2)
                                          ).then_inc(lat_lo, 1)

                def query_lo(n, par, p):
                    dve.wait_ge(q_hi, n * PAIRS + (p + 1))
                    half = slice(2 * LD, 4 * LD)
                    nc.vector.tensor_tensor(Q[half, par, 2 * p:2 * p + 2, :],
                                            psQ[half, :].rearrange("p (h q) -> p h q", h=2),
                                            Q[half, par, 2 * p:2 * p + 2, :], ALU.subtract).then_inc(q_lo, 1)

                def maximum(n, p):
                    dve.wait_ge(s_done, n * PAIRS + (p + 1))
                    nc.vector.tensor_reduce(mx[:, 1, 2 * p:2 * p + 2],
                                            psS[:, :].rearrange("p (h q) -> p h q", h=2)[:, :, 0:SEQ], AX, ALU.max)
                    nc.vector.tensor_reduce(mx[:, 0, 2 * p:2 * p + 2],
                                            psS[:, 256:512].rearrange("p (h q) -> p h q", h=2), AX, ALU.max
                                            ).then_inc(max_done, 1)

                def max_split(n):
                    dve.wait_ge(max_done, n * PAIRS + PAIRS)
                    nc.vector.tensor_scalar(mhl[:, :, 0, :].bitcast(F32R), mx[:], -1.0, None, ALU.mult
                                            ).then_inc(mh_done, 1)
                    dve.wait_ge(mh_done, n + 1)
                    nc.vector.scalar_tensor_tensor(mhl[:, :, 1, :], mx[:], -1.0, mhl[:, :, 0, :],
                                                   ALU.mult, ALU.subtract).then_inc(mhl_done, 1)

                def context(n, g):
                    dve.wait_ge(rden_done, n * GROUPS + (g + 1))
                    nc.vector.tensor_tensor(cn[:, g, :], psC[:, 0:SEQ], rden[:], ALU.mult).then_inc(ctx_done, 1)

                def residual(n):
                    dve.wait_ge(y_done, n + 1)
                    x = S.X[:, ds(n * SEQ, SEQ)]
                    nc.vector.scalar_tensor_tensor(x, psY[:, 0:SEQ], mod[:, GA, ds(n, 1)], x, ALU.mult, ALU.add
                                                   ).then_inc(x_done, 1)

                nc.vector.memset(S.spare[:, 0:1], 0.0).then_inc(pv_done, PV0)
                nc.vector.memset(S.spare[:, 1:2], 0.0).then_inc(ctx_done, CTX0)
                nc.vector.memset(S.spare[:, 2:3], 0.0).then_inc(x_done, X0)
                center(0)
                normalize(0, 0)
                latent_lo(0, 0)
                center(1)
                for p in range(PAIRS):
                    query_lo(0, 0, p)
                    if p > 0:
                        maximum(0, p - 1)
                    if p == 5:
                        normalize(1, 1)
                maximum(0, PAIRS - 1)
                max_split(0)
                latent_lo(1, 1)
                with nc.vector.Fori(0, NSEQ // 2) as j:
                    for par in range(2):
                        n = j * 2 + par
                        for p in range(PAIRS):
                            query_lo(n + 1, 1 - par, p)
                            if p > 0:
                                maximum(n + 1, p - 1)
                            if p == 2:
                                center(n + 2)
                            if p == 6:
                                normalize(n + 2, par)
                            if p >= 3 and p % 2 == 1:
                                context(n, (p - 3) // 2)
                        maximum(n + 1, PAIRS - 1)
                        max_split(n + 1)
                        context(n, GROUPS - 1)
                        latent_lo(n + 2, par)
                        residual(n)


MT = 512
NT = TOK // MT
SPT = MT // SEQ
UNITS = 2 * NALL
LEAD = 3
SUB = MT // P


def moe(nc, w, S):
    with ExitStack() as ctx:
        def sb(name, shape, dt=F32):
            return ctx.enter_context(nc.sbuf_tensor(name, shape, dt))

        def pb(name, n):
            return ctx.enter_context(nc.psum_tensor(name, [P, n, 512], F32))

        WG = [sb(f"WG{i}", [P, NALL, 2, P], F32R) for i in range(2)]
        WU = [sb(f"WU{i}", [P, NALL, 2, P], F32R) for i in range(2)]
        WD = sb("WD", [P, NALL, 2, P])
        wr = sb("wr_m", [P, NEXP])
        bias = sb("bias_m", [P, SUB, NEXP])
        tri = sb("tri", [P, NEXP, NEXP])
        sel0 = sb("sel0_m", [2 * NALL, NALL, P])
        sel = sb("sel_m", [2 * NALL, NALL, P], F32R)

        xc = sb("xc_m", [P, MT])
        sq = sb("sq_m", [P, MT])
        lnv = sb("lnv_m", [P, MT])
        rstd = sb("rstd_m", [P, MT])
        H = sb("H_m", [P, 2, MT])
        Hh = sb("Hh_m", [P, 2, MT], F32R)
        Hl = sb("Hl_m", [P, 2, MT], F32R)
        lg = sb("lg", [P, SUB, NEXP])
        pr = sb("pr", [P, SUB, NEXP])
        beats = sb("beats", [P, SUB, NEXP, NEXP])
        ties = sb("ties", [P, SUB, NEXP, NEXP])
        rank = sb("rank", [P, SUB, NEXP])
        pick = sb("pick", [P, SUB, NEXP])
        psum2 = sb("psum2", [P, SUB])
        wt = sb("wt", [P, SUB, NEXP])
        whl = sb("whl", [P, SUB, 2, NALL])
        wT = sb("wT", [2 * NALL, 2, MT], F32R)
        sg = sb("sg", [P, 2, MT])
        tt = sb("tt", [P, 2, MT])
        wbs = sb("wbs", [P, 2, MT])
        tw = sb("tw", [P, 4, MT])

        psG, psU, psY = pb("psG", 2), pb("psU", 2), pb("psY_m", 2)
        psW, psM = pb("psW", 1), pb("psM_m", 1)

        with ExitStack() as pre:
            sem = lambda n: pre.enter_context(nc.semaphore(n))
            loaded, high, filled, low = map(sem, ["m_loaded", "m_high", "m_filled", "m_low"])
            raw = [pre.enter_context(nc.sbuf_tensor(n, [P, NALL, 2, P], F32)) for n in ("rawG", "rawU")]
            with nc.Block() as block:

                @block.sync
                def _(sp):
                    for t, routed, shared in ((raw[0], "wg", "sg"), (raw[1], "wu", "su"), (WD, "wd", "sd")):
                        if routed == "wd":
                            sp.dma_start(t[:, 0:NEXP, :, :], w[routed]).then_inc(loaded, 16)
                            sp.dma_start(t[:, NEXP, :, :], w[shared]).then_inc(loaded, 16)
                        else:
                            sp.dma_start(t[:, 0:NEXP, :, :].rearrange("p e a i -> p e (a i)"), w[routed]
                                         ).then_inc(loaded, 16)
                            sp.dma_start(t[:, NEXP, :, :].rearrange("p a i -> p (a i)"), w[shared]
                                         ).then_inc(loaded, 16)
                    sp.dma_start(wr[:], w["router"]).then_inc(loaded, 16)
                    for s in range(SUB):
                        sp.dma_start(bias[:, s, :], w["rbias"].to_broadcast([P, NEXP])).then_inc(loaded, 16)
                    sp.wait_ge(loaded, 16 * (7 + SUB))

                @block.gpsimd
                def _(pool):
                    nc.gpsimd.memset(tri[:], 1.0)
                    nc.gpsimd.memset(whl[:, :, 0, NEXP], 1.0)
                    nc.gpsimd.memset(whl[:, :, 1, NEXP], 0.0)
                    nc.gpsimd.memset(sel0[:], 0.0).then_inc(filled, 1)
                    pool.wait_ge(filled, 1)
                    nc.gpsimd.affine_select(out=tri[:], in_=tri[:], compare_op=ALU.is_ge, fill=0.0, base=-1,
                                            pattern=[[1, NEXP], [-1, NEXP]], channel_multiplier=0)
                    nc.gpsimd.affine_select(out=sel0[:], in_=sel0[:], compare_op=ALU.not_equal, fill=1.0, base=0,
                                            pattern=[[-1, NALL], [0, P]], channel_multiplier=1).then_inc(filled, 1)
                    pool.wait_ge(filled, 2)
                    nc.gpsimd.affine_select(out=sel0[:], in_=sel0[:], compare_op=ALU.not_equal, fill=1.0,
                                            base=-NALL, pattern=[[-1, NALL], [0, P]], channel_multiplier=1
                                            ).then_inc(filled, 1)

                @block.scalar
                def _(act):
                    act.wait_ge(loaded, 16 * (7 + SUB))
                    for t, out in zip(raw, (WG, WU)):
                        nc.scalar.copy(out[0][:], t[:]).then_inc(high, 1)

                @block.vector
                def _(dve):
                    for n, (t, out) in enumerate(zip(raw, (WG, WU))):
                        dve.wait_ge(high, n + 1)
                        nc.vector.tensor_tensor(out[1][:], t[:], out[0][:], ALU.subtract)
                    dve.wait_ge(filled, 3)
                    nc.vector.tensor_copy(sel[:], sel0[:]).then_inc(low, 1)

        names = ["mean_done", "xc_done", "sq_done", "var_done", "lnv_done", "rstd_done", "xn_done", "h_done",
                 "hh_done", "hl_done", "lgp_done", "lg_done", "pr_done", "route", "wh_done", "whl_done", "wtp_done", "wt_done",
                 "gu_done", "silu_done", "t_done", "wb_done", "wbs_done", "tw_done",
                 "down_done", "x_done"]
        (mean_done, xc_done, sq_done, var_done, lnv_done, rstd_done, xn_done, h_done, hh_done, hl_done, lgp_done,
         lg_done, pr_done, route, wh_done, whl_done, wtp_done, wt_done, gu_done, silu_done, t_done, wb_done, wbs_done,
         tw_done, down_done, x_done) = [ctx.enter_context(nc.semaphore("m_" + n)) for n in names]
        TW0, DN0, X0 = 4, 4, 2
        ROUTE = 8
        mod = S.mod[0]

        def ahead(par, k, by):
            return ((0, par, k + by) if k + by < UNITS else (1, 1 - par, k + by - UNITS))

        with nc.Block() as block:

            @block.tensor
            def _(pe):
                def mean(n, first=False):
                    if not first:
                        pe.wait_ge(wt_done, n)
                    nc.tensor.matmul(psM[:, 0, :], S.meanw[:], S.X[:, ds(n * MT, MT)],
                                     start=True, stop=True).then_inc(mean_done, 1)

                def var(n):
                    pe.wait_ge(sq_done, n + 1)
                    nc.tensor.matmul(psM[:, 0, :], S.meanw[:], sq[:], start=True, stop=True).then_inc(var_done, 1)

                def logits(n, par):
                    pe.wait_ge(h_done, n + 1)
                    for s in range(SUB):
                        last = nc.tensor.matmul(psM[:, 0, s * NEXP:(s + 1) * NEXP], H[:, par, s * P:(s + 1) * P],
                                                wr[:], start=(s == 0), stop=(s == SUB - 1))
                    last.then_inc(lgp_done, 1)

                def weights_t(n):
                    pe.wait_ge(whl_done, n + 1)
                    for s in range(SUB):
                        last = nc.tensor.transpose(psM[0:2 * NALL, 0, s * P:(s + 1) * P],
                                                   whl[:, s, :, :].rearrange("p a e -> p (a e)"), S.ident[:])
                    last.then_inc(wtp_done, 1)

                def up(n, par, k, first=False):
                    e, half = divmod(k, 2)
                    u = par * UNITS + k
                    if k == 0:
                        pe.wait_ge(hl_done, n + 1)
                        pe.wait_ge(wt_done, n + 1)
                    if not (first and k < 2):
                        pe.wait_ge(silu_done, n * UNITS + (k - 1))
                        pe.wait_ge(t_done, n * UNITS + (k - 1))
                    for W, bank in ((WG, psG), (WU, psU)):
                        nc.tensor.matmul(bank[:, u % 2, :], W[0][:, e, half, :], Hh[:, par, :], start=True, stop=False)
                        nc.tensor.matmul(bank[:, u % 2, :], W[0][:, e, half, :], Hl[:, par, :], start=False, stop=False)
                        last = nc.tensor.matmul(bank[:, u % 2, :], W[1][:, e, half, :], Hh[:, par, :],
                                                start=False, stop=True)
                    last.then_inc(gu_done, 1)
                    if half == 0:
                        if not (first and k == 0):
                            pe.wait_ge(wbs_done, n * NALL + e)
                        nc.tensor.matmul(psW[:, 0, :], sel[:, e, :], wT[:, par, :], start=True, stop=True
                                         ).then_inc(wb_done, 1)

                def down(n, par, k):
                    e, half = divmod(k, 2)
                    u = par * UNITS + k
                    pe.wait_ge(tw_done, n * UNITS + (k + 1 + TW0))
                    if k == 0:
                        pe.wait_ge(x_done, n + (X0 - 1))
                    nc.tensor.matmul(psY[:, par, :], WD[:, e, half, :], tw[:, u % 4, :], start=(k == 0),
                                     stop=(k == UNITS - 1)).then_inc(down_done, 1)

                mean(0, first=True)
                var(0)
                logits(0, 0)
                weights_t(0)
                for k in range(LEAD):
                    up(0, 0, k, first=True)
                with nc.tensor.Fori(0, NT // 2) as j:
                    for par in range(2):
                        n = j * 2 + par
                        for k in range(UNITS):
                            on, upar, uk = ahead(par, k, LEAD)
                            up(n + on, upar, uk)
                            down(n, par, k)
                            if k == 1:
                                mean(n + 1)
                            if k == 3:
                                var(n + 1)
                            if k == 6:
                                logits(n + 1, 1 - par)
                            if k == 12:
                                weights_t(n + 1)

            @block.scalar
            def _(act):
                def square(n):
                    act.wait_ge(xc_done, n + 1)
                    nc.scalar.activation(sq[:], xc[:], ACT.Square).then_inc(sq_done, 1)

                def inv_std(n):
                    act.wait_ge(var_done, n + 1)
                    nc.scalar.activation(lnv[:], psM[:, 0, :], ACT.Ln, bias=S.eps[:, 0:1]).then_inc(lnv_done, 1)
                    act.wait_ge(lnv_done, n + 1)
                    nc.scalar.activation(rstd[:], lnv[:], ACT.Exp, scale=-0.5).then_inc(rstd_done, 1)

                def high_h(n, par):
                    act.wait_ge(h_done, n + 1)
                    nc.scalar.copy(Hh[:, par, :], H[:, par, :]).then_inc(hh_done, 1)

                def probabilities(n):
                    act.wait_ge(lg_done, n + 1)
                    nc.scalar.activation(pr[:], lg[:], ACT.Sigmoid).then_inc(pr_done, 1)

                def weights_copy(n, par):
                    act.wait_ge(wtp_done, n + 1)
                    nc.scalar.copy(wT[:, par, :], psM[0:2 * NALL, 0, :]).then_inc(wt_done, 1)

                def silu(n, par, k):
                    u = par * UNITS + k
                    act.wait_ge(gu_done, n * UNITS + (k + 1))
                    nc.scalar.activation(sg[:, u % 2, :], psG[:, u % 2, :], ACT.Silu).then_inc(silu_done, 1)
                    if k % 2 == 0:
                        e = k // 2
                        act.wait_ge(wb_done, n * NALL + (e + 1))
                        act.wait_ge(tw_done, n * UNITS + (2 * e - 2 + TW0))
                        nc.scalar.copy(wbs[:, (par * NALL + e) % 2, :], psW[:, 0, :]).then_inc(wbs_done, 1)

                square(0)
                inv_std(0)
                high_h(0, 0)
                probabilities(0)
                weights_copy(0, 0)
                for k in range(LEAD):
                    silu(0, 0, k)
                with nc.scalar.Fori(0, NT // 2) as j:
                    for par in range(2):
                        n = j * 2 + par
                        for k in range(UNITS):
                            on, upar, uk = ahead(par, k, LEAD)
                            silu(n + on, upar, uk)
                            if k == 2:
                                square(n + 1)
                            if k == 4:
                                inv_std(n + 1)
                            if k == 6:
                                high_h(n + 1, 1 - par)
                            if k == 8:
                                probabilities(n + 1)
                            if k == 13:
                                weights_copy(n + 1, 1 - par)

            @block.gpsimd
            def _(pool):
                def weigh(n, par, k):
                    u = par * UNITS + k
                    e = k // 2
                    pool.wait_ge(t_done, n * UNITS + (k + 1))
                    pool.wait_ge(wbs_done, n * NALL + (e + 1))
                    pool.wait_ge(down_done, n * UNITS + (k - 3 + DN0))
                    nc.gpsimd.tensor_tensor(tw[:, u % 4, :], tt[:, u % 2, :], wbs[:, (par * NALL + e) % 2, :],
                                            ALU.mult).then_inc(tw_done, 1)

                nc.gpsimd.memset(S.spare[:, 3:4], 0.0).then_inc(tw_done, TW0)
                for k in range(2):
                    weigh(0, 0, k)
                with nc.gpsimd.Fori(0, NT // 2) as j:
                    for par in range(2):
                        n = j * 2 + par
                        for k in range(UNITS):
                            on, upar, uk = ahead(par, k, 2)
                            weigh(n + on, upar, uk)

            @block.vector
            def _(dve):
                def center(n):
                    dve.wait_ge(mean_done, n + 1)
                    nc.vector.tensor_tensor(xc[:], S.X[:, ds(n * MT, MT)], psM[:, 0, :], ALU.subtract
                                            ).then_inc(xc_done, 1)

                def normalize(n, par):
                    dve.wait_ge(rstd_done, n + 1)
                    nc.vector.tensor_tensor(xc[:], xc[:], rstd[:], ALU.mult).then_inc(xn_done, 1)
                    dve.wait_ge(xn_done, n + 1)
                    for s in range(SPT):
                        cols = slice(s * SEQ, (s + 1) * SEQ)
                        last = nc.vector.tensor_scalar(H[:, par, cols], xc[:, cols], mod[:, SC_B, ds(n * SPT + s, 1)],
                                                       mod[:, SH_B, ds(n * SPT + s, 1)], ALU.mult, ALU.add)
                    last.then_inc(h_done, 1)

                def low_h(n, par):
                    dve.wait_ge(hh_done, n + 1)
                    nc.vector.tensor_tensor(Hl[:, par, :], H[:, par, :], Hh[:, par, :], ALU.subtract
                                            ).then_inc(hl_done, 1)

                def add_bias(n):
                    dve.wait_ge(lgp_done, n + 1)
                    nc.vector.tensor_tensor(lg[:], psM[:, 0, 0:SUB * NEXP].rearrange("p (s e) -> p s e", s=SUB),
                                            bias[:], ALU.add).then_inc(lg_done, 1)

                def choose(n):
                    dve.wait_ge(pr_done, n + 1)
                    step = [0]

                    def after(ins):
                        step[0] += 1
                        ins.then_inc(route, 1)
                        dve.wait_ge(route, n * ROUTE + step[0])

                    big = [P, SUB, NEXP, NEXP]
                    other = pr[:].unsqueeze(2).broadcast_to(big)
                    own = pr[:].unsqueeze(3).broadcast_to(big)
                    nc.vector.tensor_tensor(beats[:], other, own, ALU.is_gt)
                    after(nc.vector.tensor_tensor(ties[:], other, own, ALU.is_equal))
                    after(nc.vector.tensor_tensor(ties[:], ties[:], tri[:].unsqueeze(1).broadcast_to(big), ALU.mult))
                    after(nc.vector.tensor_tensor(beats[:], beats[:], ties[:], ALU.add))
                    after(nc.vector.tensor_reduce(rank[:], beats[:], AX, ALU.add))
                    after(nc.vector.scalar_tensor_tensor(pick[:], rank[:], 1.5, pr[:], ALU.is_lt, ALU.mult))
                    after(nc.vector.tensor_reduce(psum2[:], pick[:], AX, ALU.add))
                    after(nc.vector.reciprocal(psum2[:], psum2[:]))
                    after(nc.vector.tensor_tensor(wt[:], pick[:], psum2[:].unsqueeze(2).broadcast_to([P, SUB, NEXP]),
                                                  ALU.mult))
                    assert step[0] == ROUTE
                    split(n)

                def split(n):
                    nc.vector.tensor_copy(whl[:, :, 0, 0:NEXP].bitcast(F32R), wt[:]).then_inc(wh_done, 1)
                    dve.wait_ge(wh_done, n + 1)
                    nc.vector.tensor_tensor(whl[:, :, 1, 0:NEXP], wt[:], whl[:, :, 0, 0:NEXP], ALU.subtract
                                            ).then_inc(whl_done, 1)

                def gate_up(n, par, k):
                    u = par * UNITS + k
                    dve.wait_ge(silu_done, n * UNITS + (k + 1))
                    dve.wait_ge(tw_done, n * UNITS + (k - 1 + TW0))
                    nc.vector.tensor_tensor(tt[:, u % 2, :], sg[:, u % 2, :], psU[:, u % 2, :], ALU.mult
                                            ).then_inc(t_done, 1)

                def residual(n, par):
                    dve.wait_ge(down_done, n * UNITS + (UNITS + DN0))
                    for s in range(SPT):
                        x = S.X[:, ds((n * SPT + s) * SEQ, SEQ)]
                        last = nc.vector.scalar_tensor_tensor(x, psY[:, par, s * SEQ:(s + 1) * SEQ],
                                                              mod[:, GB, ds(n * SPT + s, 1)], x, ALU.mult, ALU.add)
                    last.then_inc(x_done, 1)

                nc.vector.memset(S.spare[:, 1:2], 0.0).then_inc(down_done, DN0)
                nc.vector.memset(S.spare[:, 2:3], 0.0).then_inc(x_done, X0)
                center(0)
                normalize(0, 0)
                low_h(0, 0)
                add_bias(0)
                choose(0)
                for k in range(2):
                    gate_up(0, 0, k)
                with nc.vector.Fori(0, NT // 2) as j:
                    for par in range(2):
                        n = j * 2 + par
                        for k in range(UNITS):
                            on, upar, uk = ahead(par, k, 2)
                            gate_up(n + on, upar, uk)
                            if k == 2:
                                center(n + 1)
                            if k == 5:
                                normalize(n + 1, 1 - par)
                            if k == 7:
                                low_h(n + 1, 1 - par)
                                add_bias(n + 1)
                            if k == 10:
                                choose(n + 1)
                        residual(n, par)


ROW = SEQ + 1
SMALL_E = 0.03
SMALL = 1e-5
ADEEP = 8

L_DECAY, L_SCAN, L_TIMES, L_SPREAD, L_SUM = 8, 6, 5, 6, 4


def mamba(nc, w, S):
    with ExitStack() as ctx:
        def sb(name, shape, dt=F32):
            return ctx.enter_context(nc.sbuf_tensor(name, shape, dt))

        def pb(name, n):
            return ctx.enter_context(nc.psum_tensor(name, [P, n, 512], F32))

        wz = sb("wz", [P, P])
        wdd = sb("wdd", [P, RDT])
        wc = sb("wc", [P, 4, NST])
        wdt = sb("wdt", [RDT, P])
        wout = sb("wout_s", [P, P])
        conv = sb("conv", [P, TAPS])
        bdt = sb("bdt", [P, 1])
        dskip = sb("dskip", [P, 1])
        negA = sb("negA", [P, NST])
        is_small = sb("is_small", [P, NST])
        is_large = sb("is_large", [P, NST])
        cst = sb("cst", [P, NST])
        diag = sb("diag", [P, NST, P])
        csT = [sb(f"csT{i}", [4 * NST, P], F32R) for i in range(2)]
        sel = sb("sel_s", [4 * NST, NST, P], F32R)
        any_small = sb("any_small", [P, 1], mybir.dt.int32)

        xn = sb("xn_s", [P, MT])
        sq = sb("sq_s", [P, MT])
        lnv = sb("lnv_s", [P, MT])
        rstd = sb("rstd_s", [P, MT])
        H = sb("H_s", [P, SPT, TAPS - 1 + SEQ])
        acc = sb("acc_s", [P, 2, SPT, SEQ])
        U = sb("U_s", [P, 2, SPT, SEQ])
        sz = sb("sz_s", [P, 2, MT])
        dtx = sb("dtx", [P, 2, SPT, ROW + 1])
        dd = sb("dd", [P, 3, SPT * ROW])
        wx = sb("wx", [P, SPT, ROW])
        part = sb("part_s", [P, SPT * ROW])
        Ch = sb("Ch", [4 * NST, 2, MT], F32R)
        dtu = sb("dtu", [RDT, MT])
        A = sb("A_s", [P, ADEEP, SPT, ROW])
        K = sb("K_s", [P, 4, SPT, ROW])
        M = sb("M_s", [P, 4, MT])
        ex = sb("ex", [P, MT])
        rx = sb("rx", [P, MT])
        big = sb("big", [P, MT])
        tiny = sb("tiny", [P, MT])
        one = sb("one", [P, 1])
        coef = sb("coef", [P, 4])
        gd = sb("gd", [P, MT])
        gu = sb("gu", [P, MT])
        ys = sb("ys", [P, MT])
        yo = sb("yo", [P, MT])

        psX, psM, psZ, psC, psY, psG = (pb("psX_s", 1), pb("psM_s", 1), pb("psZ_s", 1), pb("psC_s", 2),
                                        pb("psY_s", 2), pb("psG_s", 1))

        with ExitStack() as pre:
            sem = lambda n: pre.enter_context(nc.semaphore(n))
            loaded, expd, vstep, made, filled = map(sem, ["s_loaded", "s_expd", "s_vstep", "s_made", "s_filled"])
            alog = pre.enter_context(nc.sbuf_tensor("alog", [P, NST], F32))
            ea = pre.enter_context(nc.sbuf_tensor("ea", [P, NST], F32))
            den = pre.enter_context(nc.sbuf_tensor("den_s", [P, NST], F32))
            cs4 = pre.enter_context(nc.sbuf_tensor("cs4", [P, 4, NST], F32))
            sel0 = pre.enter_context(nc.sbuf_tensor("sel0_s", [4 * NST, NST, P], F32))
            onesq = pre.enter_context(nc.sbuf_tensor("onesq", [P, P], F32))
            some = pre.enter_context(nc.sbuf_tensor("some", [P, 1], F32))
            with nc.Block() as block:

                @block.sync
                def _(sp):
                    sp.wait_ge(filled, 1)
                    for t, src in ((wz[:], w["wz"]), (wdd[:], w["wpar"][:, 0:RDT]),
                                   (wc[:, 0, :], w["wpar"][:, RDT + NST:RDT + 2 * NST]),
                                   (wc[:, 2, :], w["wpar"][:, RDT + NST:RDT + 2 * NST]),
                                   (wdt[:], w["wdt"]), (wout[:], w["wout"]), (conv[:], w["conv"]),
                                   (bdt[:], w["bdt"]), (dskip[:], w["dskip"]), (alog[:], w["alog"])):
                        sp.dma_start(t, src).then_inc(loaded, 16)
                    sp.wait_ge(loaded, 160)

                @block.gpsimd
                def _(pool):
                    nc.gpsimd.memset(wc[:], 0.0).then_inc(filled, 1)
                    nc.gpsimd.memset(onesq[:], 1.0)
                    nc.gpsimd.memset(one[:], 1.0)
                    for i, c in enumerate((-1 / 4, 1 / 3, -1 / 2, 1.0)):
                        nc.gpsimd.memset(coef[:, i:i + 1], c)
                    nc.gpsimd.memset(cs4[:], 0.0)
                    nc.gpsimd.memset(H[:, :, 0:TAPS - 1], 0.0)
                    nc.gpsimd.memset(wx[:, :, 0:1], 0.0)
                    nc.gpsimd.memset(A[:, :, :, 0:1], 0.0)
                    for par in range(2):
                        nc.gpsimd.memset(dd[:, par, :].rearrange("p (s t) -> p s t", s=SPT)[:, :, 1:2], 0.0)
                    nc.gpsimd.memset(sel0[:], 0.0).then_inc(filled, 1)
                    pool.wait_ge(filled, 2)
                    nc.gpsimd.affine_select(out=sel0[:], in_=sel0[:], compare_op=ALU.not_equal, fill=1.0, base=0,
                                            pattern=[[-1, NST], [0, P]], channel_multiplier=1).then_inc(filled, 1)
                    pool.wait_ge(filled, 3)
                    nc.gpsimd.affine_select(out=sel0[:], in_=sel0[:], compare_op=ALU.not_equal, fill=1.0,
                                            base=-2 * NST, pattern=[[-1, NST], [0, P]], channel_multiplier=1
                                            ).then_inc(filled, 1)

                @block.scalar
                def _(act):
                    act.wait_ge(loaded, 160)
                    nc.scalar.activation(ea[:], alog[:], ACT.Exp).then_inc(expd, 1)

                @block.vector
                def _(dve):
                    n = [0]

                    def after(ins):
                        n[0] += 1
                        ins.then_inc(vstep, 1)
                        dve.wait_ge(vstep, n[0])

                    dve.wait_ge(expd, 1)
                    dve.wait_ge(filled, 4)
                    nc.vector.tensor_scalar(negA[:], ea[:], -1.0, None, ALU.mult)
                    nc.vector.tensor_scalar(is_small[:], ea[:], SMALL, None, ALU.is_lt)
                    after(nc.vector.tensor_scalar(is_large[:], ea[:], SMALL, None, ALU.is_ge))
                    after(nc.vector.scalar_tensor_tensor(den[:], negA[:], 1e-10, is_large[:], ALU.add, ALU.mult))
                    after(nc.vector.tensor_tensor(den[:], den[:], is_small[:], ALU.add))
                    after(nc.vector.reciprocal(cst[:], den[:]))
                    for r in (0, 2):
                        nc.vector.tensor_tensor(cs4[:, r, :], cst[:], is_large[:], ALU.mult)
                    for k in range(NST):
                        last = nc.vector.tensor_scalar(diag[:, k, :], S.ident[:], cst[:, k:k + 1], None, ALU.mult)
                    after(last)
                    nc.vector.tensor_copy(sel[:], sel0[:])
                    dve.wait_ge(made, 1)
                    after(nc.vector.tensor_copy(csT[0][:], psM[0:4 * NST, 0, 0:P]))
                    nc.vector.tensor_tensor(csT[1][:], psM[0:4 * NST, 0, 0:P], csT[0][:], ALU.subtract)
                    after(nc.vector.tensor_reduce(some[:], psZ[:, 0, 0:NST], AX, ALU.max))
                    after(nc.vector.tensor_scalar(any_small[:], some[:], 0.5, None, ALU.is_gt))

                @block.tensor
                def _(pe):
                    pe.wait_ge(vstep, 5)
                    nc.tensor.transpose(psM[0:4 * NST, 0, 0:P], cs4[:].rearrange("p r n -> p (r n)"), S.ident[:])
                    nc.tensor.matmul(psZ[:, 0, 0:NST], onesq[:], is_small[:], start=True, stop=True).then_inc(made, 1)

        names = ["xc_done", "sq_done", "var_done", "lnv_done", "rstd_done", "xn_done", "h_done",
                 "z_done", "c_done", "chi_done", "clo_done", "dtu_done", "dtuc_done", "dt_done", "ax_done",
                 "tap0_done", "conv_step", "conv_done", "sz_done", "u_done", "e_done", "big_done", "x_read", "series",
                 "blend_done", "dtx_done", "dd_done", "w_done", "a_done", "cb_done", "k_done", "m_done", "acc_done",
                 "g_done", "gd_done", "gu_done", "ys_done", "yo_done", "o_done", "x_done", "small_step"]
        (xc_done, sq_done, var_done, lnv_done, rstd_done, xn_done, h_done,
         z_done, c_done, chi_done, clo_done, dtu_done, dtuc_done, dt_done, ax_done,
         tap0_done, conv_step, conv_done, sz_done, u_done, e_done, big_done, x_read, series,
         blend_done, dtx_done, dd_done, w_done, a_done, cb_done, k_done, m_done, acc_done,
         g_done, gd_done, gu_done, ys_done, yo_done, o_done, x_done, small_step) = [
             ctx.enter_context(nc.semaphore("s_" + n)) for n in names]
        K0, M0, AC0, X0, YS0 = ADEEP, 4, 4, 1, 2
        SERIES = 9
        mod = S.mod[1]

        def ahead(n, par, k):
            return (n, par, k) if k < NST else (n + 1, 1 - par, k - NST)

        with nc.Block() as block:

            @block.tensor
            def _(pe):
                def centered(t):
                    nc.tensor.matmul(psX[:, 0, :], S.center[:], S.X[:, ds(t * MT, MT)],
                                     start=True, stop=True).then_inc(xc_done, 1)

                def var(t, first=False):
                    pe.wait_ge(sq_done, t + 1)
                    if not first:
                        pe.wait_ge(x_read, t)
                    nc.tensor.matmul(psM[:, 0, :], S.meanw[:], sq[:], start=True, stop=True).then_inc(var_done, 1)

                h = H[:, :, TAPS - 1:]

                def c_product(t):
                    pe.wait_ge(h_done, t + 1)
                    nc.tensor.matmul(psM[0:4 * NST, 0, :], wc[:].rearrange("p r n -> p (r n)"), h,
                                     start=True, stop=True).then_inc(c_done, 1)

                def z_product(t, first=False):
                    if not first:
                        pe.wait_ge(sz_done, t)
                    nc.tensor.matmul(psZ[:, 0, :], wz[:], h, start=True, stop=True).then_inc(z_done, 1)

                def dt_down(t):
                    pe.wait_ge(clo_done, t + 1)
                    nc.tensor.matmul(psM[0:RDT, 0, :], wdd[:], h, start=True, stop=True).then_inc(dtu_done, 1)

                def dt_up(t):
                    pe.wait_ge(dtuc_done, t + 1)
                    nc.tensor.matmul(psM[:, 0, :], wdt[:], dtu[:], start=True, stop=True).then_inc(dt_done, 1)

                def spread_c(t, par, k):
                    pe.wait_ge(m_done, t * NST + (k - 1 + M0))
                    nc.tensor.matmul(psC[:, k % 2, :], sel[:, k, :], Ch[:, par, :], start=True, stop=True
                                     ).then_inc(cb_done, 1)

                def sum_c(n, par):
                    pe.wait_ge(x_done, n + X0)
                    nc.tensor.matmul(psG[:, 0, :], csT[0][:], Ch[:, par, :], start=True, stop=False)
                    nc.tensor.matmul(psG[:, 0, :], csT[1][:], Ch[:, par, :], start=False, stop=True
                                     ).then_inc(g_done, 1)

                def accumulate(t, par, k):
                    pe.wait_ge(m_done, t * NST + (k + 1 + M0))
                    if k == 0:
                        pe.wait_ge(ys_done, t - 1 + YS0)
                    nc.tensor.matmul(psY[:, par, :], diag[:, k, :], M[:, k % 4, :], start=(k == 0),
                                     stop=(k == NST - 1)).then_inc(acc_done, 1)

                def project(n):
                    pe.wait_ge(yo_done, n + 1)
                    nc.tensor.matmul(psG[:, 0, :], wout[:], yo[:], start=True, stop=True).then_inc(o_done, 1)

                for t in range(2):
                    centered(t)
                    var(t, first=(t == 0))
                    c_product(t)
                    dt_down(t)
                    dt_up(t)
                    if t == 0:
                        z_product(0, first=True)
                for k in range(L_SPREAD):
                    spread_c(0, 0, k)
                    if k >= L_SPREAD - L_SUM:
                        accumulate(0, 0, k - (L_SPREAD - L_SUM))
                with nc.tensor.Fori(0, NT // 2) as j:
                    for par in range(2):
                        n = j * 2 + par
                        for k in range(NST):
                            spread_c(*ahead(n, par, k + L_SPREAD))
                            accumulate(*ahead(n, par, k + L_SUM))
                            if k == 0:
                                z_product(n + 1)
                            if k == 2:
                                sum_c(n, par)
                            if k == 3:
                                centered(n + 2)
                            if k == 5:
                                var(n + 2)
                            if k == 10:
                                c_product(n + 2)
                            if k == 12:
                                dt_down(n + 2)
                            if k == 13:
                                dt_up(n + 2)
                            if k == 14:
                                project(n)
                nc.tensor.matmul(psY[:, NT % 2, :], diag[:, 0, :], diag[:, 0:MT // P, :], start=False, stop=True)

            @block.scalar
            def _(act):
                def square(t):
                    act.wait_ge(xc_done, t + 1)
                    nc.scalar.activation(sq[:], psX[:, 0, :], ACT.Square).then_inc(sq_done, 1)

                def inv_std(t):
                    act.wait_ge(var_done, t + 1)
                    nc.scalar.activation(lnv[:], psM[:, 0, :], ACT.Ln, bias=S.eps[:, 0:1]).then_inc(lnv_done, 1)
                    act.wait_ge(lnv_done, t + 1)
                    nc.scalar.activation(rstd[:], lnv[:], ACT.Exp, scale=-0.5).then_inc(rstd_done, 1)

                def c_high(t, par):
                    act.wait_ge(c_done, t + 1)
                    nc.scalar.copy(Ch[:, par, :], psM[0:4 * NST, 0, :]).then_inc(chi_done, 1)

                def dt_copy(t):
                    act.wait_ge(dtu_done, t + 1)
                    nc.scalar.copy(dtu[:], psM[0:RDT, 0, :]).then_inc(dtuc_done, 1)

                def softplus_parts(t):
                    act.wait_ge(dt_done, t + 1)
                    nc.scalar.activation(ex[:], psM[:, 0, :], ACT.Abs, bias=bdt[:, 0:1]).then_inc(ax_done, 1)
                    nc.scalar.activation(rx[:], psM[:, 0, :], ACT.Relu, bias=bdt[:, 0:1]).then_inc(x_read, 1)

                def softplus_log(t):
                    act.wait_ge(ax_done, t + 1)
                    nc.scalar.activation(ex[:], ex[:], ACT.Exp, scale=-1.0).then_inc(e_done, 1)
                    act.wait_ge(e_done, t + 1)
                    nc.scalar.activation(big[:], ex[:], ACT.Ln, bias=one[:, 0:1]).then_inc(big_done, 1)

                def first_tap(t):
                    act.wait_ge(h_done, t + 1)
                    nc.scalar.activation(acc[:, 0, :, :], H[:, :, TAPS - 1:], ACT.Identity,
                                         scale=conv[:, TAPS - 1:TAPS]).then_inc(tap0_done, 1)

                def activations(t, par):
                    act.wait_ge(z_done, t + 1)
                    nc.scalar.activation(sz[:, par, :], psZ[:, 0, :], ACT.Silu).then_inc(sz_done, 1)
                    act.wait_ge(conv_done, t + 1)
                    nc.scalar.activation(U[:, par, :, :], acc[:, 1, :, :], ACT.Silu).then_inc(u_done, 1)
                    nc.scalar.preload_act_table_set("natural_log_exp_and_others")

                def decay(t, par, k):
                    if k == 0:
                        act.wait_ge(dtx_done, t + 1)
                    act.wait_ge(k_done, t * NST + (k + 1 - ADEEP + K0))
                    nc.scalar.activation(A[:, k % ADEEP, :, 1:ROW], dtx[:, par, :, 1:ROW], ACT.Exp,
                                         scale=negA[:, k:k + 1]).then_inc(a_done, 1)

                nc.scalar.preload_act_table_set("natural_log_exp_and_others")
                for t in range(2):
                    square(t)
                    inv_std(t)
                    c_high(t, t)
                    dt_copy(t)
                    if t == 1:
                        act.wait_ge(dtx_done, 1)
                    softplus_parts(t)
                    softplus_log(t)
                    first_tap(t)
                    if t == 0:
                        activations(0, 0)
                for k in range(L_DECAY):
                    decay(0, 0, k)
                with nc.scalar.Fori(0, NT // 2) as j:
                    for par in range(2):
                        n = j * 2 + par
                        for k in range(NST):
                            decay(*ahead(n, par, k + L_DECAY))
                            if k == 4:
                                square(n + 2)
                                activations(n + 1, 1 - par)
                            if k == 6:
                                inv_std(n + 2)
                            if k == 11:
                                c_high(n + 2, par)
                            if k == 13:
                                dt_copy(n + 2)
                            if k == 14:
                                softplus_parts(n + 2)
                            if k == 15:
                                softplus_log(n + 2)
                                first_tap(n + 2)

            @block.gpsimd
            def _(pool):
                def inputs(t, par):
                    pool.wait_ge(u_done, t + 1)
                    d = dd[:, par, :].rearrange("p (s t) -> p s t", s=SPT)
                    nc.gpsimd.tensor_tensor(d[:, :, 2:ROW], U[:, par, :, 1:SEQ], U[:, par, :, 0:SEQ - 1],
                                            ALU.subtract)
                    nc.gpsimd.tensor_copy(d[:, :, 0:1], U[:, par, :, 0:1]).then_inc(dd_done, 1)

                def small_log(t):
                    pool.wait_ge(e_done, t + 1)
                    coefs = [coef[:, i:i + 1].broadcast_to([P, MT]) for i in range(4)]
                    nc.gpsimd.tensor_tensor(tiny[:], ex[:], coefs[0], ALU.mult).then_inc(series, 1)
                    for i in range(3):
                        pool.wait_ge(series, t * SERIES + (2 * i + 1))
                        nc.gpsimd.tensor_tensor(tiny[:], tiny[:], coefs[i + 1], ALU.add).then_inc(series, 1)
                        pool.wait_ge(series, t * SERIES + (2 * i + 2))
                        nc.gpsimd.tensor_tensor(tiny[:], tiny[:], ex[:], ALU.mult).then_inc(series, 1)
                    pool.wait_ge(series, t * SERIES + 7)
                    pool.wait_ge(big_done, t + 1)
                    nc.gpsimd.tensor_tensor(big[:], big[:], tiny[:], ALU.subtract).then_inc(series, 1)
                    pool.wait_ge(x_read, t + 1)
                    nc.gpsimd.tensor_tensor(rx[:], rx[:], tiny[:], ALU.add).then_inc(series, 1)

                def dt_out(t, par):
                    pool.wait_ge(blend_done, t + 1)
                    s3 = lambda a: a[:].rearrange("p (s t) -> p s t", s=SPT)
                    nc.gpsimd.tensor_tensor(dtx[:, par, :, 2:2 + SEQ], s3(rx), s3(big), ALU.add)
                    nc.gpsimd.tensor_tensor(dtx[:, par, :, 1:2], s3(rx)[:, :, 0:1], s3(big)[:, :, 0:1], ALU.add
                                            ).then_inc(dtx_done, 1)

                def skip_part(n, par):
                    pool.wait_ge(gd_done, n + 1)
                    nc.gpsimd.tensor_tensor(gu[:], gd[:], U[:, par, :, :].rearrange("p s t -> p (s t)"), ALU.mult
                                            ).then_inc(gu_done, 1)

                small_log(0)
                dt_out(0, 0)
                inputs(0, 0)
                with nc.gpsimd.Fori(0, NT // 2) as j:
                    for par in range(2):
                        n = j * 2 + par
                        small_log(n + 1)
                        dt_out(n + 1, 1 - par)
                        inputs(n + 1, 1 - par)
                        skip_part(n, par)

            @block.vector
            def _(dve):
                small = nc.vector.value_load(any_small[0:1, 0:1], min_val=0, max_val=1)

                def normalize(t):
                    dve.wait_ge(rstd_done, t + 1)
                    nc.vector.tensor_tensor(xn[:], psX[:, 0, :], rstd[:], ALU.mult).then_inc(xn_done, 1)

                def modulate(t, first=False):
                    dve.wait_ge(xn_done, t + 1)
                    if not first:
                        dve.wait_ge(z_done, t)
                        dve.wait_ge(tap0_done, t)
                    for s in range(SPT):
                        last = nc.vector.tensor_scalar(H[:, s, TAPS - 1:], xn[:, s * SEQ:(s + 1) * SEQ],
                                                       mod[:, SC_A, ds(t * SPT + s, 1)],
                                                       mod[:, SH_A, ds(t * SPT + s, 1)], ALU.mult, ALU.add)
                    last.then_inc(h_done, 1)

                def c_low(t, par):
                    dve.wait_ge(chi_done, t + 1)
                    rows = slice(2 * NST, 4 * NST)
                    nc.vector.tensor_tensor(Ch[rows, par, :], psM[rows, 0, :], Ch[rows, par, :], ALU.subtract
                                            ).then_inc(clo_done, 1)

                def blend(t):
                    dve.wait_ge(series, t * SERIES + SERIES)
                    nc.vector.scalar_tensor_tensor(big[:], ex[:], SMALL_E, big[:], ALU.is_gt, ALU.mult
                                                   ).then_inc(blend_done, 1)

                def convolve(t, i):
                    if i == 1:
                        dve.wait_ge(tap0_done, t + 1)
                    else:
                        dve.wait_ge(conv_step, t * (TAPS - 2) + (i - 1))
                    at = TAPS - 1 - i
                    nc.vector.scalar_tensor_tensor(acc[:, i % 2, :, :], H[:, :, at:at + SEQ], conv[:, at:at + 1],
                                                   acc[:, 1 - i % 2, :, :], ALU.mult, ALU.add
                                                   ).then_inc(conv_done if i == TAPS - 1 else conv_step, 1)

                def scan(n, par, k):
                    with nc.vector.If(small):
                        if k == 0:
                            dve.wait_ge(dd_done, n + 1)
                            dve.wait_ge(dtx_done, n + 1)
                            nc.vector.tensor_tensor(wx[:, :, 2:ROW], dtx[:, par, :, 2:ROW], U[:, par, :, 0:SEQ - 1],
                                                    ALU.mult)
                            nc.vector.tensor_tensor(wx[:, :, 1:2], dtx[:, par, :, 1:2], U[:, par, :, 0:1], ALU.mult
                                                    ).then_inc(w_done, 1)
                            dve.wait_ge(w_done, n + 1)
                        dve.wait_ge(k_done, n * NST + (k + K0))
                        nc.vector.tensor_scalar(part[:], dd[:, par, :], is_large[:, k:k + 1], None, ALU.mult
                                                ).then_inc(small_step, 1)
                        dve.wait_ge(small_step, n * 2 * NST + (2 * k + 1))
                        nc.vector.scalar_tensor_tensor(dd[:, 2, :], wx[:].rearrange("p s t -> p (s t)"),
                                                       is_small[:, k:k + 1], part[:], ALU.mult, ALU.add
                                                       ).then_inc(small_step, 1)
                        dve.wait_ge(small_step, n * 2 * NST + (2 * k + 2))
                        nc.vector.memset(S.spare[:, 6:7], 0.0)
                    dve.wait_ge(a_done, n * NST + (k + 1))
                    if k == 0:
                        dve.wait_ge(dd_done, n + 1)
                    dve.wait_ge(m_done, n * NST + (k - 3 + M0))
                    at = small * ((2 - par) * SPT * ROW) + par * SPT * ROW
                    nc.vector.tensor_tensor_scan(K[:, k % 4, :, :].rearrange("p s t -> p (s t)"),
                                                 A[:, k % ADEEP, :, :].rearrange("p s t -> p (s t)"),
                                                 dd[:].rearrange("p i t -> p (i t)")[:, ds(at, SPT * ROW)],
                                                 0.0, ALU.mult, ALU.add).then_inc(k_done, 1)

                def times_c(n, par, k):
                    dve.wait_ge(cb_done, n * NST + (k + 1))
                    dve.wait_ge(k_done, n * NST + (k + 1 + K0))
                    dve.wait_ge(acc_done, n * NST + (k - 3 + AC0))
                    nc.vector.tensor_tensor(M[:, k % 4, :].rearrange("p (s t) -> p s t", s=SPT), K[:, k % 4, :, 1:ROW],
                                            psC[:, k % 2, :].rearrange("p (s t) -> p s t", s=SPT), ALU.mult
                                            ).then_inc(m_done, 1)

                def gate_off(n):
                    dve.wait_ge(g_done, n + 1)
                    nc.vector.tensor_scalar(gd[:], psG[:, 0, :], -1.0, dskip[:, 0:1], ALU.mult, ALU.add
                                            ).then_inc(gd_done, 1)

                def sum_y(n, par):
                    dve.wait_ge(acc_done, n * NST + (NST + AC0))
                    dve.wait_ge(gu_done, n + 1)
                    nc.vector.tensor_tensor(ys[:], psY[:, par, :], gu[:], ALU.add).then_inc(ys_done, 1)

                def gate_y(n, par):
                    dve.wait_ge(ys_done, n + 1 + YS0)
                    nc.vector.tensor_tensor(yo[:], ys[:], sz[:, par, :], ALU.mult).then_inc(yo_done, 1)

                def residual(n):
                    dve.wait_ge(o_done, n + 1)
                    for s in range(SPT):
                        x = S.X[:, ds((n * SPT + s) * SEQ, SEQ)]
                        last = nc.vector.scalar_tensor_tensor(x, psG[:, 0, s * SEQ:(s + 1) * SEQ],
                                                              mod[:, GA, ds(n * SPT + s, 1)], x, ALU.mult, ALU.add)
                    last.then_inc(x_done, 1)

                for i, (sem, count) in enumerate(((k_done, K0), (m_done, M0), (acc_done, AC0), (x_done, X0),
                                                  (ys_done, YS0))):
                    nc.vector.memset(S.spare[:, i:i + 1], 0.0).then_inc(sem, count)
                normalize(0)
                modulate(0, first=True)
                c_low(0, 0)
                for i in range(1, TAPS):
                    convolve(0, i)
                blend(0)
                normalize(1)
                modulate(1)
                c_low(1, 1)
                for k in range(L_SCAN):
                    scan(0, 0, k)
                    if k >= L_SCAN - L_TIMES:
                        times_c(0, 0, k - (L_SCAN - L_TIMES))
                with nc.vector.Fori(0, NT // 2) as j:
                    for par in range(2):
                        n = j * 2 + par
                        for k in range(NST):
                            scan(*ahead(n, par, k + L_SCAN))
                            times_c(*ahead(n, par, k + L_TIMES))
                            if k < TAPS - 1:
                                convolve(n + 1, k + 1)
                            if k == 3:
                                gate_off(n)
                            if k == 7:
                                blend(n + 1)
                            if k == 8:
                                normalize(n + 2)
                            if k == 9:
                                modulate(n + 2)
                            if k == 11:
                                c_low(n + 2, par)
                            if k == 12:
                                sum_y(n, par)
                            if k == 13:
                                gate_y(n, par)
                            if k == 15:
                                residual(n)


def rwkv(nc, w, S):
    with ExitStack() as ctx:
        def sb(name, shape, dt=F32):
            return ctx.enter_context(nc.sbuf_tensor(name, shape, dt))

        def pb(name, n):
            return ctx.enter_context(nc.psum_tensor(name, [P, n, 512], F32))

        wr, wk, wv = sb("wr_r", [P, P]), sb("wk_r", [P, P]), sb("wv_r", [P, P])
        mu = sb("mu", [P, 2])
        nmu = sb("nmu", [P, 2])
        one = sb("one_r", [P, 1])
        sq = sb("sq_r", [P, MT])
        lnv = sb("lnv_r", [P, MT])
        rstd = sb("rstd_r", [P, MT])
        xn = sb("xn_r", [P, MT])
        H = sb("H_r", [P, SPT, 1 + SEQ])
        old = sb("old_r", [P, 2, SPT, SEQ])
        mix = sb("mix_r", [P, 2, SPT, SEQ])
        az = sb("az_r", [P, MT])
        ez = sb("ez_r", [P, MT])
        lz = sb("lz_r", [P, MT])
        ls = sb("ls_r", [P, MT])
        rs = sb("rs_r", [P, MT])
        kr = sb("kr_r", [P, MT])
        ks = sb("ks_r", [P, MT])
        ov = sb("ov_r", [P, MT])
        psX, psM, psR, psK, psV = pb("psX_r", 2), pb("psM_r", 1), pb("psR_r", 2), pb("psK_r", 1), pb("psV_r", 1)

        with ExitStack() as pre:
            loaded = pre.enter_context(nc.semaphore("r_loaded"))
            with nc.Block() as block:

                @block.sync
                def _(sp):
                    for t, src in ((wr[:], "wr"), (wk[:], "wk"), (wv[:], "wv"), (mu[:, 0:1], "mur"), (mu[:, 1:2], "muk")):
                        sp.dma_start(t, w[src]).then_inc(loaded, 16)
                    sp.wait_ge(loaded, 80)

                @block.vector
                def _(dve):
                    nc.vector.memset(H[:, :, 0:1], 0.0)
                    nc.vector.memset(one[:], 1.0)
                    dve.wait_ge(loaded, 80)
                    nc.vector.tensor_scalar(nmu[:], mu[:], -1.0, 1.0, ALU.mult, ALU.add)

        names = ["xc_done", "sq_done", "var_done", "lnv_done", "rstd_done", "xn_done", "h_done", "old_done",
                 "mix_done", "r_done", "k_done", "az_done", "ez_done", "lz_done", "ls_done", "rs_done", "kr_done", "ks_done",
                 "v_done", "ov_done"]
        (xc_done, sq_done, var_done, lnv_done, rstd_done, xn_done, h_done, old_done, mix_done, r_done, k_done,
         az_done, ez_done, lz_done, ls_done, rs_done, kr_done, ks_done, v_done, ov_done) = [
             ctx.enter_context(nc.semaphore("r_" + n)) for n in names]
        XN0, LV0, MX0, LS0, KR0, KS0, V0, OV0 = 2, 1, 1, 2, 1, 1, 1, 1
        mod = S.mod[1]

        with nc.Block() as block:

            @block.tensor
            def _(pe):
                def centered(t, par):
                    pe.wait_ge(xn_done, t - 1 + XN0)
                    nc.tensor.matmul(psX[:, par, :], S.center[:], S.X[:, ds(t * MT, MT)],
                                     start=True, stop=True).then_inc(xc_done, 1)

                def var(t):
                    pe.wait_ge(sq_done, t + 1)
                    pe.wait_ge(lnv_done, t + LV0)
                    nc.tensor.matmul(psM[:, 0, :], S.meanw[:], sq[:], start=True, stop=True).then_inc(var_done, 1)

                def products(t, par):
                    pe.wait_ge(mix_done, t + 1 + MX0)
                    pe.wait_ge(ls_done, t - 1 + LS0)
                    nc.tensor.matmul(psR[:, par, :], wr[:], mix[:, 0, :, :], start=True, stop=True).then_inc(r_done, 1)
                    pe.wait_ge(kr_done, t + KR0)
                    nc.tensor.matmul(psK[:, 0, :], wk[:], mix[:, 1, :, :], start=True, stop=True).then_inc(k_done, 1)

                def value(t):
                    pe.wait_ge(ks_done, t + 1 + KS0)
                    pe.wait_ge(ov_done, t + OV0)
                    nc.tensor.matmul(psV[:, 0, :], wv[:], ks[:], start=True, stop=True).then_inc(v_done, 1)

                for t in range(3):
                    centered(t, t % 2)
                    var(t)
                    if t == 2:
                        products(0, 0)
                with nc.tensor.Fori(0, NT // 2) as j:
                    for par in range(2):
                        n = j * 2 + par
                        centered(n + 3, 1 - par)
                        products(n + 1, 1 - par)
                        value(n)
                        var(n + 3)

            @block.scalar
            def _(act):
                def square(t, par):
                    act.wait_ge(xc_done, t + 1)
                    nc.scalar.activation(sq[:], psX[:, par, :], ACT.Square).then_inc(sq_done, 1)

                def log_var(t):
                    act.wait_ge(var_done, t + 1)
                    nc.scalar.activation(lnv[:], psM[:, 0, :], ACT.Ln, bias=S.eps[:, 0:1]).then_inc(lnv_done, 1)

                def inv_std(t):
                    act.wait_ge(lnv_done, t + 1 + LV0)
                    nc.scalar.activation(rstd[:], lnv[:], ACT.Exp, scale=-0.5).then_inc(rstd_done, 1)

                def predecessor(t):
                    act.wait_ge(h_done, t + 1)
                    act.wait_ge(mix_done, t + MX0)
                    for i in range(2):
                        last = nc.scalar.activation(old[:, i, :, :], H[:, :, 0:SEQ], ACT.Identity,
                                                    scale=nmu[:, i:i + 1])
                    last.then_inc(old_done, 1)

                def magnitude(t, par):
                    act.wait_ge(r_done, t + 1)
                    nc.scalar.activation(az[:], psR[:, par, :], ACT.Abs).then_inc(az_done, 1)

                def relu(t):
                    act.wait_ge(k_done, t + 1)
                    act.wait_ge(ks_done, t + KS0)
                    nc.scalar.activation(kr[:], psK[:, 0, :], ACT.Relu).then_inc(kr_done, 1)

                def exp_z(t):
                    act.wait_ge(az_done, t + 1)
                    nc.scalar.activation(ez[:], az[:], ACT.Exp, scale=-1.0).then_inc(ez_done, 1)

                def log_z(t):
                    act.wait_ge(ez_done, t + 1)
                    nc.scalar.activation(lz[:], ez[:], ACT.Ln, bias=one[:, 0:1]).then_inc(lz_done, 1)

                def sigmoid(t):
                    act.wait_ge(ls_done, t + 1 + LS0)
                    act.wait_ge(ov_done, t + OV0)
                    nc.scalar.activation(rs[:], ls[:], ACT.Exp).then_inc(rs_done, 1)

                nc.scalar.preload_act_table_set("natural_log_exp_and_others")
                nc.scalar.copy(S.spare[:, 7:8], S.eps[:, 0:1]).then_inc(lnv_done, LV0)
                for t in range(2):
                    square(t, t)
                    log_var(t)
                    inv_std(t)
                    predecessor(t)
                    if t == 1:
                        square(2, 0)
                with nc.scalar.Fori(0, NT // 2) as j:
                    for par in range(2):
                        n = j * 2 + par
                        relu(n)
                        magnitude(n, par)
                        log_var(n + 2)
                        exp_z(n)
                        inv_std(n + 2)
                        log_z(n)
                        square(n + 3, 1 - par)
                        sigmoid(n)
                        predecessor(n + 2)

            @block.gpsimd
            def _(pool):
                def squares(t):
                    pool.wait_ge(kr_done, t + 1 + KR0)
                    pool.wait_ge(v_done, t + V0)
                    nc.gpsimd.tensor_tensor(ks[:], kr[:], kr[:], ALU.mult).then_inc(ks_done, 1)

                nc.gpsimd.memset(S.spare[:, 6:7], 0.0).then_inc(ks_done, KS0)
                nc.gpsimd.memset(S.spare[:, 5:6], 0.0).then_inc(v_done, V0)
                with nc.gpsimd.Fori(0, NT // 2) as j:
                    for par in range(2):
                        squares(j * 2 + par)

            @block.vector
            def _(dve):
                def normalize(t, par):
                    dve.wait_ge(rstd_done, t + 1)
                    nc.vector.tensor_tensor(xn[:], psX[:, par, :], rstd[:], ALU.mult).then_inc(xn_done, 1)

                def modulate(t):
                    dve.wait_ge(xn_done, t + 1 + XN0)
                    for s in range(SPT):
                        last = nc.vector.tensor_scalar(H[:, s, 1:], xn[:, s * SEQ:(s + 1) * SEQ],
                                                       mod[:, SC_B, ds(t * SPT + s, 1)],
                                                       mod[:, SH_B, ds(t * SPT + s, 1)], ALU.mult, ALU.add)
                    last.then_inc(h_done, 1)

                def mixes(t, first=False):
                    dve.wait_ge(old_done, t + 1)
                    if not first:
                        dve.wait_ge(k_done, t)
                    for i in range(2):
                        last = nc.vector.scalar_tensor_tensor(mix[:, i, :, :], H[:, :, 1:], mu[:, i:i + 1],
                                                              old[:, i, :, :], ALU.mult, ALU.add)
                    last.then_inc(mix_done, 1)

                def log_sigmoid(t, par):
                    dve.wait_ge(lz_done, t + 1)
                    nc.vector.scalar_tensor_tensor(ls[:], psR[:, par, :], 0.0, lz[:], ALU.min, ALU.subtract
                                                   ).then_inc(ls_done, 1)

                def gate_value(t):
                    dve.wait_ge(v_done, t + 1 + V0)
                    dve.wait_ge(rs_done, t + 1)
                    nc.vector.tensor_tensor(ov[:], rs[:], psV[:, 0, :], ALU.mult).then_inc(ov_done, 1)

                def residual(t):
                    dve.wait_ge(ov_done, t + 1 + OV0)
                    for s in range(SPT):
                        x = S.X[:, ds((t * SPT + s) * SEQ, SEQ)]
                        nc.vector.scalar_tensor_tensor(x, ov[:, s * SEQ:(s + 1) * SEQ],
                                                       mod[:, GB, ds(t * SPT + s, 1)], x, ALU.mult, ALU.add)

                for i, (sem, count) in enumerate(((xn_done, XN0), (mix_done, MX0), (ls_done, LS0), (kr_done, KR0),
                                                  (ov_done, OV0))):
                    nc.vector.memset(S.spare[:, i:i + 1], 0.0).then_inc(sem, count)
                normalize(0, 0)
                modulate(0)
                mixes(0, first=True)
                normalize(1, 1)
                modulate(1)
                with nc.vector.Fori(0, NT // 2) as j:
                    for par in range(2):
                        n = j * 2 + par
                        mixes(n + 1)
                        normalize(n + 2, par)
                        log_sigmoid(n, par)
                        modulate(n + 2)
                        gate_value(n)
                        residual(n)


STAGES = [attention, moe, mamba, rwkv]

def store(nc, out, S):
    with ExitStack() as ctx:
        stored = ctx.enter_context(nc.semaphore("stored"))
        with nc.Block() as block:

            @block.sync
            def _(sp):
                sp.dma_start(out, S.X[:, 0:TOK]).then_inc(stored, 16)
                sp.wait_ge(stored, 16)

def build(nc, w, out, stages):
    S = Shared()
    with ExitStack() as ctx:
        constants_and_modulation(nc, ctx, w, S)
        for stage in stages:
            stage(nc, w, S)
        store(nc, out, S)

def layouts(inputs):
    import numpy as np

    i = {k: np.asarray(v) for k, v in inputs.items()}
    t = lambda a, *o: np.ascontiguousarray(a.transpose(*o))

    down = lambda a: np.ascontiguousarray(np.moveaxis(np.swapaxes(a, -1, -2).reshape(a.shape[:-2] + (2, P, P)), -2, 0))
    arrays = {
        "x": t(i["L0_attn_x_bld"].reshape(TOK, P), 1, 0),
        "c0": t(i["L0_c"], 1, 0), "c1": t(i["L1_c"], 1, 0),
        "wmod0": i["L0_wmod"].reshape(P, 6, P), "wmod1": i["L1_wmod"].reshape(P, 6, P),
        "wqT": t(i["L0_attn_Wq"], 2, 1, 0), "wkuT": t(i["L0_attn_Wk_up"], 2, 1, 0),
        "wvuT": t(i["L0_attn_Wv_up"], 2, 1, 0), "wo": t(i["L0_attn_Wout"], 1, 0, 2),
        "wlat": i["L0_attn_Wkv_down"],
        "sg": t(i["L0_ffn_sg_w"], 1, 0), "su": t(i["L0_ffn_su_w"], 1, 0), "sd": down(i["L0_ffn_sd_w"]),
        "wg": t(i["L0_ffn_wg"], 2, 0, 1), "wu": t(i["L0_ffn_wu"], 2, 0, 1), "wd": down(i["L0_ffn_wd"]),
        "router": t(i["L0_ffn_router_w"], 1, 0), "rbias": i["L0_ffn_routing_bias"].reshape(1, NEXP),
        "wz": t(i["L1_attn_W_z"], 1, 0), "wpar": t(i["L1_attn_W_params"], 1, 0),
        "conv": i["L1_attn_conv_w"].reshape(P, TAPS), "wdt": t(i["L1_attn_W_dt"], 1, 0),
        "bdt": i["L1_attn_b_dt"].reshape(P, 1), "alog": i["L1_attn_A_log"], "dskip": i["L1_attn_D"].reshape(P, 1),
        "wout": t(i["L1_attn_W_out"], 1, 0),
        "wr": t(i["L1_ffn_W_r"], 1, 0), "wk": t(i["L1_ffn_W_k"], 1, 0), "wv": t(i["L1_ffn_W_v"], 1, 0),
        "mur": i["L1_ffn_mu_r"].reshape(P, 1), "muk": i["L1_ffn_mu_k"].reshape(P, 1),
    }
    return arrays

def kernel(**inputs):
    import numpy as np
    import concourse.bacc as bacc
    from concourse.bass_utils import run_bass_kernel_spmd

    nc = bacc.Bacc("TRN2", target_bir_lowering=False, num_devices=1)
    arrays = layouts(inputs)
    w = {k: nc.dram_tensor("in_" + k, a.shape, mybir.dt.from_np(a.dtype), kind="ExternalInput").ap()
         for k, a in arrays.items()}
    out = nc.dram_tensor("out", [P, TOK], F32, kind="ExternalOutput").ap()
    build(nc, w, out, [attention, moe, mamba, rwkv])
    r = run_bass_kernel_spmd(nc, [{"in_" + k: a for k, a in arrays.items()}], core_ids=[0])
    xT = r.results[0]["out"]
    return np.ascontiguousarray(xT.transpose(1, 0)).reshape(NSEQ, SEQ, P)
```

```python
from contextlib import ExitStack

import concourse.bass as bass
from concourse import mybir

P = 128
SEQ = 256
NSEQ = 32
TOK = NSEQ * SEQ
PAD = 6
HEADS = 16
LD = 32
HD = 64
PAIRS = HEADS // 2
GROUPS = HEADS // 4
NEXP = 8
NALL = NEXP + 1
NST = 16
RDT = 64
TAPS = 4
NEG = -1.0e30
EPS = 1e-5

F32 = mybir.dt.float32
F32R = mybir.dt.float32r
BF16 = mybir.dt.bfloat16
ACT = mybir.ActivationFunctionType
ALU = mybir.AluOpType
AX = mybir.AxisListType.X
ds = bass.ds

SH_A, SC_A, GA, SH_B, SC_B, GB = range(6)


class Shared:
    pass


def constants(nc, ctx, S):
    def sb(name, shape, dt=F32):
        return ctx.enter_context(nc.sbuf_tensor(name, shape, dt))

    S.mod = [sb("mod0", [P, 6, NSEQ + PAD]), sb("mod1", [P, 6, NSEQ + PAD])]
    S.meanw = sb("meanw", [P, P])
    S.center = sb("center", [P, P])
    S.ident = sb("ident", [P, P])
    S.identb = sb("identb", [P, P], BF16)
    S.eps = sb("eps", [P, 1])
    S.spare = sb("spare", [P, 8])


def constants_and_modulation(nc, w, S, loads):
    with ExitStack() as loc:
        def lsb(name, shape, dt=F32):
            return loc.enter_context(nc.sbuf_tensor(name, shape, dt))

        cT = [lsb("cT0", [P, NSEQ]), lsb("cT1", [P, NSEQ])]
        wmod = [lsb("wm0", [P, 6, P]), lsb("wm1", [P, 6, P])]
        sc = [lsb("siluc0", [P, NSEQ]), lsb("siluc1", [P, NSEQ])]
        gpos = lsb("gpos", [P, NSEQ])
        gneg = lsb("gneg", [P, NSEQ])
        ps = loc.enter_context(nc.psum_tensor("ps_mod", [P, 2, 512], F32))
        sem = lambda n: loc.enter_context(nc.semaphore(n))
        loaded, silu_done, mod_done, filled, gate_step = map(
            sem, ["loaded", "silu_done", "mod_done", "filled", "gate_step"])
        with nc.Block() as block:

            @block.sync
            def _(sp):
                for l in range(2):
                    sp.dma_start(cT[l][:], w[f"c{l}"]).then_inc(loaded, 16)
                    sp.dma_start(wmod[l][:], w[f"wmod{l}"]).then_inc(loaded, 16)
                for sem_loaded, dst, src in loads:
                    sp.dma_start(dst, src).then_inc(sem_loaded, 16)

            @block.scalar
            def _(act):
                act.wait_ge(loaded, 64)
                for l in range(2):
                    nc.scalar.activation(sc[l][:], cT[l][:], ACT.Silu).then_inc(silu_done, 1)

            @block.tensor
            def _(pe):
                for l in range(2):
                    pe.wait_ge(silu_done, l + 1)
                    for r in range(6):
                        last = nc.tensor.matmul(ps[:, l, r * NSEQ:(r + 1) * NSEQ], wmod[l][:, r, :], sc[l][:],
                                                start=(r == 0), stop=(r == 5))
                    last.then_inc(mod_done, 1)

            @block.gpsimd
            def _(pool):
                nc.gpsimd.memset(S.meanw[:], 1.0 / P)
                nc.gpsimd.memset(S.eps[:], EPS)
                nc.gpsimd.memset(S.X[:, TOK:], 0.0)
                for l in range(2):
                    nc.gpsimd.memset(S.mod[l][:, :, NSEQ:], 0.0)
                nc.gpsimd.memset(S.ident[:], 0.0).then_inc(filled, 1)
                pool.wait_ge(filled, 1)
                nc.gpsimd.affine_select(out=S.ident[:], in_=S.ident[:], compare_op=ALU.not_equal, fill=1.0,
                                        base=0, pattern=[[-1, P]], channel_multiplier=1).then_inc(filled, 1)
                pool.wait_ge(filled, 2)
                nc.gpsimd.tensor_copy(S.identb[:], S.ident[:])

            @block.vector
            def _(dve):
                n = 0
                for l in range(2):
                    dve.wait_ge(mod_done, l + 1)
                    for r in range(6):
                        row = ps[:, l, r * NSEQ:(r + 1) * NSEQ]
                        out = S.mod[l][:, r, 0:NSEQ]
                        if r in (SH_A, SH_B):
                            nc.vector.tensor_copy(out, row)
                        elif r in (SC_A, SC_B):
                            nc.vector.tensor_scalar(out, row, 1.0, None, ALU.add)
                        else:
                            nc.vector.tensor_scalar(gpos[:], row, 0.25, None, ALU.max)
                            nc.vector.tensor_scalar(gneg[:], row, -0.25, None, ALU.min).then_inc(gate_step, 1)
                            dve.wait_ge(gate_step, 3 * n + 1)
                            nc.vector.scalar_tensor_tensor(gpos[:], row, 0.0, gpos[:], ALU.is_ge, ALU.mult)
                            nc.vector.scalar_tensor_tensor(gneg[:], row, 0.0, gneg[:], ALU.is_lt, ALU.mult
                                                           ).then_inc(gate_step, 1)
                            dve.wait_ge(gate_step, 3 * n + 2)
                            nc.vector.tensor_tensor(out, gpos[:], gneg[:], ALU.add).then_inc(gate_step, 1)
                            n += 1
                            dve.wait_ge(gate_step, 3 * n)
                dve.wait_ge(filled, 2)
                nc.vector.tensor_tensor(S.center[:], S.ident[:], S.meanw[:], ALU.subtract)


def attention_weights(nc, ctx, w, S):
    sb = lambda name, shape: ctx.enter_context(nc.sbuf_tensor(name, shape, F32))
    S.wq = sb("wq", [HD, HEADS, P])
    S.wku = sb("wku", [HD, HEADS, LD])
    S.wvu = sb("wvu", [HD, HEADS, LD])
    S.wo = sb("wo", [HD, HEADS, P])
    S.wlat = sb("wlat", [P, 3, LD])
    return ([(S.wq[:], w["wqT"]), (S.wku[:], w["wkuT"]), (S.wvu[:], w["wvuT"]), (S.wo[:], w["wo"])]
            + [(S.wlat[:, r, :], w["wlat"]) for r in range(3)])


def attention(nc, w, S):
    with ExitStack() as ctx:
        def sb(name, shape, dt=F32):
            return ctx.enter_context(nc.sbuf_tensor(name, shape, dt))

        def pb(name, n):
            return ctx.enter_context(nc.psum_tensor(name, [P, n * 512], F32))

        wq, wku, wvu, wo, wlat = S.wq, S.wku, S.wvu, S.wo, S.wlat
        wqk = sb("wqk", [P, HEADS, LD])
        wvo = sb("wvo", [P, GROUPS, P])
        mask_s = sb("mask_s", [P, P], BF16)
        mask_t = sb("mask_t", [P, P], BF16)
        ones = sb("ones", [P, LD])

        xc = sb("xc", [P, SEQ])
        sq = sb("sq", [P, SEQ])
        lnv = sb("lnv", [P, SEQ])
        rstd = sb("rstd", [P, SEQ])
        H = sb("H", [P, 2, SEQ])
        lat = sb("lat", [P, 2, 2, SEQ], F32R)
        lat_tok = sb("lat_tok", [P, 2, 2, LD])
        Qh = sb("Qh", [P, 2, 2, SEQ], F32R)
        Ql = sb("Ql", [P, 2, 2, SEQ], F32R)
        Q = sb("Q", [P, 2, HEADS, SEQ], F32R)
        mx = sb("mx", [P, 2, HEADS])
        mhl = sb("mhl", [P, 2, 2, HEADS])
        nm = sb("nm", [2 * HEADS, SEQ], F32R)
        prob = sb("prob", [P, 4, 768])
        lden = sb("lden", [P, SEQ])
        rden = sb("rden", [P, SEQ])
        cn = sb("cn", [P, GROUPS, SEQ])

        psS, psT = pb("psS", 2), pb("psT", 2)
        psQ, psC, psM, psY = pb("psQ", 1), pb("psC", 1), pb("psM", 1), pb("psY", 1)

        with ExitStack() as pre:
            sem = lambda n: pre.enter_context(nc.semaphore(n))
            made, filled, zeroed = map(sem, ["a_made", "a_filled", "a_zeroed"])
            with nc.Block() as block:

                @block.gpsimd
                def _(pool):
                    nc.gpsimd.memset(ones[:], 1.0)
                    nc.gpsimd.memset(mask_s[:], 0.0)
                    nc.gpsimd.memset(mask_t[:], 0.0).then_inc(filled, 1)
                    pool.wait_ge(filled, 1)
                    nc.gpsimd.affine_select(out=mask_s[:], in_=mask_s[:], compare_op=ALU.is_ge, fill=NEG,
                                            base=0, pattern=[[-1, P]], channel_multiplier=1)
                    nc.gpsimd.affine_select(out=mask_t[:], in_=mask_t[:], compare_op=ALU.is_ge, fill=NEG,
                                            base=0, pattern=[[1, P]], channel_multiplier=-1)

                @block.sync
                def _(sp):
                    for sem_loaded, dst, src in S.later_loads:
                        sp.dma_start(dst, src).then_inc(sem_loaded, 16)

                @block.scalar
                def _(act):
                    for h in range(0, HEADS, 2):
                        nc.scalar.activation(Q[3 * LD:4 * LD, 1, h:h + 2, :],
                                             S.mod[0][3 * LD:4 * LD, 0, NSEQ:NSEQ + 1].broadcast_to([LD, 2 * SEQ]),
                                             ACT.Copy, scale=0.0)

                @block.tensor
                def _(pe):
                    pe.wait_ge(S.loaded_att, S.count_att)
                    for h in range(HEADS):
                        last = nc.tensor.matmul(psS[:, h * LD:(h + 1) * LD], wq[:, h, :], wku[:, h, :],
                                                start=(h == 0), stop=(h == HEADS - 1))
                    for h in range(HEADS):
                        g, q = divmod(h, 4)
                        last = nc.tensor.matmul(psT[LD * q:LD * (q + 1), g * P:(g + 1) * P], wvu[:, h, :],
                                                wo[:, h, :], start=(g == 0), stop=(g == GROUPS - 1))
                    last.then_inc(made, 1)

                @block.vector
                def _(dve):
                    nc.vector.memset(Q[3 * LD:4 * LD, 0, :, :].bitcast(F32), 0.0)
                    nc.vector.memset(lat[3 * LD:4 * LD, :, :, :].bitcast(F32), 0.0).then_inc(zeroed, 1)
                    dve.wait_ge(zeroed, 1)
                    nc.vector.memset(lat[3 * LD:3 * LD + 2, :, 1, :].bitcast(F32), 1.0)
                    dve.wait_ge(made, 1)
                    nc.vector.tensor_scalar(wqk[:], psS[:, 0:512].rearrange("p (h c) -> p h c", h=HEADS),
                                            HD ** -0.5, None, ALU.mult)
                    nc.vector.tensor_copy(wvo[:], psT[:, 0:512].rearrange("p (g c) -> p g c", g=GROUPS))

        names = ["mean_done", "xc_done", "sq_done", "var_done", "lnv_done", "rstd_done", "xn_done", "h_done",
                 "lat_done", "lat_hi", "lat_lo", "lt_done", "lt_copied", "q_done", "q_hi", "q_lo", "s_done", "max_done", "mh_done",
                 "mhl_done", "mt_done", "nm_done", "st_done", "exp_done", "pv_done", "lden_done", "rden_done",
                 "ctx_done", "y_done", "x_done"]
        (mean_done, xc_done, sq_done, var_done, lnv_done, rstd_done, xn_done, h_done, lat_done, lat_hi, lat_lo, lt_done, lt_copied,
         q_done, q_hi, q_lo, s_done, max_done, mh_done, mhl_done, mt_done, nm_done, st_done, exp_done, pv_done,
         lden_done, rden_done, ctx_done, y_done, x_done) = [ctx.enter_context(nc.semaphore("a_" + n)) for n in names]
        q_moved = [ctx.enter_context(nc.semaphore(f"a_q_moved{i}")) for i in range(2)]
        nm_moved = ctx.enter_context(nc.semaphore("a_nm_moved"))
        Q_MOVE, NM_MOVE = 12 * 16, 16
        nm_out = ctx.enter_context(nc.semaphore("a_nm_out"))
        nm_dram = nc.dram_tensor("nm_dram", [2, HEADS, SEQ], F32, kind="Internal").ap()
        BESIDE = ((0,), (1,), (2,), (3, 4), (5,), (6,), (7,), ())

        EXP0, PV0, CTX0, X0 = 1, 2, 1, 1
        mod = S.mod[0]

        with nc.Block() as block:

            @block.tensor
            def _(pe):
                def mean(n, first=False):
                    if not first:
                        pe.wait_ge(lat_lo, n)
                    nc.tensor.matmul(psM[:, 0:SEQ], S.meanw[:], S.X[:, ds(n * SEQ, SEQ)],
                                     start=True, stop=True).then_inc(mean_done, 1)

                def var(n):
                    pe.wait_ge(sq_done, n + 1)
                    nc.tensor.matmul(psM[:, 0:SEQ], S.meanw[:], sq[:], start=True, stop=True).then_inc(var_done, 1)

                def latent(n, par, first=False):
                    pe.wait_ge(h_done, n + 1)
                    if not first:
                        pe.wait_ge(nm_done, n)
                    nc.tensor.matmul(psM[0:3 * LD, 0:SEQ], wlat[:].rearrange("p r c -> p (r c)"), H[:, par, :],
                                     start=True, stop=True).then_inc(lat_done, 1)

                def latent_tokens(t, par):
                    pe.wait_ge(q_lo, t * 2 + 2)
                    for kb in range(2):
                        last = nc.tensor.matmul(psQ[:, kb * LD:(kb + 1) * LD],
                                                H[:, par, kb * P:(kb + 1) * P], wlat[:, 0, :],
                                                start=(kb == 0), stop=(kb == 1))
                    last.then_inc(lt_done, 1)

                def query(t, par, half, first=False):
                    pe.wait_ge(h_done, t + 1)
                    if not (first and half == 0):
                        pe.wait_ge(q_lo, t * 2 + half)
                    if half == 0 and not first:
                        pe.wait_ge(lt_copied, t)
                    for k in range(2):
                        g = 2 * half + k
                        last = nc.tensor.matmul(psQ[:, k * SEQ:(k + 1) * SEQ],
                                                wqk[:, 4 * g:4 * g + 4, :].rearrange("p h c -> p (h c)"),
                                                H[:, par, :], start=(k == 0), stop=(k == 1))
                    last.then_inc(q_done, 1)

                def scores(n, par, p, first=False):
                    if p % 4 == 0:
                        pe.wait_ge(q_moved[p // 4], n * Q_MOVE + Q_MOVE)
                    if not (first and p == 0):
                        pe.wait_ge(max_done, n * PAIRS + p)
                    if p == 0:
                        pe.wait_ge(lat_lo, n + 1)
                    for k in range(2):
                        h, wide = 2 * p + k, 512 * k
                        near = 256 + 128 * k
                        if k == 1:
                            nc.tensor.matmul(psS[:, near:near + P], Q[:, par, h, 0:P], lat[:, par, 0, 0:P],
                                             start=False, stop=False)
                            nc.tensor.matmul(psS[:, near:near + P], S.identb[:], mask_s[:], start=False, stop=True)
                        nc.tensor.matmul(psS[:, wide:wide + SEQ], Q[:, par, h, P:SEQ], lat[:, par, 0, :],
                                         start=True, stop=False)
                        last = nc.tensor.matmul(psS[:, wide + P:wide + SEQ], S.identb[:], mask_s[:],
                                                start=False, stop=(k == 1))
                        if k == 0:
                            nc.tensor.matmul(psS[:, near:near + P], Q[:, par, h, 0:P], lat[:, par, 0, 0:P],
                                             start=False, stop=False)
                            nc.tensor.matmul(psS[:, near:near + P], S.identb[:], mask_s[:], start=False, stop=False)
                    last.then_inc(s_done, 1)

                def scores_t(n, par, p):
                    if p == 0:
                        pe.wait_ge(nm_moved, n * NM_MOVE + NM_MOVE)
                    pe.wait_ge(exp_done, n * PAIRS + (p + EXP0))
                    for k in range(2):
                        h, wide = 2 * p + k, 512 * k
                        near = 256 + 128 * k

                        def far_keys(stop):
                            nc.tensor.matmul(psT[:, near:near + P], lat[:, par, 1, P:SEQ], Q[:, par, h, P:SEQ],
                                             start=False, stop=False)
                            nc.tensor.matmul(psT[:, near:near + P], S.identb[:], mask_t[:], start=False, stop=stop)

                        if k == 1:
                            far_keys(True)
                        nc.tensor.matmul(psT[:, wide:wide + SEQ], lat[:, par, 1, 0:P], Q[:, par, h, :],
                                         start=True, stop=False)
                        last = nc.tensor.matmul(psT[:, wide:wide + P], S.identb[:], mask_t[:],
                                                start=False, stop=(k == 1))
                        if k == 0:
                            far_keys(False)
                    last.then_inc(st_done, 1)

                def values(n, par, g):
                    pe.wait_ge(exp_done, n * PAIRS + (2 * g + 2 + EXP0))
                    pe.wait_ge(ctx_done, n * GROUPS + (g + CTX0))
                    for off, kb in ((0, 0), (0, 1), (SEQ, 0), (SEQ, 1)):
                        for q in range(4):
                            k = q % 2
                            at, cols = ((512 * k, SEQ), (256 + 128 * k, P))[kb]
                            first = off + SEQ - cols
                            last = nc.tensor.matmul(
                                psC[LD * q:LD * (q + 1), first:off + SEQ],
                                lat_tok[:, par, kb, :] if off == 0 else ones[:],
                                prob[:, (2 * g + q // 2) % 4, at:at + cols],
                                start=(off == 0 and kb == 0), stop=(off == SEQ and kb == 1))
                    last.then_inc(pv_done, 1)

                def project(n, g):
                    if g == 0:
                        pe.wait_ge(x_done, n + X0)
                    pe.wait_ge(ctx_done, n * GROUPS + (g + 1 + CTX0))
                    last = nc.tensor.matmul(psY[:, 0:SEQ], wvo[:, g, :], cn[:, g, :],
                                            start=(g == 0), stop=(g == GROUPS - 1))
                    if g == GROUPS - 1:
                        last.then_inc(y_done, 1)

                def max_t(n):
                    pe.wait_ge(mhl_done, n + 1)
                    for qb in range(2):
                        last = nc.tensor.transpose(psM[0:2 * HEADS, qb * P:(qb + 1) * P],
                                                   mhl[:, qb, :, :].rearrange("p a h -> p (a h)"), S.ident[:])
                    last.then_inc(mt_done, 1)

                pe.wait_ge(S.loaded_x, 16)
                mean(0, first=True)
                var(0)
                latent(0, 0, first=True)
                for half in range(2):
                    query(0, 0, half, first=True)
                latent_tokens(0, 0)
                mean(1)
                var(1)
                for p in range(PAIRS):
                    scores(0, 0, p, first=True)
                    if p == 0:
                        latent(1, 1, first=True)
                    if p in (1, 2):
                        query(1, 1, p - 1)
                    if p == 2:
                        latent_tokens(1, 1)
                max_t(0)
                pe.wait_ge(nm_done, 1)
                mean(2)
                def step(n, par, left=2):
                    for p in range(PAIRS):
                        if p < 4 and left:
                            scores(n + 1, 1 - par, p)
                        scores_t(n, par, p)
                        if p == 1 and left == 2:
                            var(n + 2)
                        if p == 3 and left == 2:
                            query(n + 2, par, 0)
                        if p == 5:
                            project(n, 0)
                        if p >= 2 and p % 2 == 0:
                            values(n, par, p // 2 - 1)
                        if 3 <= p < 7 and left:
                            scores(n + 1, 1 - par, p + 1)
                    if left == 2:
                        query(n + 2, par, 1)
                    if left:
                        max_t(n + 1)
                    project(n, 1)
                    if left == 2:
                        latent(n + 2, par)
                    values(n, par, GROUPS - 1)
                    project(n, 2)
                    if left == 2:
                        latent_tokens(n + 2, par)
                        mean(n + 3)
                    project(n, 3)

                with nc.tensor.Fori(0, NSEQ // 2 - 1) as j:
                    for par in range(2):
                        step(j * 2 + par, par)
                step(NSEQ - 2, 0, left=1)
                step(NSEQ - 1, 1, left=0)

            @block.sync
            def _(sp):
                def move_queries(t, par, half):
                    sp.wait_ge(q_lo, t * 2 + (half + 1))
                    for q in range(4):
                        src = slice(LD * q, LD * (q + 1))
                        for r, part in enumerate((Qh, Qh, Ql)):
                            sp.dma_start(Q[LD * r:LD * (r + 1), par, 8 * half + q:8 * half + 8:4, :].bitcast(F32),
                                         part[src, half, :, :].bitcast(F32)).then_inc(q_moved[half], 16)

                for t in range(2):
                    for half in range(2):
                        move_queries(t, t, half)
                with nc.sync.Fori(0, NSEQ // 2 - 1) as j:
                    for par in range(2):
                        n = j * 2 + par
                        for half in range(2):
                            move_queries(n + 2, par, half)
                for half in range(2):
                    sp.wait_ge(q_moved[half], NSEQ * Q_MOVE)

            @block.scalar
            def _(act):
                def square(n):
                    act.wait_ge(xc_done, n + 1)
                    nc.scalar.activation(sq[:], xc[:], ACT.Square).then_inc(sq_done, 1)

                def inv_std(n):
                    act.wait_ge(var_done, n + 1)
                    nc.scalar.activation(lnv[:], psM[:, 0:SEQ], ACT.Ln, bias=S.eps[:, 0:1]).then_inc(lnv_done, 1)
                    act.wait_ge(lnv_done, n + 1)
                    nc.scalar.activation(rstd[:], lnv[:], ACT.Exp, scale=-0.5).then_inc(rstd_done, 1)

                def latent_hi(n, par):
                    act.wait_ge(lat_done, n + 1)
                    nc.scalar.copy(lat[0:3 * LD, par, :, :],
                                   psM[0:3 * LD, 0:SEQ].unsqueeze(1).broadcast_to([3 * LD, 2, SEQ])).then_inc(lat_hi, 1)

                def query_hi(t, half, first=False):
                    act.wait_ge(q_done, t * 2 + (half + 1))
                    if not first:
                        act.wait_ge(q_moved[half], t * Q_MOVE)
                    nc.scalar.copy(Qh[:, half, :, :], psQ[:, :].rearrange("p (h q) -> p h q", h=2)).then_inc(q_hi, 1)

                def max_copy(n):
                    act.wait_ge(mt_done, n + 1)
                    nc.scalar.copy(nm[:], psM[0:2 * HEADS, 0:SEQ]).then_inc(nm_done, 1)
                    act.wait_ge(nm_done, n + 1)
                    act.dma_start(nm_dram.rearrange("a h q -> (a h) q"), nm[:].bitcast(F32)).then_inc(nm_out, 16)

                def max_move(t, par):
                    act.wait_ge(nm_out, t * 16 + 16)
                    act.dma_start(Q[3 * LD:3 * LD + 2, par, :, :].bitcast(F32), nm_dram).then_inc(nm_moved, 16)

                def softmax_exp(n, p):
                    act.wait_ge(st_done, n * PAIRS + (p + 1))
                    if p % 2 == 0:
                        act.wait_ge(pv_done, n * GROUPS + (p // 2 - 1 + PV0))
                    nc.scalar.activation(prob[:, p % 4, :], psT[:, 0:768], ACT.Exp).then_inc(exp_done, 1)

                def inv_den(n, g):
                    act.wait_ge(pv_done, n * GROUPS + (g + 1 + PV0))
                    nc.scalar.activation(lden[:], psC[:, SEQ:512], ACT.Ln).then_inc(lden_done, 1)
                    act.wait_ge(lden_done, n * GROUPS + (g + 1))
                    nc.scalar.activation(rden[:], lden[:], ACT.Exp, scale=-1.0).then_inc(rden_done, 1)

                nc.scalar.preload_act_table_set("natural_log_exp_and_others")
                for n in range(2):
                    square(n)
                    inv_std(n)
                    latent_hi(n, n)
                    for half in range(2):
                        query_hi(n, half, first=(n == 0))
                max_copy(0)
                max_move(0, 0)
                nc.scalar.copy(S.spare[:, 4:5], S.eps[:, 0:1]).then_inc(exp_done, EXP0)
                def step(n, par, left=2):
                    for p in range(PAIRS):
                        if p >= 3 and p % 2 == 1:
                            inv_den(n, (p - 3) // 2)
                        if p == 1 and left == 2:
                            square(n + 2)
                        softmax_exp(n, p)
                        if p == 1 and left == 2:
                            inv_std(n + 2)
                        if p == 3 and left == 2:
                            query_hi(n + 2, 0)
                    if left:
                        max_copy(n + 1)
                    if left == 2:
                        query_hi(n + 2, 1)
                        latent_hi(n + 2, par)
                    inv_den(n, GROUPS - 1)
                    if left:
                        max_move(n + 1, 1 - par)

                with nc.scalar.Fori(0, NSEQ // 2 - 1) as j:
                    for par in range(2):
                        step(j * 2 + par, par)
                step(NSEQ - 2, 0, left=1)
                step(NSEQ - 1, 1, left=0)
                act.wait_ge(nm_moved, NSEQ * NM_MOVE)

            @block.vector
            def _(dve):
                def center(n):
                    dve.wait_ge(mean_done, n + 1)
                    nc.vector.tensor_tensor(xc[:], S.X[:, ds(n * SEQ, SEQ)], psM[:, 0:SEQ], ALU.subtract
                                            ).then_inc(xc_done, 1)

                def normalize(n, par):
                    dve.wait_ge(rstd_done, n + 1)
                    nc.vector.tensor_tensor(xc[:], xc[:], rstd[:], ALU.mult).then_inc(xn_done, 1)
                    dve.wait_ge(xn_done, n + 1)
                    nc.vector.tensor_scalar(H[:, par, :], xc[:], mod[:, SC_A, ds(n, 1)], mod[:, SH_A, ds(n, 1)],
                                            ALU.mult, ALU.add).then_inc(h_done, 1)

                def latent_lo(n, par):
                    dve.wait_ge(lat_hi, n + 1)
                    rows = slice(LD, 2 * LD)
                    nc.vector.tensor_tensor(lat[rows, par, :, :], psM[rows, 0:SEQ].unsqueeze(1).broadcast_to([LD, 2, SEQ]),
                                            lat[rows, par, :, :], ALU.subtract).then_inc(lat_lo, 1)

                def latent_copy(t, par):
                    dve.wait_ge(lt_done, t + 1)
                    nc.vector.tensor_copy(lat_tok[:, par, :, :],
                                          psQ[:, 0:2 * LD].rearrange("p (k c) -> p k c", k=2)).then_inc(lt_copied, 1)

                def query_lo(t, half):
                    dve.wait_ge(q_hi, t * 2 + (half + 1))
                    nc.vector.tensor_tensor(Ql[:, half, :, :], psQ[:, :].rearrange("p (h q) -> p h q", h=2),
                                            Qh[:, half, :, :], ALU.subtract).then_inc(q_lo, 1)

                def maximum(n, p):
                    dve.wait_ge(s_done, n * PAIRS + (p + 1))
                    nc.vector.tensor_reduce(mx[:, 1, 2 * p:2 * p + 2],
                                            psS[:, :].rearrange("p (h q) -> p h q", h=2)[:, :, 0:SEQ], AX, ALU.max)
                    nc.vector.tensor_reduce(mx[:, 0, 2 * p:2 * p + 2],
                                            psS[:, 256:512].rearrange("p (h q) -> p h q", h=2), AX, ALU.max
                                            ).then_inc(max_done, 1)

                def max_split(n):
                    dve.wait_ge(max_done, n * PAIRS + PAIRS)
                    nc.vector.tensor_scalar(mhl[:, :, 0, :].bitcast(F32R), mx[:], -1.0, None, ALU.mult
                                            ).then_inc(mh_done, 1)
                    dve.wait_ge(mh_done, n + 1)
                    nc.vector.scalar_tensor_tensor(mhl[:, :, 1, :], mx[:], -1.0, mhl[:, :, 0, :],
                                                   ALU.mult, ALU.subtract).then_inc(mhl_done, 1)

                def context(n, g):
                    dve.wait_ge(rden_done, n * GROUPS + (g + 1))
                    nc.vector.tensor_tensor(cn[:, g, :], psC[:, 0:SEQ], rden[:], ALU.mult).then_inc(ctx_done, 1)

                def residual(n):
                    dve.wait_ge(y_done, n + 1)
                    x = S.X[:, ds(n * SEQ, SEQ)]
                    nc.vector.scalar_tensor_tensor(x, psY[:, 0:SEQ], mod[:, GA, ds(n, 1)], x, ALU.mult, ALU.add
                                                   ).then_inc(x_done, 1)

                nc.vector.memset(S.spare[:, 0:1], 0.0).then_inc(pv_done, PV0)
                nc.vector.memset(S.spare[:, 1:2], 0.0).then_inc(ctx_done, CTX0)
                nc.vector.memset(S.spare[:, 2:3], 0.0).then_inc(x_done, X0)
                center(0)
                normalize(0, 0)
                latent_lo(0, 0)
                for half in range(2):
                    query_lo(0, half)
                latent_copy(0, 0)
                center(1)
                normalize(1, 1)
                for p in range(PAIRS):
                    maximum(0, p)
                    if p == 0:
                        latent_lo(1, 1)
                    if p in (1, 2):
                        query_lo(1, p - 1)
                    if p == 2:
                        latent_copy(1, 1)
                max_split(0)
                def step(n, par, left=2):
                    for p in range(PAIRS):
                        if p == 5:
                            context(n, 1)
                        for pair in BESIDE[p]:
                            if left:
                                maximum(n + 1, pair)
                            if pair == 0 and left == 2:
                                center(n + 2)
                            if pair == 3:
                                context(n, 0)
                        if p == 1 and left == 2:
                            normalize(n + 2, par)
                        if p == 3 and left == 2:
                            query_lo(n + 2, 0)
                        if p == 6 and left:
                            max_split(n + 1)
                        if p == 7:
                            context(n, 2)
                    if left == 2:
                        query_lo(n + 2, 1)
                        latent_lo(n + 2, par)
                        latent_copy(n + 2, par)
                    context(n, GROUPS - 1)
                    residual(n)

                with nc.vector.Fori(0, NSEQ // 2 - 1) as j:
                    for par in range(2):
                        step(j * 2 + par, par)
                step(NSEQ - 2, 0, left=1)
                step(NSEQ - 1, 1, left=0)


MT = 512
NT = TOK // MT
SPT = MT // SEQ
UNITS = 2 * NALL
LEAD = 4
SUB = MT // P


def moe_weights(nc, ctx, w, S):
    sb = lambda name, shape: ctx.enter_context(nc.sbuf_tensor(name, shape, F32))
    S.raw = [sb(n, [P, NALL, 2, P]) for n in ("rawG", "rawU")]
    S.WD = sb("WD", [P, NALL, 2, P])
    S.router = sb("router", [P, NEXP])
    S.rbias = sb("rbias", [P, SUB, NEXP])
    loads = []
    for t, routed, shared in ((S.raw[0], "wg", "sg"), (S.raw[1], "wu", "su")):
        loads += [(t[:, 0:NEXP, :, :].rearrange("p e a i -> p e (a i)"), w[routed]),
                  (t[:, NEXP, :, :].rearrange("p a i -> p (a i)"), w[shared])]
    loads += [(S.WD[:, 0:NEXP, :, :], w["wd"]), (S.WD[:, NEXP, :, :], w["sd"]), (S.router[:], w["router"])]
    return loads + [(S.rbias[:, s, :], w["rbias"].to_broadcast([P, NEXP])) for s in range(SUB)]


def moe(nc, w, S):
    with ExitStack() as ctx:
        def sb(name, shape, dt=F32):
            return ctx.enter_context(nc.sbuf_tensor(name, shape, dt))

        def pb(name, n):
            return ctx.enter_context(nc.psum_tensor(name, [P, n, 512], F32))

        wr, bias = S.router, S.rbias
        raw = S.raw + [S.WD]
        WG, WU, WD = [[sb(f"{name}{i}", [P, NALL, 2, P], F32R)[:] for i in range(2)] for name in ("WG", "WU", "WD_")]
        tri = sb("tri", [P, NEXP, NEXP])
        sel = sb("sel_m", [2 * NALL, NALL, P], F32R)

        xc = sb("xc_m", [P, MT])
        sq = sb("sq_m", [P, MT])
        lnv = sb("lnv_m", [P, MT])
        rstd = sb("rstd_m", [P, MT])
        H = sb("H_m", [P, MT])
        Hh = sb("Hh_m", [P, 2, MT], F32R)
        Hl = sb("Hl_m", [P, 2, MT], F32R)
        lg = sb("lg", [P, SUB, NEXP])
        elg = sb("elg", [P, SUB, NEXP])
        pr = sb("pr", [P, SUB, NEXP])
        beats = sb("beats", [P, SUB, NEXP, NEXP])
        ties = sb("ties", [P, SUB, NEXP, NEXP])
        rank = sb("rank", [P, SUB, NEXP])
        pick = sb("pick", [P, SUB, NEXP])
        psum2 = sb("psum2", [P, SUB])
        wt = sb("wt", [P, SUB, NEXP])
        whl = sb("whl", [P, SUB, 2, NALL])
        wT = sb("wT", [2 * NALL, 2, MT], F32R)
        sg = sb("sg", [P, 2, MT])
        tt = sb("tt", [P, 2, MT])
        wbs = sb("wbs", [P, 2, MT])
        tw = sb("tw", [P, 3, MT])
        twh = sb("twh", [P, 3, MT], F32R)
        twl = sb("twl", [P, 3, MT], F32R)

        psG, psU, psY = pb("psG", 2), pb("psU", 2), pb("psY_m", 2)
        psW, psM = pb("psW", 1), pb("psM_m", 1)

        with ExitStack() as pre:
            sem = lambda n: pre.enter_context(nc.semaphore(n))
            sel0 = pre.enter_context(nc.sbuf_tensor("sel0_m", [2 * NALL, NALL, P], F32))
            high, filled = map(sem, ["m_high", "m_filled"])
            with nc.Block() as block:

                @block.gpsimd
                def _(pool):
                    nc.gpsimd.memset(tri[:], 1.0)
                    nc.gpsimd.memset(whl[:, :, 0, NEXP], 1.0)
                    nc.gpsimd.memset(whl[:, :, 1, NEXP], 0.0)
                    nc.gpsimd.memset(sel0[:], 0.0).then_inc(filled, 1)
                    pool.wait_ge(filled, 1)
                    nc.gpsimd.affine_select(out=tri[:], in_=tri[:], compare_op=ALU.is_ge, fill=0.0, base=-1,
                                            pattern=[[1, NEXP], [-1, NEXP]], channel_multiplier=0)
                    nc.gpsimd.affine_select(out=sel0[:], in_=sel0[:], compare_op=ALU.not_equal, fill=1.0, base=0,
                                            pattern=[[-1, NALL], [0, P]], channel_multiplier=1).then_inc(filled, 1)
                    pool.wait_ge(filled, 2)
                    nc.gpsimd.affine_select(out=sel0[:], in_=sel0[:], compare_op=ALU.not_equal, fill=1.0,
                                            base=-NALL, pattern=[[-1, NALL], [0, P]], channel_multiplier=1
                                            ).then_inc(filled, 1)

                @block.scalar
                def _(act):
                    act.wait_ge(S.loaded_moe, S.count_moe)
                    for t, out in zip(raw, (WG, WU, WD)):
                        nc.scalar.copy(out[0], t[:]).then_inc(high, 1)

                @block.vector
                def _(dve):
                    for n, (t, out) in enumerate(zip(raw, (WG, WU, WD))):
                        dve.wait_ge(high, n + 1)
                        nc.vector.tensor_tensor(out[1], t[:], out[0], ALU.subtract)
                    dve.wait_ge(filled, 3)
                    nc.vector.tensor_copy(sel[:], sel0[:])

        names = ["mean_done", "xc_done", "sq_done", "var_done", "lnv_done", "rstd_done", "xn_done", "h_done",
                 "hh_done", "hl_done", "lgp_done", "lg_done", "pr_done", "route", "wtp_done", "wt_done",
                 "gu_done", "silu_done", "t_done", "wb_done", "wbs_done", "tw_done", "twh_done", "twl_done",
                 "down_done", "x_done"]
        (mean_done, xc_done, sq_done, var_done, lnv_done, rstd_done, xn_done, h_done, hh_done, hl_done, lgp_done,
         lg_done, pr_done, route, wtp_done, wt_done, gu_done, silu_done, t_done, wb_done, wbs_done,
         tw_done, twh_done, twl_done, down_done, x_done) = [ctx.enter_context(nc.semaphore("m_" + n)) for n in names]
        TW0, TL0, DN0, X0 = 4, 3, 4, 2
        ROUTE = 12
        mod = S.mod[0]

        def ahead(par, k, by):
            return ((0, par, k + by) if k + by < UNITS else (1, 1 - par, k + by - UNITS))

        with nc.Block() as block:

            @block.tensor
            def _(pe):
                def mean(n, first=False):
                    if not first:
                        pe.wait_ge(wt_done, n - 1)
                    nc.tensor.matmul(psM[:, 0, :], S.meanw[:], S.X[:, ds(n * MT, MT)],
                                     start=True, stop=True).then_inc(mean_done, 1)

                def var(n):
                    pe.wait_ge(sq_done, n + 1)
                    nc.tensor.matmul(psM[:, 0, :], S.meanw[:], sq[:], start=True, stop=True).then_inc(var_done, 1)

                def logits(n, par):
                    pe.wait_ge(h_done, n + 1)
                    for s in range(SUB):
                        last = nc.tensor.matmul(psM[:, 0, s * NEXP:(s + 1) * NEXP], H[:, s * P:(s + 1) * P],
                                                wr[:], start=(s == 0), stop=(s == SUB - 1))
                    last.then_inc(lgp_done, 1)

                def weights_t(n, first=False):
                    pe.wait_ge(route, n * ROUTE + ROUTE)
                    if not first:
                        pe.wait_ge(lg_done, n + 2)
                    for s in range(SUB):
                        last = nc.tensor.transpose(psM[0:2 * NALL, 0, s * P:(s + 1) * P],
                                                   whl[:, s, :, :].rearrange("p a e -> p (a e)"), S.ident[:])
                    last.then_inc(wtp_done, 1)

                def up(n, par, k, first=False):
                    e, half = divmod(k, 2)
                    u = par * UNITS + k
                    if k == 0:
                        pe.wait_ge(hl_done, n + 1)
                    if not (first and k < 2):
                        pe.wait_ge(silu_done, n * UNITS + (k - 1))
                        pe.wait_ge(t_done, n * UNITS + (k - 1))
                    for W, bank in ((WG, psG), (WU, psU)):
                        nc.tensor.matmul(bank[:, u % 2, :], W[0][:, e, half, :], Hh[:, par, :], start=True, stop=False)
                        nc.tensor.matmul(bank[:, u % 2, :], W[0][:, e, half, :], Hl[:, par, :], start=False, stop=False)
                        last = nc.tensor.matmul(bank[:, u % 2, :], W[1][:, e, half, :], Hh[:, par, :],
                                                start=False, stop=True)
                    last.then_inc(gu_done, 1)
                    if half == 0:
                        if k == 0:
                            pe.wait_ge(wt_done, n + 1)
                        if not (first and k == 0):
                            pe.wait_ge(wbs_done, n * NALL + e)
                        nc.tensor.matmul(psW[:, 0, :], sel[:, e, :], wT[:, par, :], start=True, stop=True
                                         ).then_inc(wb_done, 1)

                def down(n, par, k):
                    e, half = divmod(k, 2)
                    u = par * UNITS + k
                    pe.wait_ge(twl_done, n * UNITS + (k + 1 + TL0))
                    if k == 0:
                        pe.wait_ge(x_done, n + (X0 - 1))
                    nc.tensor.matmul(psY[:, par, :], WD[0][:, e, half, :], twh[:, u % 3, :], start=(k == 0), stop=False)
                    nc.tensor.matmul(psY[:, par, :], WD[1][:, e, half, :], twh[:, u % 3, :], start=False, stop=False)
                    nc.tensor.matmul(psY[:, par, :], WD[0][:, e, half, :], twl[:, u % 3, :], start=False,
                                     stop=(k == UNITS - 1)).then_inc(down_done, 1)

                mean(0, first=True)
                var(0)
                logits(0, 0)
                weights_t(0, first=True)
                for k in range(LEAD):
                    up(0, 0, k, first=True)
                    if k == 1:
                        pe.wait_ge(wt_done, 1)
                        mean(1, first=True)
                    if k == 2:
                        var(1)
                logits(1, 1)
                with nc.tensor.Fori(0, NT // 2) as j:
                    for par in range(2):
                        n = j * 2 + par
                        for k in range(UNITS):
                            on, upar, uk = ahead(par, k, LEAD)
                            up(n + on, upar, uk)
                            down(n, par, k)
                            if k == 1:
                                mean(n + 2)
                            if k == 3:
                                var(n + 2)
                            if k == 9:
                                logits(n + 2, par)
                            if k == 12:
                                weights_t(n + 1)

            @block.scalar
            def _(act):
                def square(n):
                    act.wait_ge(xc_done, n + 1)
                    nc.scalar.activation(sq[:], xc[:], ACT.Square).then_inc(sq_done, 1)

                def inv_std(n):
                    act.wait_ge(var_done, n + 1)
                    nc.scalar.activation(lnv[:], psM[:, 0, :], ACT.Ln, bias=S.eps[:, 0:1]).then_inc(lnv_done, 1)
                    act.wait_ge(lnv_done, n + 1)
                    nc.scalar.activation(rstd[:], lnv[:], ACT.Exp, scale=-0.5).then_inc(rstd_done, 1)

                def high_h(n, par):
                    act.wait_ge(h_done, n + 1)
                    nc.scalar.copy(Hh[:, par, :], H[:]).then_inc(hh_done, 1)

                def exp_logits(n):
                    act.wait_ge(lg_done, n + 1)
                    nc.scalar.activation(elg[:], lg[:], ACT.Exp, scale=-1.0).then_inc(pr_done, 1)

                def weights_copy(n, par):
                    act.wait_ge(wtp_done, n + 1)
                    nc.scalar.copy(wT[:, par, :], psM[0:2 * NALL, 0, :]).then_inc(wt_done, 1)

                def silu(n, par, k):
                    u = par * UNITS + k
                    act.wait_ge(gu_done, n * UNITS + (k + 1))
                    nc.scalar.activation(sg[:, u % 2, :], psG[:, u % 2, :], ACT.Silu).then_inc(silu_done, 1)
                    if k % 2 == 0:
                        e = k // 2
                        act.wait_ge(wb_done, n * NALL + (e + 1))
                        act.wait_ge(tw_done, n * UNITS + (2 * e - 2 + TW0))
                        nc.scalar.copy(wbs[:, (par * NALL + e) % 2, :], psW[:, 0, :]).then_inc(wbs_done, 1)

                def product_high(n, par, k):
                    u = par * UNITS + k
                    act.wait_ge(tw_done, n * UNITS + (k + 1 + TW0))
                    act.wait_ge(down_done, n * UNITS + (k - 2 + DN0))
                    nc.scalar.copy(twh[:, u % 3, :], tw[:, u % 3, :]).then_inc(twh_done, 1)

                nc.scalar.preload_act_table_set("natural_log_exp_and_others")
                square(0)
                inv_std(0)
                high_h(0, 0)
                exp_logits(0)
                weights_copy(0, 0)
                for k in range(LEAD):
                    silu(0, 0, k)
                    if k == 1:
                        square(1)
                nc.scalar.preload_act_table_set("natural_log_exp_and_others")
                inv_std(1)
                high_h(1, 1)
                for k in range(2):
                    product_high(0, 0, k)
                with nc.scalar.Fori(0, NT // 2) as j:
                    for par in range(2):
                        n = j * 2 + par
                        for k in range(UNITS):
                            on, upar, uk = ahead(par, k, LEAD)
                            silu(n + on, upar, uk)
                            if k == 13:
                                weights_copy(n + 1, 1 - par)
                            on, upar, uk = ahead(par, k, 2)
                            product_high(n + on, upar, uk)
                            if k == 2:
                                square(n + 2)
                            if k == 5:
                                nc.scalar.preload_act_table_set("natural_log_exp_and_others")
                                exp_logits(n + 1)
                                inv_std(n + 2)
                            if k == 14:
                                high_h(n + 2, par)

            @block.gpsimd
            def _(pool):
                def weigh(n, par, k):
                    u = par * UNITS + k
                    e = k // 2
                    pool.wait_ge(t_done, n * UNITS + (k + 1))
                    pool.wait_ge(wbs_done, n * NALL + (e + 1))
                    pool.wait_ge(twl_done, n * UNITS + (k - 2 + TL0))
                    nc.gpsimd.tensor_tensor(tw[:, u % 3, :], tt[:, u % 2, :], wbs[:, (par * NALL + e) % 2, :],
                                            ALU.mult).then_inc(tw_done, 1)

                nc.gpsimd.memset(S.spare[:, 3:4], 0.0).then_inc(tw_done, TW0)
                for k in range(LEAD - 1):
                    weigh(0, 0, k)
                with nc.gpsimd.Fori(0, NT // 2) as j:
                    for par in range(2):
                        n = j * 2 + par
                        for k in range(UNITS):
                            on, upar, uk = ahead(par, k, LEAD - 1)
                            weigh(n + on, upar, uk)

            @block.vector
            def _(dve):
                def center(n):
                    dve.wait_ge(mean_done, n + 1)
                    nc.vector.tensor_tensor(xc[:], S.X[:, ds(n * MT, MT)], psM[:, 0, :], ALU.subtract
                                            ).then_inc(xc_done, 1)

                def normalize(n, par):
                    dve.wait_ge(rstd_done, n + 1)
                    nc.vector.tensor_tensor(xc[:], xc[:], rstd[:], ALU.mult).then_inc(xn_done, 1)
                    dve.wait_ge(xn_done, n + 1)
                    for s in range(SPT):
                        cols = slice(s * SEQ, (s + 1) * SEQ)
                        last = nc.vector.tensor_scalar(H[:, cols], xc[:, cols], mod[:, SC_B, ds(n * SPT + s, 1)],
                                                       mod[:, SH_B, ds(n * SPT + s, 1)], ALU.mult, ALU.add)
                    last.then_inc(h_done, 1)

                def low_h(n, par):
                    dve.wait_ge(hh_done, n + 1)
                    nc.vector.tensor_tensor(Hl[:, par, :], H[:], Hh[:, par, :], ALU.subtract
                                            ).then_inc(hl_done, 1)

                def add_bias(n, first=False):
                    dve.wait_ge(lgp_done, n + 1)
                    if not first:
                        dve.wait_ge(pr_done, n)
                    nc.vector.tensor_tensor(lg[:], psM[:, 0, 0:SUB * NEXP].rearrange("p (s e) -> p s e", s=SUB),
                                            bias[:], ALU.add).then_inc(lg_done, 1)

                def choose(n, step):
                    if step == 0:
                        dve.wait_ge(pr_done, n + 1)
                    else:
                        dve.wait_ge(route, n * ROUTE + step)
                    big = [P, SUB, NEXP, NEXP]
                    other = pr[:].unsqueeze(2).broadcast_to(big)
                    own = pr[:].unsqueeze(3).broadcast_to(big)
                    if step == 0:
                        last = nc.vector.tensor_scalar(elg[:], elg[:], 1.0, None, ALU.add)
                    elif step == 1:
                        last = nc.vector.reciprocal(pr[:], elg[:])
                    elif step == 2:
                        nc.vector.tensor_tensor(beats[:], other, own, ALU.is_gt)
                        last = nc.vector.tensor_tensor(ties[:], other, own, ALU.is_equal)
                    elif step == 3:
                        last = nc.vector.tensor_tensor(ties[:], ties[:], tri[:].unsqueeze(1).broadcast_to(big), ALU.mult)
                    elif step == 4:
                        last = nc.vector.tensor_tensor(beats[:], beats[:], ties[:], ALU.add)
                    elif step == 5:
                        last = nc.vector.tensor_reduce(rank[:], beats[:], AX, ALU.add)
                    elif step == 6:
                        last = nc.vector.scalar_tensor_tensor(pick[:], rank[:], 1.5, pr[:], ALU.is_lt, ALU.mult)
                    elif step == 7:
                        last = nc.vector.tensor_reduce(psum2[:], pick[:], AX, ALU.add)
                    elif step == 8:
                        last = nc.vector.reciprocal(psum2[:], psum2[:])
                    elif step == 9:
                        last = nc.vector.tensor_tensor(wt[:], pick[:],
                                                       psum2[:].unsqueeze(2).broadcast_to([P, SUB, NEXP]), ALU.mult)
                    elif step == 10:
                        last = nc.vector.tensor_copy(whl[:, :, 0, 0:NEXP].bitcast(F32R), wt[:])
                    else:
                        last = nc.vector.tensor_tensor(whl[:, :, 1, 0:NEXP], wt[:], whl[:, :, 0, 0:NEXP], ALU.subtract)
                    last.then_inc(route, 1)

                def gate_up(n, par, k):
                    u = par * UNITS + k
                    dve.wait_ge(silu_done, n * UNITS + (k + 1))
                    dve.wait_ge(tw_done, n * UNITS + (k - 1 + TW0))
                    nc.vector.tensor_tensor(tt[:, u % 2, :], sg[:, u % 2, :], psU[:, u % 2, :], ALU.mult
                                            ).then_inc(t_done, 1)

                def product_low(n, par, k):
                    u = par * UNITS + k
                    dve.wait_ge(twh_done, n * UNITS + (k + 1))
                    nc.vector.tensor_tensor(twl[:, u % 3, :], tw[:, u % 3, :], twh[:, u % 3, :], ALU.subtract
                                            ).then_inc(twl_done, 1)

                def residual(n, par):
                    dve.wait_ge(down_done, n * UNITS + (UNITS + DN0))
                    for s in range(SPT):
                        x = S.X[:, ds((n * SPT + s) * SEQ, SEQ)]
                        last = nc.vector.scalar_tensor_tensor(x, psY[:, par, s * SEQ:(s + 1) * SEQ],
                                                              mod[:, GB, ds(n * SPT + s, 1)], x, ALU.mult, ALU.add)
                    last.then_inc(x_done, 1)

                nc.vector.memset(S.spare[:, 0:1], 0.0).then_inc(twl_done, TL0)
                nc.vector.memset(S.spare[:, 1:2], 0.0).then_inc(down_done, DN0)
                nc.vector.memset(S.spare[:, 2:3], 0.0).then_inc(x_done, X0)
                center(0)
                normalize(0, 0)
                low_h(0, 0)
                add_bias(0, first=True)
                for step in range(ROUTE):
                    choose(0, step)
                for k in range(LEAD - 1):
                    gate_up(0, 0, k)
                    if k == 1:
                        center(1)
                normalize(1, 1)
                low_h(1, 1)
                add_bias(1)
                product_low(0, 0, 0)
                with nc.vector.Fori(0, NT // 2) as j:
                    for par in range(2):
                        n = j * 2 + par
                        for k in range(UNITS):
                            on, upar, uk = ahead(par, k, LEAD - 1)
                            gate_up(n + on, upar, uk)
                            if 6 <= k < 12:
                                choose(n + 1, 2 * (k - 6))
                            on, upar, uk = ahead(par, k, 1)
                            product_low(n + on, upar, uk)
                            if 6 <= k < 12:
                                choose(n + 1, 2 * (k - 6) + 1)
                            if k == 2:
                                center(n + 2)
                            if k == 6:
                                normalize(n + 2, par)
                            if k == 10:
                                add_bias(n + 2)
                            if k == 15:
                                low_h(n + 2, par)
                        residual(n, par)


ROW = SEQ + 1
SMALL_E = 0.03
SMALL = 1e-5
ADEEP = 8

L_DECAY, L_SCAN, L_TIMES, L_SPREAD, L_SUM = 8, 6, 5, 6, 4


def mamba_weights(nc, ctx, w, S):
    sb = lambda name, shape: ctx.enter_context(nc.sbuf_tensor(name, shape, F32))
    S.wz = sb("wz", [P, P])
    S.wdd = sb("wdd", [P, RDT])
    S.wc = sb("wc", [P, 4, NST])
    S.wdt = sb("wdt", [RDT, P])
    S.wout = sb("wout_s", [P, P])
    S.conv = sb("conv", [P, TAPS])
    S.bdt = sb("bdt", [P, 1])
    S.dskip = sb("dskip", [P, 1])
    S.alog = sb("alog", [P, NST])
    columns = w["wpar"][:, RDT + NST:RDT + 2 * NST]
    return [(S.wz[:], w["wz"]), (S.wdd[:], w["wpar"][:, 0:RDT]), (S.wc[:, 0, :], columns), (S.wc[:, 2, :], columns),
            (S.wdt[:], w["wdt"]), (S.wout[:], w["wout"]), (S.conv[:], w["conv"]), (S.bdt[:], w["bdt"]),
            (S.dskip[:], w["dskip"]), (S.alog[:], w["alog"])]


def mamba(nc, w, S):
    with ExitStack() as ctx:
        def sb(name, shape, dt=F32):
            return ctx.enter_context(nc.sbuf_tensor(name, shape, dt))

        def pb(name, n):
            return ctx.enter_context(nc.psum_tensor(name, [P, n, 512], F32))

        wz, wdd, wc, wdt, wout, conv, bdt, dskip, alog = (S.wz, S.wdd, S.wc, S.wdt, S.wout, S.conv, S.bdt, S.dskip,
                                                          S.alog)
        negA = sb("negA", [P, NST])
        is_small = sb("is_small", [P, NST])
        is_large = sb("is_large", [P, NST])
        cst = sb("cst", [P, NST])
        diag = sb("diag", [P, NST, P])
        csT = [sb(f"csT{i}", [4 * NST, P], F32R) for i in range(2)]
        sel = sb("sel_s", [4 * NST, NST, P], F32R)
        any_small = sb("any_small", [P, 1], mybir.dt.int32)

        xn = sb("xn_s", [P, MT])
        sq = sb("sq_s", [P, MT])
        lnv = sb("lnv_s", [P, MT])
        rstd = sb("rstd_s", [P, MT])
        H = sb("H_s", [P, SPT, TAPS - 1 + SEQ])
        acc = sb("acc_s", [P, 2, SPT, SEQ])
        U = sb("U_s", [P, 2, SPT, SEQ])
        sz = sb("sz_s", [P, 2, MT])
        dtx = sb("dtx", [P, 2, SPT, ROW + 1])
        dd = sb("dd", [P, 3, SPT * ROW])
        wx = sb("wx", [P, SPT, ROW])
        part = sb("part_s", [P, SPT * ROW])
        Ch = sb("Ch", [4 * NST, 2, MT], F32R)
        dtu = sb("dtu", [RDT, MT])
        A = sb("A_s", [P, ADEEP, SPT, ROW])
        K = sb("K_s", [P, 4, SPT, ROW])
        M = sb("M_s", [P, 4, MT])
        ex = sb("ex", [P, MT])
        rx = sb("rx", [P, MT])
        big = sb("big", [P, MT])
        tiny = sb("tiny", [P, MT])
        one = sb("one", [P, 1])
        coef = sb("coef", [P, 4])
        gd = sb("gd", [P, MT])
        gu = sb("gu", [P, MT])
        ys = sb("ys", [P, MT])
        yo = sb("yo", [P, MT])

        psX, psM, psZ, psC, psY, psG = (pb("psX_s", 1), pb("psM_s", 1), pb("psZ_s", 1), pb("psC_s", 2),
                                        pb("psY_s", 2), pb("psG_s", 1))

        with ExitStack() as pre:
            sem = lambda n: pre.enter_context(nc.semaphore(n))
            expd, vstep, made, filled = map(sem, ["s_expd", "s_vstep", "s_made", "s_filled"])
            ea = pre.enter_context(nc.sbuf_tensor("ea", [P, NST], F32))
            den = pre.enter_context(nc.sbuf_tensor("den_s", [P, NST], F32))
            cs4 = pre.enter_context(nc.sbuf_tensor("cs4", [P, 4, NST], F32))
            sel0 = pre.enter_context(nc.sbuf_tensor("sel0_s", [4 * NST, NST, P], F32))
            onesq = pre.enter_context(nc.sbuf_tensor("onesq", [P, P], F32))
            some = pre.enter_context(nc.sbuf_tensor("some", [P, 1], F32))
            with nc.Block() as block:

                @block.gpsimd
                def _(pool):
                    for r in (1, 3):
                        nc.gpsimd.memset(wc[:, r, :], 0.0)
                    nc.gpsimd.memset(onesq[:], 1.0)
                    nc.gpsimd.memset(one[:], 1.0)
                    for i, c in enumerate((-1 / 4, 1 / 3, -1 / 2, 1.0)):
                        nc.gpsimd.memset(coef[:, i:i + 1], c)
                    nc.gpsimd.memset(cs4[:], 0.0)
                    nc.gpsimd.memset(H[:, :, 0:TAPS - 1], 0.0)
                    nc.gpsimd.memset(wx[:, :, 0:1], 0.0)
                    nc.gpsimd.memset(A[:, :, :, 0:1], 0.0)
                    for par in range(2):
                        nc.gpsimd.memset(dd[:, par, :].rearrange("p (s t) -> p s t", s=SPT)[:, :, 1:2], 0.0)
                    nc.gpsimd.memset(sel0[:], 0.0).then_inc(filled, 1)
                    pool.wait_ge(filled, 1)
                    nc.gpsimd.affine_select(out=sel0[:], in_=sel0[:], compare_op=ALU.not_equal, fill=1.0, base=0,
                                            pattern=[[-1, NST], [0, P]], channel_multiplier=1).then_inc(filled, 1)
                    pool.wait_ge(filled, 2)
                    nc.gpsimd.affine_select(out=sel0[:], in_=sel0[:], compare_op=ALU.not_equal, fill=1.0,
                                            base=-2 * NST, pattern=[[-1, NST], [0, P]], channel_multiplier=1
                                            ).then_inc(filled, 1)

                @block.scalar
                def _(act):
                    act.wait_ge(S.loaded_mamba, S.count_mamba)
                    nc.scalar.activation(ea[:], alog[:], ACT.Exp).then_inc(expd, 1)

                @block.vector
                def _(dve):
                    n = [0]

                    def after(ins):
                        n[0] += 1
                        ins.then_inc(vstep, 1)
                        dve.wait_ge(vstep, n[0])

                    dve.wait_ge(expd, 1)
                    dve.wait_ge(filled, 3)
                    nc.vector.tensor_scalar(negA[:], ea[:], -1.0, None, ALU.mult)
                    nc.vector.tensor_scalar(is_small[:], ea[:], SMALL, None, ALU.is_lt)
                    after(nc.vector.tensor_scalar(is_large[:], ea[:], SMALL, None, ALU.is_ge))
                    after(nc.vector.scalar_tensor_tensor(den[:], negA[:], 1e-10, is_large[:], ALU.add, ALU.mult))
                    after(nc.vector.tensor_tensor(den[:], den[:], is_small[:], ALU.add))
                    after(nc.vector.reciprocal(cst[:], den[:]))
                    for r in (0, 2):
                        nc.vector.tensor_tensor(cs4[:, r, :], cst[:], is_large[:], ALU.mult)
                    for k in range(NST):
                        last = nc.vector.tensor_scalar(diag[:, k, :], S.ident[:], cst[:, k:k + 1], None, ALU.mult)
                    after(last)
                    nc.vector.tensor_copy(sel[:], sel0[:])
                    dve.wait_ge(made, 1)
                    after(nc.vector.tensor_copy(csT[0][:], psM[0:4 * NST, 0, 0:P]))
                    nc.vector.tensor_tensor(csT[1][:], psM[0:4 * NST, 0, 0:P], csT[0][:], ALU.subtract)
                    after(nc.vector.tensor_reduce(some[:], psZ[:, 0, 0:NST], AX, ALU.max))
                    after(nc.vector.tensor_scalar(any_small[:], some[:], 0.5, None, ALU.is_gt))

                @block.tensor
                def _(pe):
                    pe.wait_ge(vstep, 5)
                    nc.tensor.transpose(psM[0:4 * NST, 0, 0:P], cs4[:].rearrange("p r n -> p (r n)"), S.ident[:])
                    nc.tensor.matmul(psZ[:, 0, 0:NST], onesq[:], is_small[:], start=True, stop=True).then_inc(made, 1)

        names = ["xc_done", "sq_done", "var_done", "lnv_done", "rstd_done", "xn_done", "h_done",
                 "z_done", "c_done", "chi_done", "clo_done", "dtu_done", "dtuc_done", "dt_done", "ax_done",
                 "tap0_done", "conv_step", "conv_done", "sz_done", "u_done", "e_done", "big_done", "x_read", "series",
                 "blend_done", "dtx_done", "dd_done", "w_done", "a_done", "cb_done", "k_done", "m_done", "acc_done",
                 "g_done", "gd_done", "gu_done", "ys_done", "yo_done", "o_done", "x_done", "small_step"]
        (xc_done, sq_done, var_done, lnv_done, rstd_done, xn_done, h_done,
         z_done, c_done, chi_done, clo_done, dtu_done, dtuc_done, dt_done, ax_done,
         tap0_done, conv_step, conv_done, sz_done, u_done, e_done, big_done, x_read, series,
         blend_done, dtx_done, dd_done, w_done, a_done, cb_done, k_done, m_done, acc_done,
         g_done, gd_done, gu_done, ys_done, yo_done, o_done, x_done, small_step) = [
             ctx.enter_context(nc.semaphore("s_" + n)) for n in names]
        K0, M0, AC0, X0, YS0, GU0 = ADEEP, 4, 4, 1, 2, 1
        SERIES = 9
        mod = S.mod[1]

        def ahead(n, par, k):
            return (n, par, k) if k < NST else (n + 1, 1 - par, k - NST)

        with nc.Block() as block:

            @block.tensor
            def _(pe):
                def centered(t):
                    nc.tensor.matmul(psX[:, 0, :], S.center[:], S.X[:, ds(t * MT, MT)],
                                     start=True, stop=True).then_inc(xc_done, 1)

                def var(t, first=False):
                    pe.wait_ge(sq_done, t + 1)
                    if not first:
                        pe.wait_ge(x_read, t)
                    nc.tensor.matmul(psM[:, 0, :], S.meanw[:], sq[:], start=True, stop=True).then_inc(var_done, 1)

                h = H[:, :, TAPS - 1:]

                def c_product(t):
                    pe.wait_ge(h_done, t + 1)
                    nc.tensor.matmul(psM[0:4 * NST, 0, :], wc[:].rearrange("p r n -> p (r n)"), h,
                                     start=True, stop=True).then_inc(c_done, 1)

                def z_product(t, first=False):
                    if not first:
                        pe.wait_ge(sz_done, t)
                    nc.tensor.matmul(psZ[:, 0, :], wz[:], h, start=True, stop=True).then_inc(z_done, 1)

                def dt_down(t):
                    pe.wait_ge(clo_done, t + 1)
                    nc.tensor.matmul(psM[0:RDT, 0, :], wdd[:], h, start=True, stop=True).then_inc(dtu_done, 1)

                def dt_up(t):
                    pe.wait_ge(dtuc_done, t + 1)
                    nc.tensor.matmul(psM[:, 0, :], wdt[:], dtu[:], start=True, stop=True).then_inc(dt_done, 1)

                def spread_c(t, par, k):
                    pe.wait_ge(m_done, t * NST + (k - 1 + M0))
                    nc.tensor.matmul(psC[:, k % 2, :], sel[:, k, :], Ch[:, par, :], start=True, stop=True
                                     ).then_inc(cb_done, 1)

                def sum_c(n, par):
                    pe.wait_ge(x_done, n + X0)
                    nc.tensor.matmul(psG[:, 0, :], csT[0][:], Ch[:, par, :], start=True, stop=False)
                    nc.tensor.matmul(psG[:, 0, :], csT[1][:], Ch[:, par, :], start=False, stop=True
                                     ).then_inc(g_done, 1)

                def accumulate(t, par, k):
                    pe.wait_ge(m_done, t * NST + (k + 1 + M0))
                    if k == 0:
                        pe.wait_ge(ys_done, t - 1 + YS0)
                    nc.tensor.matmul(psY[:, par, :], diag[:, k, :], M[:, k % 4, :], start=(k == 0),
                                     stop=(k == NST - 1)).then_inc(acc_done, 1)

                def project(n):
                    pe.wait_ge(yo_done, n + 1)
                    nc.tensor.matmul(psG[:, 0, :], wout[:], yo[:], start=True, stop=True).then_inc(o_done, 1)

                for t in range(2):
                    centered(t)
                    var(t, first=(t == 0))
                    c_product(t)
                    dt_down(t)
                    dt_up(t)
                    if t == 0:
                        z_product(0, first=True)
                for k in range(L_SPREAD):
                    spread_c(0, 0, k)
                    if k >= L_SPREAD - L_SUM:
                        accumulate(0, 0, k - (L_SPREAD - L_SUM))
                with nc.tensor.Fori(0, NT // 2) as j:
                    for par in range(2):
                        n = j * 2 + par
                        for k in range(NST):
                            spread_c(*ahead(n, par, k + L_SPREAD))
                            accumulate(*ahead(n, par, k + L_SUM))
                            if k == 0:
                                z_product(n + 1)
                            if k == 2:
                                sum_c(n, par)
                            if k == 1:
                                centered(n + 2)
                            if k == 5:
                                var(n + 2)
                            if k == 10:
                                c_product(n + 2)
                            if k == 13:
                                dt_down(n + 2)
                            if k == 14:
                                dt_up(n + 2)
                            if k == 14:
                                project(n)
                nc.tensor.matmul(psY[:, NT % 2, :], diag[:, 0, :], diag[:, 0:MT // P, :], start=False, stop=True)

            @block.scalar
            def _(act):
                def square(t):
                    act.wait_ge(xc_done, t + 1)
                    nc.scalar.activation(sq[:], psX[:, 0, :], ACT.Square).then_inc(sq_done, 1)

                def inv_std(t):
                    act.wait_ge(var_done, t + 1)
                    nc.scalar.activation(lnv[:], psM[:, 0, :], ACT.Ln, bias=S.eps[:, 0:1]).then_inc(lnv_done, 1)
                    act.wait_ge(lnv_done, t + 1)
                    nc.scalar.activation(rstd[:], lnv[:], ACT.Exp, scale=-0.5).then_inc(rstd_done, 1)

                def modulate(t, first=False):
                    act.wait_ge(xn_done, t + 1)
                    if not first:
                        act.wait_ge(z_done, t)
                        act.wait_ge(conv_done, t)
                    for s in range(SPT):
                        last = nc.scalar.activation(H[:, s, TAPS - 1:], xn[:, s * SEQ:(s + 1) * SEQ], ACT.Identity,
                                                    scale=mod[:, SC_A, ds(t * SPT + s, 1)],
                                                    bias=mod[:, SH_A, ds(t * SPT + s, 1)])
                    last.then_inc(h_done, 1)

                def gate_off(n):
                    act.wait_ge(g_done, n + 1)
                    act.wait_ge(gu_done, n + GU0)
                    nc.scalar.activation(gd[:], psG[:, 0, :], ACT.Identity, scale=-1.0, bias=dskip[:, 0:1]
                                         ).then_inc(gd_done, 1)

                def c_high(t, par):
                    act.wait_ge(c_done, t + 1)
                    nc.scalar.copy(Ch[:, par, :], psM[0:4 * NST, 0, :]).then_inc(chi_done, 1)

                def dt_copy(t):
                    act.wait_ge(dtu_done, t + 1)
                    nc.scalar.copy(dtu[:], psM[0:RDT, 0, :]).then_inc(dtuc_done, 1)

                def softplus_parts(t):
                    act.wait_ge(dt_done, t + 1)
                    nc.scalar.activation(ex[:], psM[:, 0, :], ACT.Abs, bias=bdt[:, 0:1]).then_inc(ax_done, 1)
                    nc.scalar.activation(rx[:], psM[:, 0, :], ACT.Relu, bias=bdt[:, 0:1]).then_inc(x_read, 1)

                def softplus_log(t):
                    act.wait_ge(ax_done, t + 1)
                    nc.scalar.activation(ex[:], ex[:], ACT.Exp, scale=-1.0).then_inc(e_done, 1)
                    act.wait_ge(e_done, t + 1)
                    nc.scalar.activation(big[:], ex[:], ACT.Ln, bias=one[:, 0:1]).then_inc(big_done, 1)

                def first_tap(t):
                    act.wait_ge(h_done, t + 1)
                    nc.scalar.activation(acc[:, 0, :, :], H[:, :, TAPS - 1:], ACT.Identity,
                                         scale=conv[:, TAPS - 1:TAPS]).then_inc(tap0_done, 1)

                def activations(t, par):
                    act.wait_ge(z_done, t + 1)
                    nc.scalar.activation(sz[:, par, :], psZ[:, 0, :], ACT.Silu).then_inc(sz_done, 1)
                    act.wait_ge(conv_done, t + 1)
                    nc.scalar.activation(U[:, par, :, :], acc[:, 1, :, :], ACT.Silu).then_inc(u_done, 1)
                    nc.scalar.preload_act_table_set("natural_log_exp_and_others")

                def decay(t, par, k):
                    if k == 0:
                        act.wait_ge(dtx_done, t + 1)
                    act.wait_ge(k_done, t * NST + (k + 1 - ADEEP + K0))
                    nc.scalar.activation(A[:, k % ADEEP, :, 1:ROW], dtx[:, par, :, 1:ROW], ACT.Exp,
                                         scale=negA[:, k:k + 1]).then_inc(a_done, 1)

                nc.scalar.preload_act_table_set("natural_log_exp_and_others")
                for t in range(2):
                    square(t)
                    inv_std(t)
                    modulate(t, first=(t == 0))
                    c_high(t, t)
                    dt_copy(t)
                    if t == 1:
                        for k in range(L_DECAY):
                            decay(0, 0, k)
                    softplus_parts(t)
                    softplus_log(t)
                    first_tap(t)
                    if t == 0:
                        activations(0, 0)
                with nc.scalar.Fori(0, NT // 2) as j:
                    for par in range(2):
                        n = j * 2 + par
                        for k in range(NST):
                            decay(*ahead(n, par, k + L_DECAY))
                            if k == 3:
                                square(n + 2)
                            if k == 4:
                                activations(n + 1, 1 - par)
                            if k == 6:
                                inv_std(n + 2)
                            if k == 7:
                                gate_off(n)
                            if k == 9:
                                modulate(n + 2)
                            if k == 11:
                                c_high(n + 2, par)
                            if k == 14:
                                dt_copy(n + 2)
                            if k == 15:
                                softplus_parts(n + 2)
                                softplus_log(n + 2)
                                first_tap(n + 2)

            @block.gpsimd
            def _(pool):
                def inputs(t, par):
                    pool.wait_ge(u_done, t + 1)
                    d = dd[:, par, :].rearrange("p (s t) -> p s t", s=SPT)
                    nc.gpsimd.tensor_tensor(d[:, :, 2:ROW], U[:, par, :, 1:SEQ], U[:, par, :, 0:SEQ - 1],
                                            ALU.subtract)
                    nc.gpsimd.tensor_copy(d[:, :, 0:1], U[:, par, :, 0:1]).then_inc(dd_done, 1)

                def small_log(t):
                    pool.wait_ge(e_done, t + 1)
                    coefs = [coef[:, i:i + 1].broadcast_to([P, MT]) for i in range(4)]
                    nc.gpsimd.tensor_tensor(tiny[:], ex[:], coefs[0], ALU.mult).then_inc(series, 1)
                    for i in range(3):
                        pool.wait_ge(series, t * SERIES + (2 * i + 1))
                        nc.gpsimd.tensor_tensor(tiny[:], tiny[:], coefs[i + 1], ALU.add).then_inc(series, 1)
                        pool.wait_ge(series, t * SERIES + (2 * i + 2))
                        nc.gpsimd.tensor_tensor(tiny[:], tiny[:], ex[:], ALU.mult).then_inc(series, 1)
                    pool.wait_ge(series, t * SERIES + 7)
                    pool.wait_ge(big_done, t + 1)
                    nc.gpsimd.tensor_tensor(big[:], big[:], tiny[:], ALU.subtract).then_inc(series, 1)
                    pool.wait_ge(x_read, t + 1)
                    nc.gpsimd.tensor_tensor(rx[:], rx[:], tiny[:], ALU.add).then_inc(series, 1)

                def dt_out(t, par):
                    pool.wait_ge(blend_done, t + 1)
                    s3 = lambda a: a[:].rearrange("p (s t) -> p s t", s=SPT)
                    nc.gpsimd.tensor_tensor(dtx[:, par, :, 2:2 + SEQ], s3(rx), s3(big), ALU.add)
                    nc.gpsimd.tensor_tensor(dtx[:, par, :, 1:2], s3(rx)[:, :, 0:1], s3(big)[:, :, 0:1], ALU.add
                                            ).then_inc(dtx_done, 1)

                def skip_part(n, par):
                    pool.wait_ge(gd_done, n + 1)
                    nc.gpsimd.tensor_tensor(gu[:], gd[:], U[:, par, :, :].rearrange("p s t -> p (s t)"), ALU.mult
                                            ).then_inc(gu_done, 1)

                small_log(0)
                dt_out(0, 0)
                inputs(0, 0)
                with nc.gpsimd.Fori(0, NT // 2) as j:
                    for par in range(2):
                        n = j * 2 + par
                        small_log(n + 1)
                        dt_out(n + 1, 1 - par)
                        inputs(n + 1, 1 - par)
                        skip_part(n, par)

            @block.vector
            def _(dve):
                small = nc.vector.value_load(any_small[0:1, 0:1], min_val=0, max_val=1)

                def normalize(t):
                    dve.wait_ge(rstd_done, t + 1)
                    nc.vector.tensor_tensor(xn[:], psX[:, 0, :], rstd[:], ALU.mult).then_inc(xn_done, 1)

                def c_low(t, par):
                    dve.wait_ge(chi_done, t + 1)
                    rows = slice(2 * NST, 4 * NST)
                    nc.vector.tensor_tensor(Ch[rows, par, :], psM[rows, 0, :], Ch[rows, par, :], ALU.subtract
                                            ).then_inc(clo_done, 1)

                def blend(t):
                    dve.wait_ge(series, t * SERIES + SERIES)
                    nc.vector.scalar_tensor_tensor(big[:], ex[:], SMALL_E, big[:], ALU.is_gt, ALU.mult
                                                   ).then_inc(blend_done, 1)

                def convolve(t, i):
                    if i == 1:
                        dve.wait_ge(tap0_done, t + 1)
                    else:
                        dve.wait_ge(conv_step, t * (TAPS - 2) + (i - 1))
                    at = TAPS - 1 - i
                    nc.vector.scalar_tensor_tensor(acc[:, i % 2, :, :], H[:, :, at:at + SEQ], conv[:, at:at + 1],
                                                   acc[:, 1 - i % 2, :, :], ALU.mult, ALU.add
                                                   ).then_inc(conv_done if i == TAPS - 1 else conv_step, 1)

                def scan(n, par, k):
                    with nc.vector.If(small):
                        if k == 0:
                            dve.wait_ge(dd_done, n + 1)
                            dve.wait_ge(dtx_done, n + 1)
                            nc.vector.tensor_tensor(wx[:, :, 2:ROW], dtx[:, par, :, 2:ROW], U[:, par, :, 0:SEQ - 1],
                                                    ALU.mult)
                            nc.vector.tensor_tensor(wx[:, :, 1:2], dtx[:, par, :, 1:2], U[:, par, :, 0:1], ALU.mult
                                                    ).then_inc(w_done, 1)
                            dve.wait_ge(w_done, n + 1)
                        dve.wait_ge(k_done, n * NST + (k + K0))
                        nc.vector.tensor_scalar(part[:], dd[:, par, :], is_large[:, k:k + 1], None, ALU.mult
                                                ).then_inc(small_step, 1)
                        dve.wait_ge(small_step, n * 2 * NST + (2 * k + 1))
                        nc.vector.scalar_tensor_tensor(dd[:, 2, :], wx[:].rearrange("p s t -> p (s t)"),
                                                       is_small[:, k:k + 1], part[:], ALU.mult, ALU.add
                                                       ).then_inc(small_step, 1)
                        dve.wait_ge(small_step, n * 2 * NST + (2 * k + 2))
                        nc.vector.memset(S.spare[:, 6:7], 0.0)
                    dve.wait_ge(a_done, n * NST + (k + 1))
                    if k == 0:
                        dve.wait_ge(dd_done, n + 1)
                    dve.wait_ge(m_done, n * NST + (k - 3 + M0))
                    at = small * ((2 - par) * SPT * ROW) + par * SPT * ROW
                    nc.vector.tensor_tensor_scan(K[:, k % 4, :, :].rearrange("p s t -> p (s t)"),
                                                 A[:, k % ADEEP, :, :].rearrange("p s t -> p (s t)"),
                                                 dd[:].rearrange("p i t -> p (i t)")[:, ds(at, SPT * ROW)],
                                                 0.0, ALU.mult, ALU.add).then_inc(k_done, 1)

                def times_c(n, par, k):
                    dve.wait_ge(cb_done, n * NST + (k + 1))
                    dve.wait_ge(k_done, n * NST + (k + 1 + K0))
                    dve.wait_ge(acc_done, n * NST + (k - 3 + AC0))
                    nc.vector.tensor_tensor(M[:, k % 4, :].rearrange("p (s t) -> p s t", s=SPT), K[:, k % 4, :, 1:ROW],
                                            psC[:, k % 2, :].rearrange("p (s t) -> p s t", s=SPT), ALU.mult
                                            ).then_inc(m_done, 1)

                def sum_y(n, par):
                    dve.wait_ge(acc_done, n * NST + (NST + AC0))
                    dve.wait_ge(gu_done, n + 1 + GU0)
                    nc.vector.tensor_tensor(ys[:], psY[:, par, :], gu[:], ALU.add).then_inc(ys_done, 1)

                def gate_y(n, par):
                    dve.wait_ge(ys_done, n + 1 + YS0)
                    nc.vector.tensor_tensor(yo[:], ys[:], sz[:, par, :], ALU.mult).then_inc(yo_done, 1)

                def residual(n):
                    dve.wait_ge(o_done, n + 1)
                    for s in range(SPT):
                        x = S.X[:, ds((n * SPT + s) * SEQ, SEQ)]
                        last = nc.vector.scalar_tensor_tensor(x, psG[:, 0, s * SEQ:(s + 1) * SEQ],
                                                              mod[:, GA, ds(n * SPT + s, 1)], x, ALU.mult, ALU.add)
                    last.then_inc(x_done, 1)

                for i, (sem, count) in enumerate(((k_done, K0), (m_done, M0), (acc_done, AC0), (x_done, X0),
                                                  (ys_done, YS0), (gu_done, GU0))):
                    nc.vector.memset(S.spare[:, i:i + 1], 0.0).then_inc(sem, count)
                normalize(0)
                c_low(0, 0)
                for i in range(1, TAPS):
                    convolve(0, i)
                blend(0)
                normalize(1)
                c_low(1, 1)
                for k in range(L_SCAN):
                    scan(0, 0, k)
                    if k >= L_SCAN - L_TIMES:
                        times_c(0, 0, k - (L_SCAN - L_TIMES))
                with nc.vector.Fori(0, NT // 2) as j:
                    for par in range(2):
                        n = j * 2 + par
                        for k in range(NST):
                            scan(*ahead(n, par, k + L_SCAN))
                            times_c(*ahead(n, par, k + L_TIMES))
                            if k < TAPS - 1:
                                convolve(n + 1, k + 1)
                            if k == 7:
                                blend(n + 1)
                            if k == 8:
                                normalize(n + 2)
                            if k == 12:
                                sum_y(n, par)
                                c_low(n + 2, par)
                            if k == 13:
                                gate_y(n, par)
                            if k == 15:
                                residual(n)


def rwkv_weights(nc, ctx, w, S):
    sb = lambda name, shape: ctx.enter_context(nc.sbuf_tensor(name, shape, F32))
    S.wr, S.wk, S.wv = sb("wr_r", [P, P]), sb("wk_r", [P, P]), sb("wv_r", [P, P])
    S.mu = sb("mu", [P, 2])
    return [(S.wr[:], w["wr"]), (S.wk[:], w["wk"]), (S.wv[:], w["wv"]), (S.mu[:, 0:1], w["mur"]),
            (S.mu[:, 1:2], w["muk"])]


def rwkv(nc, w, S):
    with ExitStack() as ctx:
        def sb(name, shape, dt=F32):
            return ctx.enter_context(nc.sbuf_tensor(name, shape, dt))

        def pb(name, n):
            return ctx.enter_context(nc.psum_tensor(name, [P, n, 512], F32))

        wr, wk, wv, mu = S.wr, S.wk, S.wv, S.mu
        nmu = sb("nmu", [P, 2])
        one = sb("one_r", [P, 1])
        sq = sb("sq_r", [P, MT])
        lnv = sb("lnv_r", [P, MT])
        rstd = sb("rstd_r", [P, MT])
        xn = sb("xn_r", [P, MT])
        H = sb("H_r", [P, SPT, 1 + SEQ])
        old = sb("old_r", [P, 2, SPT, SEQ])
        mix = sb("mix_r", [P, 2, SPT, SEQ])
        az = sb("az_r", [P, MT])
        ez = sb("ez_r", [P, MT])
        lz = sb("lz_r", [P, MT])
        ls = sb("ls_r", [P, MT])
        rs = sb("rs_r", [P, MT])
        kr = sb("kr_r", [P, MT])
        ks = sb("ks_r", [P, MT])
        ov = sb("ov_r", [P, MT])
        psX, psM, psR, psK, psV = pb("psX_r", 2), pb("psM_r", 1), pb("psR_r", 2), pb("psK_r", 1), pb("psV_r", 1)

        with nc.Block() as block:

            @block.vector
            def _(dve):
                nc.vector.memset(H[:, :, 0:1], 0.0)
                nc.vector.memset(one[:], 1.0)
                dve.wait_ge(S.loaded_rwkv, S.count_rwkv)
                nc.vector.tensor_scalar(nmu[:], mu[:], -1.0, 1.0, ALU.mult, ALU.add)

        names = ["xc_done", "sq_done", "var_done", "lnv_done", "rstd_done", "xn_done", "h_done", "old_done",
                 "mix_done", "r_done", "k_done", "az_done", "ez_done", "lz_done", "ls_done", "rs_done", "kr_done", "ks_done",
                 "v_done", "ov_done", "x_done", "stored"]
        (xc_done, sq_done, var_done, lnv_done, rstd_done, xn_done, h_done, old_done, mix_done, r_done, k_done,
         az_done, ez_done, lz_done, ls_done, rs_done, kr_done, ks_done, v_done, ov_done, x_done, stored) = [
             ctx.enter_context(nc.semaphore("r_" + n)) for n in names]
        XN0, LV0, MX0, LS0, KR0, KS0, V0, OV0 = 2, 1, 1, 2, 1, 1, 1, 1
        mod = S.mod[1]

        with nc.Block() as block:

            @block.sync
            def _(sp):
                with nc.sync.Fori(0, NT) as n:
                    sp.wait_ge(x_done, n + 1)
                    sp.dma_start(S.out[:, ds(n * MT, MT)], S.X[:, ds(n * MT, MT)]).then_inc(stored, 16)
                sp.wait_ge(stored, 16 * NT)

            @block.tensor
            def _(pe):
                def centered(t, par):
                    pe.wait_ge(xn_done, t - 1 + XN0)
                    nc.tensor.matmul(psX[:, par, :], S.center[:], S.X[:, ds(t * MT, MT)],
                                     start=True, stop=True).then_inc(xc_done, 1)

                def var(t):
                    pe.wait_ge(sq_done, t + 1)
                    pe.wait_ge(lnv_done, t + LV0)
                    nc.tensor.matmul(psM[:, 0, :], S.meanw[:], sq[:], start=True, stop=True).then_inc(var_done, 1)

                def products(t, par):
                    pe.wait_ge(mix_done, t + 1 + MX0)
                    pe.wait_ge(ls_done, t - 1 + LS0)
                    nc.tensor.matmul(psR[:, par, :], wr[:], mix[:, 0, :, :], start=True, stop=True).then_inc(r_done, 1)
                    pe.wait_ge(kr_done, t + KR0)
                    nc.tensor.matmul(psK[:, 0, :], wk[:], mix[:, 1, :, :], start=True, stop=True).then_inc(k_done, 1)

                def value(t):
                    pe.wait_ge(ks_done, t + 1 + KS0)
                    pe.wait_ge(ov_done, t + OV0)
                    nc.tensor.matmul(psV[:, 0, :], wv[:], ks[:], start=True, stop=True).then_inc(v_done, 1)

                for t in range(3):
                    centered(t, t % 2)
                    var(t)
                    if t == 2:
                        products(0, 0)
                with nc.tensor.Fori(0, NT // 2) as j:
                    for par in range(2):
                        n = j * 2 + par
                        centered(n + 3, 1 - par)
                        value(n)
                        products(n + 1, 1 - par)
                        var(n + 3)

            @block.scalar
            def _(act):
                def square(t, par):
                    act.wait_ge(xc_done, t + 1)
                    nc.scalar.activation(sq[:], psX[:, par, :], ACT.Square).then_inc(sq_done, 1)

                def log_var(t):
                    act.wait_ge(var_done, t + 1)
                    nc.scalar.activation(lnv[:], psM[:, 0, :], ACT.Ln, bias=S.eps[:, 0:1]).then_inc(lnv_done, 1)

                def inv_std(t):
                    act.wait_ge(lnv_done, t + 1 + LV0)
                    nc.scalar.activation(rstd[:], lnv[:], ACT.Exp, scale=-0.5).then_inc(rstd_done, 1)

                def predecessor(t):
                    act.wait_ge(h_done, t + 1)
                    act.wait_ge(mix_done, t + MX0)
                    for i in range(2):
                        last = nc.scalar.activation(old[:, i, :, :], H[:, :, 0:SEQ], ACT.Identity,
                                                    scale=nmu[:, i:i + 1])
                    last.then_inc(old_done, 1)

                def magnitude(t, par):
                    act.wait_ge(r_done, t + 1)
                    nc.scalar.activation(az[:], psR[:, par, :], ACT.Abs).then_inc(az_done, 1)

                def relu(t):
                    act.wait_ge(k_done, t + 1)
                    act.wait_ge(ks_done, t + KS0)
                    nc.scalar.activation(kr[:], psK[:, 0, :], ACT.Relu).then_inc(kr_done, 1)

                def exp_z(t):
                    act.wait_ge(az_done, t + 1)
                    nc.scalar.activation(ez[:], az[:], ACT.Exp, scale=-1.0).then_inc(ez_done, 1)

                def log_z(t):
                    act.wait_ge(ez_done, t + 1)
                    nc.scalar.activation(lz[:], ez[:], ACT.Ln, bias=one[:, 0:1]).then_inc(lz_done, 1)

                def sigmoid(t):
                    act.wait_ge(ls_done, t + 1 + LS0)
                    act.wait_ge(ov_done, t + OV0)
                    nc.scalar.activation(rs[:], ls[:], ACT.Exp).then_inc(rs_done, 1)

                nc.scalar.preload_act_table_set("natural_log_exp_and_others")
                nc.scalar.copy(S.spare[:, 7:8], S.eps[:, 0:1]).then_inc(lnv_done, LV0)
                for t in range(2):
                    square(t, t)
                    log_var(t)
                    inv_std(t)
                    predecessor(t)
                    if t == 1:
                        square(2, 0)
                with nc.scalar.Fori(0, NT // 2) as j:
                    for par in range(2):
                        n = j * 2 + par
                        relu(n)
                        magnitude(n, par)
                        log_var(n + 2)
                        exp_z(n)
                        inv_std(n + 2)
                        log_z(n)
                        square(n + 3, 1 - par)
                        sigmoid(n)
                        predecessor(n + 2)

            @block.gpsimd
            def _(pool):
                def squares(t):
                    pool.wait_ge(kr_done, t + 1 + KR0)
                    pool.wait_ge(v_done, t + V0)
                    nc.gpsimd.tensor_tensor(ks[:], kr[:], kr[:], ALU.mult).then_inc(ks_done, 1)

                nc.gpsimd.memset(S.spare[:, 6:7], 0.0).then_inc(ks_done, KS0)
                nc.gpsimd.memset(S.spare[:, 5:6], 0.0).then_inc(v_done, V0)
                with nc.gpsimd.Fori(0, NT // 2) as j:
                    for par in range(2):
                        squares(j * 2 + par)

            @block.vector
            def _(dve):
                def normalize(t, par):
                    dve.wait_ge(rstd_done, t + 1)
                    nc.vector.tensor_tensor(xn[:], psX[:, par, :], rstd[:], ALU.mult).then_inc(xn_done, 1)

                def modulate(t):
                    dve.wait_ge(xn_done, t + 1 + XN0)
                    for s in range(SPT):
                        last = nc.vector.tensor_scalar(H[:, s, 1:], xn[:, s * SEQ:(s + 1) * SEQ],
                                                       mod[:, SC_B, ds(t * SPT + s, 1)],
                                                       mod[:, SH_B, ds(t * SPT + s, 1)], ALU.mult, ALU.add)
                    last.then_inc(h_done, 1)

                def mixes(t, first=False):
                    dve.wait_ge(old_done, t + 1)
                    if not first:
                        dve.wait_ge(k_done, t)
                    for i in range(2):
                        last = nc.vector.scalar_tensor_tensor(mix[:, i, :, :], H[:, :, 1:], mu[:, i:i + 1],
                                                              old[:, i, :, :], ALU.mult, ALU.add)
                    last.then_inc(mix_done, 1)

                def log_sigmoid(t, par):
                    dve.wait_ge(lz_done, t + 1)
                    nc.vector.scalar_tensor_tensor(ls[:], psR[:, par, :], 0.0, lz[:], ALU.min, ALU.subtract
                                                   ).then_inc(ls_done, 1)

                def gate_value(t):
                    dve.wait_ge(v_done, t + 1 + V0)
                    dve.wait_ge(rs_done, t + 1)
                    nc.vector.tensor_tensor(ov[:], rs[:], psV[:, 0, :], ALU.mult).then_inc(ov_done, 1)

                def residual(t):
                    dve.wait_ge(ov_done, t + 1 + OV0)
                    for s in range(SPT):
                        x = S.X[:, ds((t * SPT + s) * SEQ, SEQ)]
                        last = nc.vector.scalar_tensor_tensor(x, ov[:, s * SEQ:(s + 1) * SEQ],
                                                              mod[:, GB, ds(t * SPT + s, 1)], x, ALU.mult, ALU.add)
                    last.then_inc(x_done, 1)

                for i, (sem, count) in enumerate(((xn_done, XN0), (mix_done, MX0), (ls_done, LS0), (kr_done, KR0),
                                                  (ov_done, OV0))):
                    nc.vector.memset(S.spare[:, i:i + 1], 0.0).then_inc(sem, count)
                normalize(0, 0)
                modulate(0)
                mixes(0, first=True)
                normalize(1, 1)
                modulate(1)
                with nc.vector.Fori(0, NT // 2) as j:
                    for par in range(2):
                        n = j * 2 + par
                        mixes(n + 1)
                        normalize(n + 2, par)
                        log_sigmoid(n, par)
                        modulate(n + 2)
                        gate_value(n)
                        residual(n)



def build(nc, w, out, stages):
    S = Shared()
    S.out = out
    sem = lambda name: ctx.enter_context(nc.semaphore(name))
    with ExitStack() as ctx:
        S.X = ctx.enter_context(nc.sbuf_tensor("X", [P, TOK + PAD * SEQ], F32))
        S.loaded_x, S.loaded_att, S.loaded_moe, S.loaded_mamba, S.loaded_rwkv = map(
            sem, ["loaded_x", "loaded_att", "loaded_moe", "loaded_mamba", "loaded_rwkv"])
        moe_loads, mamba_loads, rwkv_loads = (moe_weights(nc, ctx, w, S), mamba_weights(nc, ctx, w, S),
                                              rwkv_weights(nc, ctx, w, S))
        S.count_moe, S.count_mamba, S.count_rwkv = (16 * len(moe_loads), 16 * len(mamba_loads),
                                                    16 * len(rwkv_loads))
        constants(nc, ctx, S)
        with ExitStack() as first:
            att_loads = attention_weights(nc, first, w, S)
            S.count_att = 16 * len(att_loads)
            loads = [(S.loaded_att, *l) for l in att_loads] + [(S.loaded_x, S.X[:, 0:TOK], w["x"])]
            S.later_loads = []
            for sem_loaded, pieces in ((S.loaded_moe, moe_loads), (S.loaded_mamba, mamba_loads),
                                       (S.loaded_rwkv, rwkv_loads)):
                S.later_loads += [(sem_loaded, *l) for l in pieces]
            constants_and_modulation(nc, w, S, loads)
            if attention in stages:
                attention(nc, w, S)
        for stage in stages:
            if stage is not attention:
                stage(nc, w, S)

def layouts(inputs):
    import numpy as np

    i = {k: np.asarray(v) for k, v in inputs.items()}
    t = lambda a, *o: np.ascontiguousarray(a.transpose(*o))

    down = lambda a: np.ascontiguousarray(np.moveaxis(np.swapaxes(a, -1, -2).reshape(a.shape[:-2] + (2, P, P)), -2, 0))
    arrays = {
        "x": t(i["L0_attn_x_bld"].reshape(TOK, P), 1, 0),
        "c0": t(i["L0_c"], 1, 0), "c1": t(i["L1_c"], 1, 0),
        "wmod0": i["L0_wmod"].reshape(P, 6, P), "wmod1": i["L1_wmod"].reshape(P, 6, P),
        "wqT": t(i["L0_attn_Wq"], 2, 1, 0), "wkuT": t(i["L0_attn_Wk_up"], 2, 1, 0),
        "wvuT": t(i["L0_attn_Wv_up"], 2, 1, 0), "wo": t(i["L0_attn_Wout"], 1, 0, 2),
        "wlat": i["L0_attn_Wkv_down"],
        "sg": t(i["L0_ffn_sg_w"], 1, 0), "su": t(i["L0_ffn_su_w"], 1, 0), "sd": down(i["L0_ffn_sd_w"]),
        "wg": t(i["L0_ffn_wg"], 2, 0, 1), "wu": t(i["L0_ffn_wu"], 2, 0, 1), "wd": down(i["L0_ffn_wd"]),
        "router": t(i["L0_ffn_router_w"], 1, 0), "rbias": i["L0_ffn_routing_bias"].reshape(1, NEXP),
        "wz": t(i["L1_attn_W_z"], 1, 0), "wpar": t(i["L1_attn_W_params"], 1, 0),
        "conv": i["L1_attn_conv_w"].reshape(P, TAPS), "wdt": t(i["L1_attn_W_dt"], 1, 0),
        "bdt": i["L1_attn_b_dt"].reshape(P, 1), "alog": i["L1_attn_A_log"], "dskip": i["L1_attn_D"].reshape(P, 1),
        "wout": t(i["L1_attn_W_out"], 1, 0),
        "wr": t(i["L1_ffn_W_r"], 1, 0), "wk": t(i["L1_ffn_W_k"], 1, 0), "wv": t(i["L1_ffn_W_v"], 1, 0),
        "mur": i["L1_ffn_mu_r"].reshape(P, 1), "muk": i["L1_ffn_mu_k"].reshape(P, 1),
    }
    return arrays

def kernel(**inputs):
    import numpy as np
    import concourse.bacc as bacc
    from concourse.bass_utils import run_bass_kernel_spmd

    nc = bacc.Bacc("TRN2", target_bir_lowering=False, num_devices=1)
    arrays = layouts(inputs)
    w = {k: nc.dram_tensor("in_" + k, a.shape, mybir.dt.from_np(a.dtype), kind="ExternalInput").ap()
         for k, a in arrays.items()}
    out = nc.dram_tensor("out", [P, TOK], F32, kind="ExternalOutput").ap()
    build(nc, w, out, [attention, moe, mamba, rwkv])
    r = run_bass_kernel_spmd(nc, [{"in_" + k: a for k, a in arrays.items()}], core_ids=[0])
    xT = r.results[0]["out"]
    return np.ascontiguousarray(xT.transpose(1, 0)).reshape(NSEQ, SEQ, P)
```
